# Optimizing a Trainium2 kernel written in Bass

```python
import numpy as np
import jax
import jax.numpy as jnp

def _softmax(x, axis=-1):
    return jax.nn.softmax(x, axis=axis)

def _gelu(x):
    return jax.nn.gelu(x, approximate=True)

def _silu(x):
    return jax.nn.silu(x)

def _sigmoid(x):
    return jax.nn.sigmoid(x)

def _layernorm(x, axis=-1, eps=1e-05):
    m = jnp.mean(x, axis=axis, keepdims=True)
    v = jnp.var(x, axis=axis, keepdims=True)
    return (x - m) / jnp.sqrt(v + eps)

def _scatter_add(tgt, idx, src, axis=0):
    return tgt.at[idx].add(src)

def _segment_sum(src, seg, n):
    return jax.ops.segment_sum(src, seg, n)
kernel_name = 'mk_perceiver_d1_seqx_r8_78c792'

def setup_inputs(seed: int=0):
    np.random.seed(seed)
    _w = jnp.asarray

    def _rec_inputs():
        import jax
        import jax.numpy as jnp
        _rk = jax.random.key(seed)
        x = -0.0003929 + 0.9999 * jax.random.normal(jax.random.fold_in(_rk, 1), (16, 64, 512), jnp.float32)
        _lenS = 64 - jax.random.randint(jax.random.fold_in(_rk, 7), (16,), 0, max(1, 64 // 4) + 1, jnp.int32)
        _lenS2 = 128 - jax.random.randint(jax.random.fold_in(_rk, 8), (16,), 0, max(1, 128 // 4) + 1, jnp.int32)
        _ctx_4096P = jax.random.normal(jax.random.fold_in(_rk, 11), (16, 16, 512), jnp.float32)
        _ctx_4096c = jax.random.dirichlet(jax.random.fold_in(_rk, 511), 0.3 * jnp.ones((16,), jnp.float32), (16, 128))
        _ctx_4096t = jnp.einsum('bsk,bkd->bsd', _ctx_4096c, _ctx_4096P)
        _ctx_4096t = _ctx_4096t * jax.lax.rsqrt(jnp.mean(jnp.square(_ctx_4096t)) + 1e-12) * 0.953939
        ctx_4096 = 2.81802e-05 + 1.00001 * (_ctx_4096t + 0.3 * jax.random.normal(jax.random.fold_in(_rk, 611), (16, 128, 512), jnp.float32))
        return (x, ctx_4096)
    x, ctx_4096 = _rec_inputs()

    def _L0_xattn_setup():
        import jax, jax.numpy as jnp
        import numpy as np
        EMB_DIM = 512
        NHEADS = 32
        KVHEADS = 8
        HEAD_DIM = 128
        ROPE_BASE = 10000.0

        def _rope(x):
            B, H, S, D = x.shape
            inv_freq = 1.0 / ROPE_BASE ** (jnp.arange(0, D, 2, dtype=jnp.float32) / D)
            ang = jnp.arange(S, dtype=jnp.float32)[:, None] * inv_freq[None, :]
            cos = jnp.concatenate([jnp.cos(ang), jnp.cos(ang)], axis=-1)
            sin = jnp.concatenate([jnp.sin(ang), jnp.sin(ang)], axis=-1)
            x1, x2 = (x[..., :D // 2], x[..., D // 2:])
            rot = jnp.concatenate([-x2, x1], axis=-1)
            return x * cos + rot * sin
        key = jax.random.key(seed)
        ks = jax.random.split(key, 7)
        B, S = (2, 256)
        std_qk = EMB_DIM ** (-0.5)
        std_vd = (1.0 / (EMB_DIM * NHEADS * HEAD_DIM) ** 0.5) ** 0.5
        return {'q': jax.random.normal(ks[0], (B, S, EMB_DIM), jnp.float32), 'k': jax.random.normal(ks[1], (B, S, EMB_DIM), jnp.float32), 'v': jax.random.normal(ks[2], (B, S, EMB_DIM), jnp.float32), 'Wq': jax.random.normal(ks[3], (NHEADS * HEAD_DIM, EMB_DIM), jnp.float32) * std_qk, 'Wk': jax.random.normal(ks[4], (KVHEADS * HEAD_DIM, EMB_DIM), jnp.float32) * std_qk, 'Wv': jax.random.normal(ks[5], (KVHEADS * HEAD_DIM, EMB_DIM), jnp.float32) * std_vd, 'Wd': jax.random.normal(ks[6], (EMB_DIM, NHEADS * HEAD_DIM), jnp.float32) * std_vd}
    _L0_xattn_all = _L0_xattn_setup()
    _L0_xattn_in = {k: v for k, v in _L0_xattn_all.items() if k in ('Wq', 'Wk', 'Wv', 'Wd')}
    del _L0_xattn_all

    def _L0_attn_setup():
        import jax, jax.numpy as jnp
        import numpy as np
        import math
        B, L, D, H = (32, 64, 512, 32)
        HD = D // H
        key = jax.random.key(seed)
        ks = jax.random.split(key, 9)
        s = 1.0 / math.sqrt(D)
        return {'x': jax.random.normal(ks[0], (B, L, D), jnp.float32), 'Wq': jax.random.normal(ks[1], (D, D), jnp.float32) * s, 'bq': jax.random.normal(ks[2], (D,), jnp.float32) * s, 'Wk': jax.random.normal(ks[3], (D, D), jnp.float32) * s, 'bk': jax.random.normal(ks[4], (D,), jnp.float32) * s, 'Wv': jax.random.normal(ks[5], (D, D), jnp.float32) * s, 'bv': jax.random.normal(ks[6], (D,), jnp.float32) * s, 'Wo': jax.random.normal(ks[7], (D, D), jnp.float32) * s, 'bo': jax.random.normal(ks[8], (D,), jnp.float32) * s}
    _L0_attn_all = _L0_attn_setup()
    _L0_attn_in = {k: v for k, v in _L0_attn_all.items() if k in ('Wq', 'bq', 'Wk', 'bk', 'Wv', 'bv', 'Wo', 'bo')}
    del _L0_attn_all

    def _L0_ffn_setup():
        import jax, jax.numpy as jnp
        import numpy as np
        MAX_THRESHOLD = 1.0 / 8.0
        SCALING = 32.0 / 16.0
        key = jax.random.key(seed)
        ks = jax.random.split(key, 8)
        B_, S, D, O, E, R = (4, 256, 512, 512, 8, 16)
        sd = 1.0 / np.sqrt(D)
        return {'x': jax.random.normal(ks[0], (B_, S, D), jnp.float32), 'W_base': jax.random.normal(ks[1], (O, D), jnp.float32) * sd, 'b_base': jax.random.normal(ks[2], (O,), jnp.float32) * 0.01, 'W_gate': jax.random.normal(ks[3], (E, D), jnp.float32) * sd, 'W_thr': jax.random.normal(ks[4], (1, D), jnp.float32) * sd, 'b_thr': jax.random.normal(ks[5], (1,), jnp.float32) * 0.01, 'A': jax.random.normal(ks[6], (E, R, D), jnp.float32) * sd, 'B': jax.random.normal(ks[7], (O,), jnp.float32)[None, :, None] * jnp.zeros((E, O, R), jnp.float32) + jax.random.normal(jax.random.fold_in(key, 7), (E, O, R), jnp.float32) * (1.0 / np.sqrt(R))}
    _L0_ffn_all = _L0_ffn_setup()
    _L0_ffn_in = {k: v for k, v in _L0_ffn_all.items() if k in ('W_base', 'b_base', 'W_gate', 'W_thr', 'b_thr', 'A', 'B')}
    del _L0_ffn_all
    return {'x': x, 'ctx_4096': ctx_4096, 'L0_xattn_Wq': _L0_xattn_in['Wq'], 'L0_xattn_Wk': _L0_xattn_in['Wk'], 'L0_xattn_Wv': _L0_xattn_in['Wv'], 'L0_xattn_Wd': _L0_xattn_in['Wd'], 'L0_attn_Wq': _L0_attn_in['Wq'], 'L0_attn_bq': _L0_attn_in['bq'], 'L0_attn_Wk': _L0_attn_in['Wk'], 'L0_attn_bk': _L0_attn_in['bk'], 'L0_attn_Wv': _L0_attn_in['Wv'], 'L0_attn_bv': _L0_attn_in['bv'], 'L0_attn_Wo': _L0_attn_in['Wo'], 'L0_attn_bo': _L0_attn_in['bo'], 'L0_ffn_W_base': _L0_ffn_in['W_base'], 'L0_ffn_b_base': _L0_ffn_in['b_base'], 'L0_ffn_W_gate': _L0_ffn_in['W_gate'], 'L0_ffn_W_thr': _L0_ffn_in['W_thr'], 'L0_ffn_b_thr': _L0_ffn_in['b_thr'], 'L0_ffn_A': _L0_ffn_in['A'], 'L0_ffn_B': _L0_ffn_in['B']}

def reference(x, ctx_4096, L0_xattn_Wq, L0_xattn_Wk, L0_xattn_Wv, L0_xattn_Wd, L0_attn_Wq, L0_attn_bq, L0_attn_Wk, L0_attn_bk, L0_attn_Wv, L0_attn_bv, L0_attn_Wo, L0_attn_bo, L0_ffn_W_base, L0_ffn_b_base, L0_ffn_W_gate, L0_ffn_W_thr, L0_ffn_b_thr, L0_ffn_A, L0_ffn_B):
    import jax
    import jax.numpy as jnp

    def _L0_xattn_ref(q, k, v, Wq, Wk, Wv, Wd):
        import jax, jax.numpy as jnp
        import numpy as np
        EMB_DIM = 512
        NHEADS = 32
        KVHEADS = 8
        HEAD_DIM = 128
        ROPE_BASE = 10000.0

        def _rope(x):
            B, H, S, D = x.shape
            inv_freq = 1.0 / ROPE_BASE ** (jnp.arange(0, D, 2, dtype=jnp.float32) / D)
            ang = jnp.arange(S, dtype=jnp.float32)[:, None] * inv_freq[None, :]
            cos = jnp.concatenate([jnp.cos(ang), jnp.cos(ang)], axis=-1)
            sin = jnp.concatenate([jnp.sin(ang), jnp.sin(ang)], axis=-1)
            x1, x2 = (x[..., :D // 2], x[..., D // 2:])
            rot = jnp.concatenate([-x2, x1], axis=-1)
            return x * cos + rot * sin
        B, Sq, _ = q.shape
        Skv = k.shape[1]
        queries = (q @ Wq.T).reshape(B, Sq, NHEADS, HEAD_DIM).transpose(0, 2, 1, 3)
        keys = (k @ Wk.T).reshape(B, Skv, KVHEADS, HEAD_DIM).transpose(0, 2, 1, 3)
        values = (v @ Wv.T).reshape(B, Skv, KVHEADS, HEAD_DIM).transpose(0, 2, 1, 3)
        queries = _rope(queries)
        keys = _rope(keys)
        exp = NHEADS // KVHEADS
        keys = jnp.repeat(keys, exp, axis=1)
        values = jnp.repeat(values, exp, axis=1)
        scale = HEAD_DIM ** (-0.5)
        scores = jnp.einsum('bhqd,bhkd->bhqk', queries, keys) * scale
        causal = jnp.tril(jnp.ones((Sq, Skv), dtype=bool))
        scores = jnp.where(causal[None, None], scores, jnp.finfo(scores.dtype).min)
        attn = jax.nn.softmax(scores, axis=-1)
        ctx = jnp.einsum('bhqk,bhkd->bhqd', attn, values)
        ctx = ctx.transpose(0, 2, 1, 3).reshape(B, Sq, NHEADS * HEAD_DIM)
        return ctx @ Wd.T

    def _L0_attn_ref(x, Wq, bq, Wk, bk, Wv, bv, Wo, bo):
        import jax, jax.numpy as jnp
        import numpy as np
        import math
        B, L, D, H = (32, 64, 512, 32)
        HD = D // H
        b, l, d = x.shape
        h, hd = (H, HD)
        q = (x @ Wq.T + bq).reshape(b, l, h, hd).transpose(0, 2, 1, 3)
        k = (x @ Wk.T + bk).reshape(b, l, h, hd).transpose(0, 2, 1, 3)
        v = (x @ Wv.T + bv).reshape(b, l, h, hd).transpose(0, 2, 1, 3)
        scores = jnp.einsum('bhqd,bhkd->bhqk', q, k) / math.sqrt(hd)
        causal = jnp.tril(jnp.ones((l, l), bool))
        scores = jnp.where(causal, scores, -jnp.inf)
        att = jax.nn.softmax(scores, axis=-1)
        out = jnp.einsum('bhqk,bhkd->bhqd', att, v)
        out = out.transpose(0, 2, 1, 3).reshape(b, l, d)
        return out @ Wo.T + bo

    def _L0_ffn_ref(x, W_base, b_base, W_gate, W_thr, b_thr, A, B):
        import jax, jax.numpy as jnp
        import numpy as np
        MAX_THRESHOLD = 1.0 / 8.0
        SCALING = 32.0 / 16.0
        base = jnp.einsum('bsd,od->bso', x, W_base) + b_base
        D = x.shape[-1]
        xf = x.reshape(-1, D)
        gate_logits = jax.nn.softmax(xf @ W_gate.T, axis=-1)
        thresholds = jax.nn.sigmoid(xf @ W_thr.T + b_thr) * MAX_THRESHOLD
        adapted = gate_logits - thresholds
        selected = (adapted >= 0).astype(x.dtype)
        weights = adapted * selected
        wsum = jnp.sum(weights, axis=-1, keepdims=True)
        wsum = jnp.where(wsum == 0, jnp.ones_like(wsum), wsum)
        weights = weights / wsum
        h = jnp.einsum('nd,erd->ner', xf, A)
        moe = jnp.einsum('ner,ne,eor->no', h, weights, B) * SCALING
        out = base + moe.reshape(base.shape)
        return out
    x = x + _L0_xattn_ref(_layernorm(x, axis=-1), ctx_4096, ctx_4096, L0_xattn_Wq, L0_xattn_Wk, L0_xattn_Wv, L0_xattn_Wd)
    x = x + _L0_attn_ref(_layernorm(x, axis=-1), L0_attn_Wq, L0_attn_bq, L0_attn_Wk, L0_attn_bk, L0_attn_Wv, L0_attn_bv, L0_attn_Wo, L0_attn_bo)
    x = x + _L0_ffn_ref(_layernorm(x, axis=-1), L0_ffn_W_base, L0_ffn_b_base, L0_ffn_W_gate, L0_ffn_W_thr, L0_ffn_b_thr, L0_ffn_A, L0_ffn_B)
    return x

_drawn_inputs = setup_inputs


def setup_inputs(seed=0):
    import zlib

    import numpy as np

    out = dict(_drawn_inputs(seed))
    spreads = {}
    factors = {'L0_attn_bq': 7.506, 'L0_attn_bk': 8.0, 'L0_ffn_b_base': 8.0}
    for name, (base, spread) in spreads.items():
        noise = np.random.default_rng([zlib.crc32(name.encode()), seed]).standard_normal(out[name].shape)
        drawn = base * np.exp(spread * noise) if base else spread * noise
        out[name] = jnp.asarray(drawn.astype(out[name].dtype))
    for name, factor in factors.items():
        out[name] = (out[name] * factor).astype(out[name].dtype)
    return out
```

```python
from contextlib import ExitStack

import concourse.bass as bass
from concourse import mybir

F32 = mybir.dt.float32
F32R = mybir.dt.float32r
ALU = mybir.AluOpType
ACT = mybir.ActivationFunctionType
AXX = mybir.AxisListType.X

P = 128
B, S, D = 16, 64, 512
KT = D // P
TOK = B * S
NT = TOK // P
HALF = TOK // 2
HB = B // 2
DH = 128
NKV = 8
REP = 4
SH = 32
SD = D // SH
NE, NR = 8, 16
NG = NE + 1
EPS = 1e-5
NEG = -1.0e30
X_SCALE = float(DH) ** -0.5
S_SCALE = float(SD) ** -0.5
MAX_THR = 0.125
SCALING = 2.0

XT = 2 + REP
NU = 2 * NKV
XCH = 2
ST = 3
SCH = 4
NSU = 2 * KT
PIECE = 1024
C_ID, C_COS, C_SIN, C_MASK, C_PAR = 0, 128, 192, 256, 320
NCONST = 322


def build(nc, x, ctxT, w_x, w_s, w_o, w_b, w_ag, w_eb, consts, bias_cols, bias_rows, b_thr, out):
    es = ExitStack()
    with es:
        def sem(name):
            return es.enter_context(nc.semaphore(name))

        def sb(stack, name, shape, dt=F32):
            return stack.enter_context(nc.sbuf_tensor(name, shape, dt))

        X = sb(es, "X", [P, NT, D])
        xh = sb(es, "xh", [P, KT, TOK], F32R)
        xl = sb(es, "xl", [P, KT, TOK], F32R)
        ah = sb(es, "ah", [P, KT, TOK], F32R)
        al = sb(es, "al", [P, KT, TOK], F32R)
        raw = [sb(es, f"raw{i}", [P, PIECE]) for i in range(2)]
        sm = [sb(es, f"sm{i}", [P, 512]) for i in range(2)]
        cst = sb(es, "cst", [P, NCONST])
        bcol = sb(es, "bcol", [P, 3, KT])
        bthr = sb(es, "bthr", [P, 1])
        stats = sb(es, "stats", [P, NT, 6])
        mv = sb(es, "mv", [P, NT, 2])
        veps = sb(es, "veps", [P, NT])
        rstd = sb(es, "rstd", [P, NT])
        mhalf = sb(es, "mhalf", [P, NT])
        mx = sb(es, "mx", [P, 2, 8])
        zs = sb(es, "zs", [P, 2, 8])
        rz = sb(es, "rz", [P, 2, 8])
        xs = ExitStack()
        wqh = sb(xs, "wqh", [P, 3, KT, 256], F32R)
        wql = sb(xs, "wql", [P, 3, KT, 256], F32R)
        wdh = sb(xs, "wdh", [P, REP, D], F32R)
        wdl = sb(xs, "wdl", [P, REP, D], F32R)
        kr = [sb(xs, f"kr{i}", [P, HB, S]) for i in range(2)]
        qr2 = sb(xs, "qr2", [P, 2, HB, REP, S])
        qr = [qr2[:, i] for i in range(2)]
        vt = sb(xs, "vt", [P, HB, 2, S])
        v2h = [sb(xs, f"v2h{i}", [P, HB, DH], F32R) for i in range(2)]
        v2l = [sb(xs, f"v2l{i}", [P, HB, DH], F32R) for i in range(2)]
        ch = sb(xs, "ch", [P, REP, HALF], F32R)
        cl = sb(xs, "cl", [P, REP, HALF], F32R)
        pt = [sb(xs, f"pt{i}", [P, 1024], F32R) for i in range(2)]
        t1 = [sb(xs, f"t1{i}", [P, HALF]) for i in range(2)]
        sw = [sb(xs, f"sw{i}", [P, HALF]) for i in range(2)]
        xs.close()
        ss = ExitStack()
        wsh = sb(ss, "wsh", [P, KT, KT, 384], F32R)
        wsl = sb(ss, "wsl", [P, KT, KT, 384], F32R)
        woh = sb(ss, "woh", [P, KT, D], F32R)
        wol = sb(ss, "wol", [P, KT, D], F32R)
        kb = [sb(ss, f"kb{i}", [P, HB, 4, S]) for i in range(2)]
        qm = [sb(ss, f"qm{i}", [P, HB, 2, S]) for i in range(2)]
        vc = [sb(ss, f"vc{i}", [P, HB, 2, 64]) for i in range(2)]
        vts = sb(ss, "vts", [P, HALF])
        ot = [sb(ss, f"ot{i}", [P, HALF]) for i in range(2)]
        osel = [sb(ss, f"osel{i}", [P, 2 * S]) for i in range(2)]
        pts = [sb(ss, f"pts{i}", [P, 512]) for i in range(2)]
        bqm = sb(ss, "bqm", [P, 2, KT])
        xns = [sb(ss, f"xns{i}", [P, D]) for i in range(2)]
        brow_o = sb(ss, "brow_o", [P, D])
        ss.close()
        fs = ExitStack()
        wbh = sb(fs, "wbh", [P, KT, D], F32R)
        wbl = sb(fs, "wbl", [P, KT, D], F32R)
        weh = sb(fs, "weh", [P, D], F32R)
        wel = sb(fs, "wel", [P, D], F32R)
        wag = sb(fs, "wag", [P, KT, P + NG])
        xf = sb(fs, "xf", [P, KT, TOK])
        hg = sb(fs, "hg", [P, NT, P + NG])
        xnf = [sb(fs, f"xnf{i}", [P, D]) for i in range(2)]
        brow_b = sb(fs, "brow_b", [P, D])
        hw = sb(fs, "hw", [P, NT, P])
        hth = sb(fs, "hth", [P, TOK], F32R)
        htl = sb(fs, "htl", [P, TOK], F32R)
        gm = sb(fs, "gm", [P, NT])
        ge = sb(fs, "ge", [P, NT, NE])
        gz = sb(fs, "gz", [P, NT])
        gr = sb(fs, "gr", [P, NT])
        gt = sb(fs, "gt", [P, NT])
        gw = sb(fs, "gw", [P, NT, NE])
        gs = sb(fs, "gs", [P, NT])
        fs.close()

        def pb(name):
            return es.enter_context(nc.psum_tensor(name, [P, 2, 512], F32))
        pj, sc, tp, pv = pb("pj"), pb("sc"), pb("tp"), pb("pv")

        s_const = sem("s_const")
        s_x = [sem(f"s_x{i}") for i in range(2)]
        s_ctx = [sem(f"s_ctx{i}") for i in range(KT)]
        s_w = [sem(f"s_w{i}") for i in range(2)]
        s_row = sem("s_row")
        s_row2 = sem("s_row2")
        s_out = sem("s_out")
        whi = sem("whi")
        wlo = sem("wlo")
        chi = sem("chi")
        clo = sem("clo")
        mh_set = sem("mh_set")
        dve_seq = sem("dve_seq")
        ln_var = sem("ln_var")
        ln_rstd = sem("ln_rstd")
        ln_xn = sem("ln_xn")
        ln_t = sem("ln_t")
        ln_hi = sem("ln_hi")
        pj_dve = sem("pj_dve")
        pj_act = sem("pj_act")
        proj = sem("proj")
        t1_done = sem("t1_done")
        sin_done = sem("sin_done")
        rope = sem("rope")
        tp_t = sem("tp_t")
        tp_hi = sem("tp_hi")
        tp_lo = sem("tp_lo")
        scored = sem("scored")
        masked = sem("masked")
        maxed = sem("maxed")
        subbed = sem("subbed")
        exped = sem("exped")
        summed = sem("summed")
        recd = sem("recd")
        normed = sem("normed")
        pv_t = sem("pv_t")
        pv_hi = sem("pv_hi")
        pv_lo = sem("pv_lo")
        outp = sem("outp")
        zeroed = sem("zeroed")
        bq_done = sem("bq_done")
        k_done, q_done, v_done = sem("k_done"), sem("q_done"), sem("v_done")
        vt_t, vc_done = sem("vt_t"), sem("vc_done")
        pt_t, pt_done = sem("pt_t"), sem("pt_done")
        spv, ssel, ssel1 = sem("spv"), sem("ssel"), sem("ssel1")
        o_hi, o_lo = sem("o_hi"), sem("o_lo")
        xbo = sem("xbo")
        hg_t, hg_c = sem("hg_t"), sem("hg_c")
        gate = sem("gate")
        gexp = sem("gexp")
        hw_done = sem("hw_done")
        hw_t, hw_hi, hw_lo = sem("hw_t"), sem("hw_hi"), sem("hw_lo")
        fin_t, fin = sem("fin_t"), sem("fin")

        ident = cst[:, C_ID:C_ID + P]

        def rep(ap, n):
            return ap.unsqueeze(1).to_broadcast([ap.shape[0], n, S])

        def per_group(ap, n):
            return ap.unsqueeze(2).to_broadcast([P, n, S])

        mask3 = rep(cst[:, C_MASK:C_MASK + S], 8)
        W_X = 5 * NKV
        PD_LN1 = NT
        PD_X = PD_LN1 + 4 * NU
        PD_LN2 = PD_X + NT
        PD_O = PD_LN2 + NT
        PD_LN3 = PD_O + NT
        PA_X = XT * NU
        N_SM = XCH * NU
        N_SS = SCH * NSU

        late = []
        for t in range(KT):
            late.append((w_s[t, :, 0:1024], wsh[:, t, :, 0:256], wsl[:, t, :, 0:256], 256))
            late.append((w_s[t, :, 1024:1536], wsh[:, t, :, 256:384], wsl[:, t, :, 256:384], 128))
        for i in range(2):
            late.append((w_o[:, i * 1024:(i + 1) * 1024], woh[:, 2 * i:2 * i + 2, :], wol[:, 2 * i:2 * i + 2, :], D))
        N_SELF = len(late)
        for i in range(2):
            late.append((w_b[:, i * 1024:(i + 1) * 1024], wbh[:, 2 * i:2 * i + 2, :], wbl[:, 2 * i:2 * i + 2, :], D))
        late.append((w_eb, weh[:, :].unsqueeze(1), wel[:, :].unsqueeze(1), D))

        def late_buf(i):
            b = 1 - i % 2
            return b, 16 * ((17 if b == 0 else 23) + i // 2 + 1)

        def late_raw(i):
            width = late[i][3]
            n = late[i][1].shape[1]
            return raw[late_buf(i)[0]][:, 0:n * width].rearrange("p (k c) -> p k c", k=n)

        def fin_bank(i):
            return (pj, sc, pv)[i // 2 % 3][:, i % 2, :]

        block = es.enter_context(nc.Block())

        @block.sync
        def _(sp):
            sp.dma_start(cst[:, :], consts).then_inc(s_const, 16)
            sp.dma_start(bcol[:, :, :], bias_cols).then_inc(s_const, 16)
            sp.dma_start(bthr[:, :], b_thr).then_inc(s_const, 16)
            rawctx = qr2[:, :, :, :, :].rearrange("p a b r s -> p (a b r s)").rearrange("p (k t) -> p k t", k=KT)
            sp.dma_start(raw[0][:, :], w_x[0, :, 0, :]).then_inc(s_w[0], 16)
            for k in range(KT):
                sp.dma_start(rawctx[:, k, :], ctxT[k]).then_inc(s_ctx[k], 16)
            for i in range(2):
                sp.dma_start(X[:, 4 * i:4 * i + 4, :], x[:, 4 * i:4 * i + 4, :]).then_inc(s_x[i], 16)
            sp.dma_start(raw[1][:, :], w_x[0, :, 1, :]).then_inc(s_w[1], 16)
            sp.wait_ge(wlo, 1)
            sp.dma_start(raw[0][:, :], w_x[0, :, 2, :]).then_inc(s_w[0], 16)

            def stream(g, last):
                srcs = [(g, 3), (g, 4)] + ([] if last else [(g + 1, 0), (g + 1, 1), (g + 1, 2)])
                for i, (gg, j) in enumerate(srcs):
                    src = w_x[gg, :, j, :]
                    b = (1, 0, 1, 0, 1)[i]
                    sp.wait_ge(wlo, 5 * g + (3, 3, 4, 5, 6)[i])
                    sp.dma_start(raw[b][:, :], src).then_inc(s_w[b], 16)

            with sp.Fori(0, NKV - 1) as g:
                stream(g, False)
            stream(NKV - 1, True)

            def late_load(i):
                b, _ = late_buf(i)
                sp.wait_ge(wlo, W_X + i - 1)
                n = late[i][1].shape[1] * late[i][3]
                sp.dma_start(raw[b][:, 0:n], late[i][0]).then_inc(s_w[b], 16)

            late_load(0)
            sp.wait_ge(pj_dve, PD_X)
            sp.dma_start(brow_o[:, :], bias_rows[0]).then_inc(s_row, 16)
            for i in range(1, len(late)):
                late_load(i)
            sp.wait_ge(pj_dve, PD_O)
            sp.dma_start(wag[:, :, :], w_ag).then_inc(s_row2, 16)
            sp.dma_start(brow_b[:, :], bias_rows[1]).then_inc(s_row2, 16)
            for i in range(NT):
                sp.wait_ge(fin, i + 1)
                sp.dma_start(out[:, i, :], X[:, i, :]).then_inc(s_out, 16)
            sp.wait_ge(s_out, 16 * NT)

        @block.gpsimd
        def _(pool):
            pool.memset(mhalf[:, :], -0.5).then_inc(mh_set, 1)

            def split_lo(n, hi, lo, src):
                pool.wait_ge(whi, n + 1)
                pool.tensor_tensor(lo, src, hi.bitcast(F32), ALU.subtract).then_inc(wlo, 1)

            def split_x(n, j, b):
                r = raw[b][:, :]
                if j < 3:
                    split_lo(n, wqh[:, j].rearrange("p k c -> p (k c)"), wql[:, j].rearrange("p k c -> p (k c)"), r)
                else:
                    i = 2 * (j - 3)
                    split_lo(n, wdh[:, i:i + 2].rearrange("p k c -> p (k c)"),
                             wdl[:, i:i + 2].rearrange("p k c -> p (k c)"), r)

            def ln_pow(grp):
                pool.wait_ge(ln_var, grp + 1)
                c = slice(4 * (grp % 2), 4 * (grp % 2) + 4)
                pool.tensor_tensor(rstd[:, c], veps[:, c], mhalf[:, c], ALU.pow).then_inc(ln_rstd, 1)

            rawctx = qr2[:, :, :, :, :].rearrange("p a b r s -> p (a b r s)").rearrange("p (k t) -> p k t", k=KT)
            split_x(0, 0, 0)
            for k in range(KT):
                pool.wait_ge(chi, k + 1)
                pool.tensor_tensor(al[:, k, :], rawctx[:, k, :], ah[:, k, :].bitcast(F32),
                                   ALU.subtract).then_inc(clo, 1)
            pool.wait_ge(mh_set, 1)
            ln_pow(0)
            ln_pow(1)
            split_x(1, 1, 1)
            split_x(2, 2, 0)

            def rope_tile(u, h, idx):
                par = (h + idx) % 2
                pj_n = XT * u + (1 if idx == 0 else 2 + idx)
                pool.wait_ge(pj_act, pj_n)
                pool.tensor_tensor(sw[par][:, :].rearrange("p (b s) -> p b s", s=S),
                                   sw[par][:, :].rearrange("p (b s) -> p b s", s=S),
                                   rep(cst[:, C_SIN:C_SIN + S], HB), ALU.mult).then_inc(sin_done, 1)
                pool.wait_ge(sin_done, 5 * u + idx + 1)
                o = kr[h][:, :, :] if idx == 0 else qr[h][:, :, idx - 1, :]
                pool.tensor_tensor(o, t1[par][:, :].rearrange("p (b s) -> p b s", s=S),
                                   sw[par][:, :].rearrange("p (b s) -> p b s", s=S),
                                   ALU.add).then_inc(rope, 1)

            def subtract_max(n, c):
                pool.wait_ge(maxed, n + 1)
                s3 = sm[c][:, :].rearrange("p (n s) -> p n s", s=S)
                pool.tensor_tensor(s3, s3, per_group(mx[:, c, :], 8), ALU.subtract).then_inc(subbed, 1)

            def normalise(n, c):
                pool.wait_ge(recd, n + 1)
                s3 = sm[c][:, :].rearrange("p (n s) -> p n s", s=S)
                pool.tensor_tensor(s3, s3, per_group(rz[:, c, :], 8), ALU.mult).then_inc(normed, 1)

            for idx in range(5):
                rope_tile(0, 0, idx)

            def phase(u, h, g, nxt):
                subtract_max(2 * u, 0)
                subtract_max(2 * u + 1, 1)
                normalise(2 * u, 0)
                if nxt:
                    rope_tile(u + 1, 1 - h, 0)
                normalise(2 * u + 1, 1)
                if nxt:
                    rope_tile(u + 1, 1 - h, 1)
                if h == 0:
                    split_x(5 * g + 3, 3, 1)
                    split_x(5 * g + 4, 4, 0)
                if nxt:
                    for idx in range(2, 5):
                        rope_tile(u + 1, 1 - h, idx)
                if h == 0 and nxt == "loop":
                    split_x(5 * g + 5, 0, 1)
                    split_x(5 * g + 6, 1, 0)
                    split_x(5 * g + 7, 2, 1)

            with pool.Fori(0, NKV - 1) as g:
                phase(2 * g, 0, g, "loop")
                phase(2 * g + 1, 1, g, "loop")
            phase(NU - 2, 0, NKV - 1, "last")
            phase(NU - 1, 1, NKV - 1, None)

            def late_lo(i):
                split_lo(W_X + i, late[i][1], late[i][2], late_raw(i))

            pool.wait_ge(pj_dve, PD_X)
            for i in range(2):
                pool.memset(kb[i][:, :, :, :], 0.0)
                pool.memset(vc[i][:, :, :, :], 0.0).then_inc(zeroed, 1)
            late_lo(0)
            late_lo(1)
            ln_pow(2)
            ln_pow(3)
            late_lo(2)
            late_lo(3)
            pool.wait_ge(s_row, 16)
            pool.wait_ge(ln_xn, 2 * NT)
            for i in range(NT):
                pool.tensor_tensor(X[:, i, :], X[:, i, :], brow_o[:, :], ALU.add).then_inc(xbo, 1)
            nl = 4
            subtract_max(N_SM, 0)
            subtract_max(N_SM + 1, 1)
            for n in range(N_SS):
                if n == 0:
                    normalise(N_SM, 0)
                if n + 1 < N_SS:
                    normalise(N_SM + n + 1, (n + 1) % 2)
                if n + 2 < N_SS:
                    subtract_max(N_SM + n + 2, n % 2)
                if n % 2 == 1 and nl < N_SELF:
                    late_lo(nl)
                    nl += 1
                if n % SCH == SCH - 1:
                    v = n // SCH
                    t, h = v // 2, v % 2
                    pool.wait_ge(o_hi, v + 1)
                    pool.tensor_tensor(al[:, t, h * HALF:(h + 1) * HALF], ot[h][:, :],
                                       ah[:, t, h * HALF:(h + 1) * HALF].bitcast(F32),
                                       ALU.subtract).then_inc(o_lo, 1)
            assert nl == N_SELF
            late_lo(N_SELF)
            late_lo(N_SELF + 1)
            late_lo(N_SELF + 2)
            ln_pow(4)
            ln_pow(5)
            pool.wait_ge(s_row2, 32)
            pool.wait_ge(ln_xn, 3 * NT)
            for i in range(NT):
                pool.tensor_tensor(X[:, i, :], X[:, i, :], brow_b[:, :], ALU.add).then_inc(xbo, 1)

        @block.scalar
        def _(act):
            def hi(src, dst, s):
                act.activation(dst, src, ACT.Copy).then_inc(s, 1)

            def split_x(j, b, w_n):
                act.wait_ge(s_w[b], 16 * w_n)
                if j < 3:
                    hi(raw[b][:, :], wqh[:, j].rearrange("p k c -> p (k c)"), whi)
                else:
                    hi(raw[b][:, :], wdh[:, 2 * (j - 3):2 * (j - 3) + 2].rearrange("p k c -> p (k c)"), whi)

            def ln_hi_tile(n, also=None):
                i = n % NT
                act.wait_ge(ln_t, n + 1)
                src = pj[:, i % 2, :].rearrange("p (k t) -> p k t", k=KT)
                if also is not None:
                    act.activation(also[:, :, i * P:(i + 1) * P], src, ACT.Copy)
                hi(src, xh[:, :, i * P:(i + 1) * P], ln_hi)

            rawctx = qr2[:, :, :, :, :].rearrange("p a b r s -> p (a b r s)").rearrange("p (k t) -> p k t", k=KT)
            split_x(0, 0, 1)
            for k in range(KT):
                act.wait_ge(s_ctx[k], 16)
                hi(rawctx[:, k, :], ah[:, k, :], chi)
            split_x(1, 1, 1)
            split_x(2, 0, 2)

            def swap_halves(u, h, idx, first):
                par = (h + idx) % 2
                act.wait_ge(t1_done, 5 * u + idx + 1)
                if not (first and idx < 2):
                    act.wait_ge(rope, 5 * u + idx - 1)
                bank = (1 + idx) % 2 if idx else 0
                src = pj[:, bank, :]
                act.activation(sw[par][0:64, :], src[64:128, :], ACT.Copy)
                act.activation(sw[par][64:128, :], src[0:64, :], ACT.Copy).then_inc(pj_act, 1)

            def copy_v(u):
                act.wait_ge(proj, XT * u + 2)
                act.activation(vt[:, :, :, :], pj[:, 1, :].rearrange("p (b s) -> p b s", s=S).unsqueeze(2)
                               .to_broadcast([P, HB, 2, S]), ACT.Copy).then_inc(pj_act, 1)

            def v_hi(u, h):
                act.wait_ge(tp_t, 3 * u + 1)
                hi(tp[:, :, :].rearrange("p a c -> p (a c)"), v2h[h][:, :, :].rearrange("p b d -> p (b d)"), tp_hi)

            def p_hi(u, c):
                act.wait_ge(tp_t, 3 * u + 2 + c)
                for hp in range(2):
                    last = act.activation(pt[c][0:64, :].rearrange("p (b r q) -> p b r q", b=4, r=2)[:, :, hp, :],
                                          tp[64 * hp:64 * hp + 64, c, :].rearrange("p (b q) -> p b q", b=4), ACT.Copy)
                last.then_inc(tp_hi, 1)

            def exp(n, c, scale):
                act.wait_ge(subbed, n + 1)
                act.activation(sm[c][:, :], sm[c][:, :], ACT.Exp, scale=scale).then_inc(exped, 1)

            def c_hi(u, c):
                act.wait_ge(pv_t, 2 * u + c + 1)
                for r in range(REP):
                    last = act.activation(
                        ch[:, r, c * 256:(c + 1) * 256].rearrange("p (b q) -> p b q", q=S),
                        pv[:, :, :].rearrange("p a (b r q) -> p (a b) r q", b=2, r=REP)[:, :, r, :], ACT.Copy)
                last.then_inc(pv_hi, 1)

            swap_halves(0, 0, 0, True)
            copy_v(0)
            v_hi(0, 0)
            for n in range(NT):
                ln_hi_tile(n)
            for idx in range(1, 5):
                swap_halves(0, 0, idx, True)

            def phase(u, h, g, nxt):
                exp(2 * u, 0, X_SCALE)
                if nxt:
                    swap_halves(u + 1, 1 - h, 0, False)
                exp(2 * u + 1, 1, X_SCALE)
                if nxt:
                    copy_v(u + 1)
                p_hi(u, 0)
                if nxt:
                    swap_halves(u + 1, 1 - h, 1, False)
                p_hi(u, 1)
                if h == 0:
                    act.wait_ge(pj_dve, PD_LN1 + 8 * g)
                    split_x(3, 1, 2 + 3 * g)
                    split_x(4, 0, 3 + 2 * g)
                if nxt:
                    swap_halves(u + 1, 1 - h, 2, False)
                    v_hi(u + 1, 1 - h)
                c_hi(u, 0)
                if nxt:
                    swap_halves(u + 1, 1 - h, 3, False)
                c_hi(u, 1)
                if nxt:
                    swap_halves(u + 1, 1 - h, 4, False)
                if h == 0 and nxt == "loop":
                    split_x(0, 1, 3 + 3 * g)
                    split_x(1, 0, 4 + 2 * g)
                    split_x(2, 1, 4 + 3 * g)

            with act.Fori(0, NKV - 1) as g:
                phase(2 * g, 0, g, "loop")
                phase(2 * g + 1, 1, g, "loop")
            phase(NU - 2, 0, NKV - 1, "last")
            phase(NU - 1, 1, NKV - 1, None)

            def late_hi(i):
                b, n = late_buf(i)
                act.wait_ge(s_w[b], n)
                act.activation(late[i][1], late_raw(i), ACT.Copy).then_inc(whi, 1)

            act.wait_ge(pj_dve, PD_X)
            late_hi(0)
            late_hi(1)
            act.wait_ge(s_const, 48)
            for par in range(2):
                act.activation(bqm[:, par, :], bcol[:, 0, :], ACT.Copy,
                               scale=cst[:, C_PAR + par:C_PAR + par + 1]).then_inc(bq_done, 1)
            late_hi(2)
            late_hi(3)
            for n in range(NT, 2 * NT):
                ln_hi_tile(n)
            nl = 4

            def k_tile(v):
                t, h = v // 2, v % 2
                act.wait_ge(proj, PA_X + ST * v + 1)
                src = pj[:, (ST * v) % 2, :].rearrange("p (b s) -> p b s", s=S)
                for j in range(4):
                    r = slice(32 * j, 32 * j + 32)
                    last = act.activation(kb[h][r, :, j, :], src[r], ACT.Identity, bias=bcol[r, 1, t:t + 1])
                last.then_inc(pj_act, 1)

            def q_tile(v):
                t, h = v // 2, v % 2
                act.wait_ge(proj, PA_X + ST * v + 2)
                src = pj[:, (ST * v + 1) % 2, :].rearrange("p (b s) -> p b s", s=S)
                for par in range(2):
                    last = act.activation(qm[h][:, :, par, :], src, ACT.Identity,
                                          bias=bqm[:, par, t:t + 1], scale=cst[:, C_PAR + par:C_PAR + par + 1])
                last.then_inc(pj_act, 1)

            def v_tile(v):
                t = v // 2
                act.wait_ge(proj, PA_X + ST * v + 3)
                act.activation(vts[:, :], pj[:, (ST * v + 2) % 2, :], ACT.Copy).then_inc(pj_act, 1)

            def pt_copy(n):
                act.wait_ge(pt_t, n + 1)
                act.activation(pts[n % 2][:, :], tp[:, n % 2, :], ACT.Copy).then_inc(pt_done, 1)

            act.wait_ge(zeroed, 2)
            act.wait_ge(bq_done, 2)
            k_tile(0)
            q_tile(0)
            v_tile(0)
            exp(N_SM, 0, S_SCALE)
            exp(N_SM + 1, 1, S_SCALE)
            for n in range(N_SS):
                v, c = n // SCH, n % SCH
                pt_copy(n)
                if v + 1 < NSU and c < 3:
                    (k_tile, q_tile, v_tile)[c](v + 1)
                if n % 2 == 1 and nl < N_SELF:
                    late_hi(nl)
                    nl += 1
                if n + 2 < N_SS:
                    exp(N_SM + n + 2, n % 2, S_SCALE)
                if c == SCH - 1:
                    t, h = v // 2, v % 2
                    act.wait_ge(ssel, n + 1)
                    hi(ot[h][:, :], ah[:, t, h * HALF:(h + 1) * HALF], o_hi)
            assert nl == N_SELF
            act.wait_ge(pj_dve, PD_O)
            for i in range(3):
                late_hi(N_SELF + i)
            for n in range(2 * NT, 3 * NT):
                ln_hi_tile(n, xf)
            act.wait_ge(gate, 3)
            act.activation(ge[:, :, :], ge[:, :, :], ACT.Exp)
            act.activation(gt[:, :], gt[:, :], ACT.Exp, scale=-1.0).then_inc(gexp, 1)
            for i in range(2):
                act.wait_ge(hw_t, i + 1)
                hi(tp[:, i, :], hth[:, i * 512:(i + 1) * 512], hw_hi)

        @block.vector
        def _(dve):
            seq = [0]

            def link(ins):
                seq[0] += 1
                ins.then_inc(dve_seq, 1)
                dve.wait_ge(dve_seq, seq[0])

            def ln_stats(i):
                dve.bn_stats(stats[:, i, :], X[:, i, :]).then_inc(dve_seq, 1)
                seq[0] += 1
                dve.wait_ge(dve_seq, seq[0])
                dve.bn_aggr(mv[:, i, :], stats[:, i, :]).then_inc(dve_seq, 1)
                seq[0] += 1

            def ln_eps(grp):
                dve.wait_ge(dve_seq, seq[0])
                c = slice(4 * grp, 4 * grp + 4)
                dve.tensor_scalar(veps[:, c], mv[:, c, 1], EPS, None, ALU.add).then_inc(ln_var, 1)

            def ln_apply(n, xn):
                i = n % NT
                if i % 4 == 0:
                    dve.wait_ge(ln_rstd, n // 4 + 1)
                if i >= 2:
                    dve.wait_ge(ln_t, n - 1)
                dve.tensor_scalar(xn[i % 2], X[:, i, :], mv[:, i, 0:1], rstd[:, i:i + 1],
                                  ALU.subtract, ALU.mult).then_inc(ln_xn, 1)

            def ln_lo(n):
                i = n % NT
                dve.wait_ge(ln_hi, n + 1)
                dve.tensor_tensor(xl[:, :, i * P:(i + 1) * P], pj[:, i % 2, :].rearrange("p (k t) -> p k t", k=KT),
                                  xh[:, :, i * P:(i + 1) * P].bitcast(F32), ALU.subtract).then_inc(pj_dve, 1)

            def ln_all(stage, xn):
                for i in range(NT):
                    ln_apply(stage * NT + i, xn)
                    if i:
                        ln_lo(stage * NT + i - 1)
                ln_lo(stage * NT + NT - 1)

            def rope_cos(u, h, idx, first):
                par = (h + idx) % 2
                tile = 0 if idx == 0 else 1 + idx
                dve.wait_ge(proj, XT * u + tile + 1)
                if not (first and idx < 2):
                    dve.wait_ge(rope, 5 * u + idx - 1)
                bank = tile % 2
                dve.tensor_tensor(t1[par][:, :].rearrange("p (b s) -> p b s", s=S),
                                  pj[:, bank, :].rearrange("p (b s) -> p b s", s=S),
                                  rep(cst[:, C_COS:C_COS + S], HB), ALU.mult).then_inc(t1_done, 1)

            def mask_max(n, c):
                s3 = sm[c][:, :].rearrange("p (n s) -> p n s", s=S)
                dve.wait_ge(scored, n + 1)
                dve.tensor_tensor(s3, sc[:, c, :].rearrange("p (n s) -> p n s", s=S), mask3,
                                  ALU.add).then_inc(masked, 1)
                dve.wait_ge(masked, n + 1)
                dve.tensor_reduce(mx[:, c, :], s3, AXX, ALU.max).then_inc(maxed, 1)

            def sum_rec(n, c):
                dve.wait_ge(exped, n + 1)
                dve.tensor_reduce(zs[:, c, :], sm[c][:, :].rearrange("p (n s) -> p n s", s=S), AXX,
                                  ALU.add).then_inc(summed, 1)
                dve.wait_ge(summed, n + 1)
                dve.reciprocal(rz[:, c, :], zs[:, c, :]).then_inc(recd, 1)

            def v_lo(u, h):
                dve.wait_ge(tp_hi, 3 * u + 1)
                dve.tensor_tensor(v2l[h][:, :, :].rearrange("p b d -> p (b d)"),
                                  tp[:, :, :].rearrange("p a c -> p (a c)"),
                                  v2h[h][:, :, :].rearrange("p b d -> p (b d)").bitcast(F32),
                                  ALU.subtract).then_inc(tp_lo, 1)

            def p_lo(u, c):
                dve.wait_ge(tp_hi, 3 * u + 2 + c)
                for hp in range(2):
                    p4 = pt[c][:, :].rearrange("p (b r q) -> p b r q", b=4, r=2)[:, :, hp, :]
                    last = dve.tensor_tensor(p4[64:128], tp[64 * hp:64 * hp + 64, c, :].rearrange("p (b q) -> p b q", b=4),
                                             p4[0:64].bitcast(F32), ALU.subtract)
                last.then_inc(tp_lo, 1)

            def c_lo(u, c):
                dve.wait_ge(pv_hi, 2 * u + c + 1)
                for r in range(REP):
                    cs = slice(c * 256, (c + 1) * 256)
                    last = dve.tensor_tensor(
                        cl[:, r, cs].rearrange("p (b q) -> p b q", q=S),
                        pv[:, :, :].rearrange("p a (b r q) -> p (a b) r q", b=2, r=REP)[:, :, r, :],
                        ch[:, r, cs].bitcast(F32).rearrange("p (b q) -> p b q", q=S), ALU.subtract)
                last.then_inc(pv_lo, 1)

            def out_add(u, h, i):
                dve.wait_ge(outp, 4 * u + i + 1)
                dve.tensor_tensor(X[:, 4 * h + i, :], X[:, 4 * h + i, :], pj[:, i % 2, :],
                                  ALU.add).then_inc(pj_dve, 1)

            dve.wait_ge(s_x[0], 16)
            for i in range(4):
                ln_stats(i)
            ln_eps(0)
            dve.wait_ge(s_x[1], 16)
            for i in range(4, NT):
                ln_stats(i)
            ln_eps(1)
            dve.wait_ge(s_const, 48)
            rope_cos(0, 0, 0, True)
            v_lo(0, 0)
            xn1 = [t1[1][:, :], sw[1][:, :]]
            ln_all(0, xn1)
            for idx in range(1, 5):
                rope_cos(0, 0, idx, True)

            def phase(u, h, g, nxt):
                mask_max(2 * u, 0)
                mask_max(2 * u + 1, 1)
                if nxt:
                    rope_cos(u + 1, 1 - h, 0, False)
                sum_rec(2 * u, 0)
                sum_rec(2 * u + 1, 1)
                p_lo(u, 0)
                if nxt:
                    rope_cos(u + 1, 1 - h, 1, False)
                p_lo(u, 1)
                if nxt:
                    rope_cos(u + 1, 1 - h, 2, False)
                    v_lo(u + 1, 1 - h)
                c_lo(u, 0)
                if nxt:
                    rope_cos(u + 1, 1 - h, 3, False)
                c_lo(u, 1)
                if nxt:
                    rope_cos(u + 1, 1 - h, 4, False)
                for i in range(4):
                    out_add(u, h, i)

            with dve.Fori(0, NKV - 1) as g:
                phase(2 * g, 0, g, "loop")
                phase(2 * g + 1, 1, g, "loop")
            phase(NU - 2, 0, NKV - 1, "last")
            phase(NU - 1, 1, NKV - 1, None)

            dve.wait_ge(pj_dve, PD_X)
            for i in range(NT):
                ln_stats(i)
                if i % 4 == 3:
                    ln_eps(i // 4)
            ln_all(1, [xns[i][:, :] for i in range(2)])

            def vc_copy(v):
                h = v % 2
                dve.wait_ge(vt_t, v + 1)
                src = tp[:, 0, :].rearrange("p (b t j d) -> p b t j d", b=4, t=2, j=2)
                dst = vc[h][:, :, :, :].rearrange("p (b o) t c -> p b o t c", o=2)
                for j in range(2):
                    for odd in range(2):
                        last = dve.tensor_copy(dst[64 * j:64 * j + 64, :, odd, :, 32 * j:32 * j + 32],
                                               src[64 * odd:64 * odd + 64, :, :, j, :])
                last.then_inc(vc_done, 1)

            def select_out(n):
                v, c = n // SCH, n % SCH
                t, h = v // 2, v % 2
                src = pv[:, n % 2, 0:256].rearrange("p (b r q) -> p b r q", b=2, r=2)
                dve.wait_ge(spv, n + 1)
                if n >= 2:
                    dve.wait_ge(ssel, n - 1)
                o3 = osel[n % 2][:, :].rearrange("p (b q) -> p b q", q=S)
                dve.tensor_scalar(o3, src[:, :, 0, :], cst[:, C_PAR:C_PAR + 1], bcol[:, 2, t:t + 1],
                                  ALU.mult, ALU.add).then_inc(ssel1, 1)
                dve.wait_ge(ssel1, n + 1)
                if c == 0 and v >= 2:
                    dve.wait_ge(o_lo, v - 1)
                dve.scalar_tensor_tensor(ot[h][:, c * P:(c + 1) * P].rearrange("p (b q) -> p b q", q=S),
                                         src[:, :, 1, :], cst[:, C_PAR + 1:C_PAR + 2], o3,
                                         ALU.mult, ALU.add).then_inc(ssel, 1)

            dve.wait_ge(zeroed, 2)
            vc_copy(0)
            mask_max(N_SM, 0)
            mask_max(N_SM + 1, 1)
            sum_rec(N_SM, 0)
            for n in range(N_SS):
                if n + 1 < N_SS:
                    sum_rec(N_SM + n + 1, (n + 1) % 2)
                if n + 2 < N_SS:
                    mask_max(N_SM + n + 2, n % 2)
                select_out(n)
                if n % SCH == SCH - 1 and n // SCH + 1 < NSU:
                    vc_copy(n // SCH + 1)
            for i in range(NT):
                dve.wait_ge(outp, 4 * NU + i + 1)
                dve.wait_ge(xbo, i + 1)
                dve.tensor_tensor(X[:, i, :], X[:, i, :], pj[:, i % 2, :], ALU.add).then_inc(pj_dve, 1)
                dve.wait_ge(pj_dve, PD_LN2 + i + 1)
                ln_stats(i)
                if i % 4 == 3:
                    ln_eps(i // 4)
            ln_all(2, [xnf[i][:, :] for i in range(2)])
            for i in range(4):
                dve.wait_ge(hg_t, i + 1)
                dve.tensor_copy(hg[:, 2 * i:2 * i + 2, :],
                                tp[:, i % 2, 0:2 * (P + NG)].rearrange("p (a c) -> p a c", a=2)).then_inc(hg_c, 1)
            dve.wait_ge(hg_c, 4)
            logits = hg[:, :, P:P + NE]

            def per_e(ap):
                return ap.unsqueeze(2).to_broadcast([P, NT, NE])

            dve.tensor_reduce(gm[:, :], logits, AXX, ALU.max).then_inc(gate, 1)
            dve.wait_ge(gate, 1)
            dve.tensor_tensor(ge[:, :, :], logits, per_e(gm[:, :]), ALU.subtract).then_inc(gate, 1)
            dve.tensor_scalar(gt[:, :], hg[:, :, P + NE], bthr[:, 0:1], None, ALU.add).then_inc(gate, 1)
            dve.wait_ge(gexp, 1)
            link(dve.tensor_reduce(gz[:, :], ge[:, :, :], AXX, ALU.add))
            link(dve.reciprocal(gr[:, :], gz[:, :]))
            link(dve.tensor_tensor(ge[:, :, :], ge[:, :, :], per_e(gr[:, :]), ALU.mult))
            link(dve.tensor_scalar(gt[:, :], gt[:, :], 1.0, None, ALU.add))
            link(dve.reciprocal(gt[:, :], gt[:, :]))
            link(dve.tensor_scalar(gt[:, :], gt[:, :], MAX_THR, None, ALU.mult))
            link(dve.tensor_tensor(gw[:, :, :], ge[:, :, :], per_e(gt[:, :]), ALU.subtract))
            link(dve.tensor_scalar(gw[:, :, :], gw[:, :, :], 0.0, None, ALU.max))
            link(dve.tensor_reduce(gs[:, :], gw[:, :, :], AXX, ALU.add))
            link(dve.tensor_scalar(gm[:, :], gs[:, :], 0.0, None, ALU.is_equal))
            link(dve.tensor_tensor(gs[:, :], gs[:, :], gm[:, :], ALU.add))
            link(dve.reciprocal(gs[:, :], gs[:, :]))
            link(dve.tensor_scalar(gs[:, :], gs[:, :], SCALING, None, ALU.mult))
            link(dve.tensor_tensor(gw[:, :, :], gw[:, :, :], per_e(gs[:, :]), ALU.mult))
            for i in range(NT):
                dve.tensor_tensor(hw[:, i, :].rearrange("p (e r) -> p e r", r=NR),
                                  hg[:, i, 0:P].rearrange("p (e r) -> p e r", r=NR),
                                  gw[:, i, :].unsqueeze(2).to_broadcast([P, NE, NR]),
                                  ALU.mult).then_inc(hw_done, 1)
            for i in range(2):
                dve.wait_ge(hw_hi, i + 1)
                dve.tensor_tensor(htl[:, i * 512:(i + 1) * 512], tp[:, i, :],
                                  hth[:, i * 512:(i + 1) * 512].bitcast(F32), ALU.subtract).then_inc(hw_lo, 1)
            for i in range(NT):
                dve.wait_ge(fin_t, i + 1)
                dve.wait_ge(xbo, NT + i + 1)
                dve.tensor_tensor(X[:, i, :], X[:, i, :], fin_bank(i), ALU.add).then_inc(fin, 1)

        @block.tensor
        def _(pe):
            def three(o, pairs):
                n = 3 * len(pairs)
                m = 0
                for (wh, wl), (mh, ml) in pairs:
                    for w, r in ((wh, mh), (wh, ml), (wl, mh)):
                        last = pe.matmul(o, w, r, start=(m == 0), stop=(m == n - 1))
                        m += 1
                return last

            def ln_tile(n, xn):
                i = n % NT
                pe.wait_ge(ln_xn, n + 1)
                for k in range(KT):
                    last = pe.transpose(pj[:, i % 2, k * P:(k + 1) * P], xn[i % 2][:, k * P:(k + 1) * P], ident)
                last.then_inc(ln_t, 1)

            def proj_x(u, h, tile):
                piece, col = (0, tile) if tile < 2 else (1 + (tile - 2) // 2, tile % 2)
                tok = slice(h * HALF, (h + 1) * HALF)
                a, b = (ah, al) if tile < 2 else (xh, xl)
                c = slice(col * P, (col + 1) * P)
                three(pj[:, tile % 2, :],
                      [((wqh[:, piece, k, c], wql[:, piece, k, c]), (a[:, k, tok], b[:, k, tok]))
                       for k in range(KT)]).then_inc(proj, 1)

            def v_transposes(u, h):
                pe.wait_ge(pj_act, XT * u + 2)
                for b in range(HB):
                    last = pe.transpose(tp[:, b // 4, (b % 4) * P:(b % 4 + 1) * P],
                                        vt[:, b, :, :], ident)
                last.then_inc(tp_t, 1)

            def scores_x(u, h, c):
                for b in range(4):
                    bb = 4 * c + b
                    for hp in range(2):
                        last = pe.matmul(sc[:, c, (2 * b + hp) * S:(2 * b + hp + 1) * S],
                                         qr[h][:, bb, 2 * hp:2 * hp + 2, :], kr[h][:, bb, :],
                                         start=True, stop=True)
                last.then_inc(scored, 1)

            def p_transposes(u, c):
                for b in range(4):
                    last = pe.transpose(tp[:, c, b * P:(b + 1) * P], sm[c][:, b * P:(b + 1) * P], ident)
                last.then_inc(tp_t, 1)

            def pv_x(u, h, c):
                for b in range(4):
                    o = pv[:, b // 2, (b % 2) * 256:(b % 2 + 1) * 256]
                    p = pt[c][:, b * 256:(b + 1) * 256]
                    pe.matmul(o, v2h[h][:, 4 * c + b, :], p, start=True, stop=False)
                    last = pe.matmul(o, v2l[h][:, 4 * c + b, :], p, start=False, stop=True)
                last.then_inc(pv_t, 1)

            def out_x(u, i):
                tok = slice(i * P, (i + 1) * P)
                three(pj[:, i % 2, :], [((ch[:, r, tok], cl[:, r, tok]), (wdh[:, r, :], wdl[:, r, :]))
                                        for r in range(REP)]).then_inc(outp, 1)

            pe.wait_ge(s_const, 48)
            pe.wait_ge(wlo, 1)
            pe.wait_ge(clo, KT)
            proj_x(0, 0, 0)
            proj_x(0, 0, 1)
            v_transposes(0, 0)
            for n in range(NT):
                if n < 2:
                    pe.wait_ge(pj_act, n + 1)
                else:
                    pe.wait_ge(pj_dve, n - 1)
                ln_tile(n, [t1[1][:, :], sw[1][:, :]])
            for tile in range(2, XT):
                if tile == 2:
                    pe.wait_ge(pj_dve, NT)
                    pe.wait_ge(wlo, 2)
                if tile >= 4:
                    pe.wait_ge(pj_act, tile - 1)
                if tile == 4:
                    pe.wait_ge(wlo, 3)
                proj_x(0, 0, tile)

            def phase(u, h, g, nxt):
                n = u + 1

                def project(tile):
                    if not nxt:
                        return
                    if tile < 2:
                        pe.wait_ge(pj_act, XT * u + 5 + tile)
                        pe.wait_ge(pj_dve, PD_LN1 + 4 * u - 1 + tile)
                    else:
                        pe.wait_ge(pj_act, XT * n + tile - 1)
                    if h == 1 and tile in (0, 2, 4):
                        pe.wait_ge(wlo, 5 * (g + 1) + 1 + tile // 2)
                    proj_x(n, 1 - h, tile)

                pe.wait_ge(rope, 5 * u + 5)
                scores_x(u, h, 0)
                scores_x(u, h, 1)
                project(0)
                project(1)
                for c in range(XCH):
                    pe.wait_ge(normed, 2 * u + c + 1)
                    pe.wait_ge(tp_lo, 3 * u + 1)
                    p_transposes(u, c)
                    project(2 + c)
                if nxt:
                    pe.wait_ge(tp_lo, 3 * u + 3)
                    v_transposes(n, 1 - h)
                for c in range(XCH):
                    pe.wait_ge(tp_lo, 3 * u + 2 + c)
                    if c:
                        pe.wait_ge(pv_lo, 2 * u + c)
                    pv_x(u, h, c)
                    project(4 + c)
                if h == 0:
                    pe.wait_ge(wlo, 5 * g + 5)
                for i in range(4):
                    if i % 2 == 0:
                        pe.wait_ge(pv_lo, 2 * u + i // 2 + 1)
                    if nxt and i < 2:
                        pe.wait_ge(pj_act, XT * n + 5 + i)
                    pe.wait_ge(pj_dve, PD_LN1 + 4 * u + i - 1)
                    out_x(u, i)

            with pe.Fori(0, NKV - 1) as g:
                phase(2 * g, 0, g, "loop")
                phase(2 * g + 1, 1, g, "loop")
            phase(NU - 2, 0, NKV - 1, "last")
            phase(NU - 1, 1, NKV - 1, None)

            for n in range(NT, 2 * NT):
                pe.wait_ge(pj_dve, PD_X + (n - NT) - 1)
                ln_tile(n, [xns[i][:, :] for i in range(2)])

            def proj_s(v, tile):
                t, h = v // 2, v % 2
                k = ST * v + tile
                if k < 2:
                    pe.wait_ge(pj_dve, PD_LN2)
                else:
                    pe.wait_ge(pj_act, PA_X + k - 1)
                if h == 0:
                    pe.wait_ge(wlo, W_X + 2 * t + (2 if tile == 1 else 1))
                c = (slice(0, P), slice(256, 384), slice(P, 256))[tile]
                tok = slice(h * HALF, (h + 1) * HALF)
                three(pj[:, k % 2, :], [((wsh[:, t, i, c], wsl[:, t, i, c]), (xh[:, i, tok], xl[:, i, tok]))
                                        for i in range(KT)]).then_inc(proj, 1)

            def v_transposes_s(v):
                pe.wait_ge(pj_act, PA_X + ST * v + 3)
                if v:
                    pe.wait_ge(pt_done, SCH * v - 1)
                for b in range(4):
                    last = pe.transpose(tp[:, 0, b * P:(b + 1) * P], vts[:, b * P:(b + 1) * P], ident)
                last.then_inc(vt_t, 1)

            def scores_s(n):
                v, c = n // SCH, n % SCH
                h = v % 2
                if c == 0:
                    pe.wait_ge(pj_act, PA_X + ST * v + 2)
                for b in range(2):
                    bb = 2 * c + b
                    last = pe.matmul(sc[:, n % 2, b * 256:(b + 1) * 256], qm[h][:, bb, :, :], kb[h][:, bb, :, :],
                                     start=True, stop=True)
                last.then_inc(scored, 1)

            def p_transposes_s(n):
                pe.wait_ge(normed, N_SM + n + 1)
                if n % SCH == 0:
                    pe.wait_ge(vc_done, n // SCH + 1)
                elif n % SCH >= 2:
                    pe.wait_ge(pt_done, n - 1)
                for i in range(4):
                    last = pe.transpose(tp[:, n % 2, i * P:(i + 1) * P], sm[n % 2][:, i * P:(i + 1) * P], ident)
                last.then_inc(pt_t, 1)

            def pv_s(n):
                v, c = n // SCH, n % SCH
                h = v % 2
                pe.wait_ge(pt_done, n + 1)
                if n >= 2:
                    pe.wait_ge(ssel, n - 1)
                for b in range(2):
                    for t in range(2):
                        last = pe.matmul(pv[64 * t:64 * t + 64, n % 2, b * P:(b + 1) * P],
                                         vc[h][:, 2 * c + b, t, :],
                                         pts[n % 2][:, (2 * b + t) * P:(2 * b + t + 1) * P], start=True, stop=True)
                last.then_inc(spv, 1)

            for tile in range(ST):
                proj_s(0, tile)
            v_transposes_s(0)
            scores_s(0)
            scores_s(1)
            for n in range(N_SS):
                v, c = n // SCH, n % SCH
                p_transposes_s(n)
                if v + 1 < NSU and c < 3:
                    proj_s(v + 1, c)
                if n + 2 < N_SS:
                    scores_s(n + 2)
                pv_s(n)
                if v + 1 < NSU and c == 3:
                    v_transposes_s(v + 1)
            pe.wait_ge(wlo, W_X + N_SELF)
            for i in range(NT):
                if i == 0:
                    pe.wait_ge(o_lo, NSU)
                if i < 2:
                    pe.wait_ge(pj_act, PA_X + ST * NSU - 1 + i)
                else:
                    pe.wait_ge(pj_dve, PD_LN2 + i - 1)
                tok = slice(i * P, (i + 1) * P)
                three(pj[:, i % 2, :], [((ah[:, k, tok], al[:, k, tok]), (woh[:, k, :], wol[:, k, :]))
                                        for k in range(KT)]).then_inc(outp, 1)
            for n in range(2 * NT, 3 * NT):
                pe.wait_ge(pj_dve, PD_O + (n - 2 * NT) - 1)
                ln_tile(n, [xnf[i][:, :] for i in range(2)])
            pe.wait_ge(s_row2, 32)
            pe.wait_ge(ln_hi, 3 * NT)
            for i in range(NT):
                if i % 2 == 0 and i >= 4:
                    pe.wait_ge(hg_c, i // 2 - 1)
                o = tp[:, i // 2 % 2, (i % 2) * (P + NG):(i % 2 + 1) * (P + NG)]
                for k in range(KT):
                    last = pe.matmul(o, xf[:, k, i * P:(i + 1) * P], wag[:, k, :], start=(k == 0), stop=(k == KT - 1))
                if i % 2:
                    last.then_inc(hg_t, 1)

            def base(i):
                if i < 6 and i % 2 == 0 and i == 0:
                    pe.wait_ge(pj_dve, PD_LN3)
                if i >= 6:
                    pe.wait_ge(fin, i - 5)
                tok = slice(i * P, (i + 1) * P)
                m = 0
                for k in range(KT):
                    for w, r in ((xh, wbh), (xh, wbl), (xl, wbh)):
                        pe.matmul(fin_bank(i), w[:, k, tok], r[:, k, :], start=(m == 0), stop=False)
                        m += 1

            def moe(i):
                tok = slice(i * P, (i + 1) * P)
                pe.matmul(fin_bank(i), hth[:, tok], weh[:, :], start=False, stop=False)
                pe.matmul(fin_bank(i), hth[:, tok], wel[:, :], start=False, stop=False)
                pe.matmul(fin_bank(i), htl[:, tok], weh[:, :], start=False, stop=True).then_inc(fin_t, 1)

            pe.wait_ge(wlo, W_X + N_SELF + 3)
            for i in range(6):
                base(i)
            pe.wait_ge(hg_c, 4)
            for i in range(NT):
                pe.wait_ge(hw_done, i + 1)
                last = pe.transpose(tp[:, i // 4, (i % 4) * P:(i % 4 + 1) * P], hw[:, i, :], ident)
                if i % 4 == 3:
                    last.then_inc(hw_t, 1)
            for i in range(6):
                if i % 4 == 0:
                    pe.wait_ge(hw_lo, i // 4 + 1)
                moe(i)
            for i in range(6, NT):
                base(i)
                moe(i)


def kernel(x, ctx_4096, L0_xattn_Wq, L0_xattn_Wk, L0_xattn_Wv, L0_xattn_Wd, L0_attn_Wq, L0_attn_bq,
           L0_attn_Wk, L0_attn_bk, L0_attn_Wv, L0_attn_bv, L0_attn_Wo, L0_attn_bo, L0_ffn_W_base,
           L0_ffn_b_base, L0_ffn_W_gate, L0_ffn_W_thr, L0_ffn_b_thr, L0_ffn_A, L0_ffn_B):
    import numpy as np
    import concourse.bacc as bacc
    from concourse.bass_utils import run_bass_kernel_spmd

    def A(a):
        return np.asarray(a)

    consts = np.zeros((P, NCONST), np.float32)
    consts[:, C_ID:C_ID + P] = np.eye(P, dtype=np.float32)
    inv = (np.float32(1.0) / np.float32(10000.0) ** (np.arange(0, DH, 2, dtype=np.float32) / np.float32(DH)))
    ang = (np.arange(S, dtype=np.float32)[None, :] * inv.astype(np.float32)[:, None]).astype(np.float32)
    consts[:, C_COS:C_COS + S] = np.concatenate([np.cos(ang), np.cos(ang)], 0)
    consts[:, C_SIN:C_SIN + S] = np.concatenate([-np.sin(ang), np.sin(ang)], 0)
    row = np.arange(P)[:, None] % S
    consts[:, C_MASK:C_MASK + S] = np.where(np.arange(S)[None, :] <= row, 0.0, NEG)
    consts[:, C_PAR] = np.arange(P) // SD % 2 == 0
    consts[:, C_PAR + 1] = np.arange(P) // SD % 2 == 1

    def rows(w):
        return A(w).T.reshape(-1, P, A(w).shape[0]).transpose(1, 0, 2)

    xin = A(x).reshape(NT, P, D).transpose(1, 0, 2)
    ctxT = A(ctx_4096)[:, :S, :].reshape(TOK, KT, P).transpose(1, 2, 0)
    wq, wk, wv = (rows(w) for w in (L0_xattn_Wq, L0_xattn_Wk, L0_xattn_Wv))
    wd = rows(L0_xattn_Wd)
    w_x = np.empty((NKV, P, 5, PIECE), np.float32)
    for g in range(NKV):
        kv = slice(g * P, (g + 1) * P)
        w_x[g, :, 0] = np.concatenate([wk[:, :, kv], wv[:, :, kv]], 2).reshape(P, -1)
        for i in range(2):
            q = slice((REP * g + 2 * i) * P, (REP * g + 2 * i + 2) * P)
            w_x[g, :, 1 + i] = wq[:, :, q].reshape(P, -1)
            w_x[g, :, 3 + i] = wd[:, REP * g + 2 * i:REP * g + 2 * i + 2].reshape(P, -1)
    sq, sk, sv = (rows(w) for w in (L0_attn_Wq, L0_attn_Wk, L0_attn_Wv))
    w_s = np.empty((KT, P, 1536), np.float32)
    for t in range(KT):
        c = slice(t * P, (t + 1) * P)
        w_s[t, :, :1024] = np.concatenate([sk[:, :, c], sv[:, :, c]], 2).reshape(P, -1)
        w_s[t, :, 1024:] = sq[:, :, c].reshape(P, -1)
    arrays = {
        "x": xin, "ctxT": ctxT, "w_x": w_x, "w_s": w_s,
        "w_o": rows(L0_attn_Wo).reshape(P, -1), "w_b": rows(L0_ffn_W_base).reshape(P, -1),
        "w_ag": np.concatenate([rows(A(L0_ffn_A).reshape(NE * NR, D)), rows(L0_ffn_W_gate), rows(L0_ffn_W_thr)], 2),
        "w_eb": A(L0_ffn_B).transpose(0, 2, 1).reshape(NE * NR, D),
        "consts": consts,
        "bias_cols": np.stack([A(b).reshape(KT, P).T for b in (L0_attn_bq, L0_attn_bk, L0_attn_bv)], 1),
        "bias_rows": np.stack([np.broadcast_to(A(b), (P, D)) for b in (L0_attn_bo, L0_ffn_b_base)]),
        "b_thr": np.broadcast_to(A(L0_ffn_b_thr), (P, 1)),
    }
    nc = bacc.Bacc("TRN2", target_bir_lowering=False, num_devices=1)
    arrays = {f"in_{n}": np.ascontiguousarray(a) for n, a in arrays.items()}
    args = [nc.dram_tensor(n, a.shape, mybir.dt.from_np(a.dtype), kind="ExternalInput").ap()
            for n, a in arrays.items()]
    out = nc.dram_tensor("out", (P, NT, D), F32, kind="ExternalOutput").ap()
    build(nc, *args, out)
    r = run_bass_kernel_spmd(nc, [arrays], core_ids=[0])
    return r.results[0]["out"].reshape(P, NT, D).transpose(1, 0, 2).reshape(B, S, D)
```

```python
from contextlib import ExitStack

import concourse.bass as bass
from concourse import mybir

F32 = mybir.dt.float32
F32R = mybir.dt.float32r
ALU = mybir.AluOpType
ACT = mybir.ActivationFunctionType
AXX = mybir.AxisListType.X

P = 128
B, S, D = 16, 64, 512
KT = D // P
TOK = B * S
NT = TOK // P
HALF = TOK // 2
HB = B // 2
DH = 128
NKV = 8
REP = 4
SH = 32
SD = D // SH
NE, NR = 8, 16
NG = NE + 1
EPS = 1e-5
NEG = -1.0e30
X_SCALE = float(DH) ** -0.5
S_SCALE = float(SD) ** -0.5
MAX_THR = 0.125
SCALING = 2.0

XT = 2 + REP
NU = 2 * NKV
XCH = 2
ST = 3
SCH = 4
NSU = 2 * KT
UNITS = [(0, 0), (1, 0), (0, 1), (1, 1), (2, 0), (2, 1), (3, 0), (3, 1)]
PIECE = 1024
C_ID, C_COS, C_SIN, C_MASK, C_PAR = 0, 128, 192, 256, 320
NCONST = 322


def build(nc, x, ctxT, w_x, w_s, w_o, w_b, w_ag, w_eb, consts, bias_cols, bias_rows, b_thr, out):
    es = ExitStack()
    with es:
        def sem(name):
            return es.enter_context(nc.semaphore(name))

        def sb(stack, name, shape, dt=F32):
            return stack.enter_context(nc.sbuf_tensor(name, shape, dt))

        X = sb(es, "X", [P, NT, D])
        xh = sb(es, "xh", [P, KT, TOK], F32R)
        xl = sb(es, "xl", [P, KT, TOK], F32R)
        ah = sb(es, "ah", [P, KT, TOK], F32R)
        al = sb(es, "al", [P, KT, TOK], F32R)
        raw = [sb(es, f"raw{i}", [P, PIECE]) for i in range(2)]
        sm = [sb(es, f"sm{i}", [P, 512]) for i in range(2)]
        cst = sb(es, "cst", [P, NCONST])
        bcol = sb(es, "bcol", [P, 3, KT])
        bthr = sb(es, "bthr", [P, 1])
        stats = sb(es, "stats", [P, NT, 6])
        mv = sb(es, "mv", [P, NT, 2])
        veps = sb(es, "veps", [P, NT])
        rstd = sb(es, "rstd", [P, NT])
        mhalf = sb(es, "mhalf", [P, NT])
        mx = sb(es, "mx", [P, 4, 8])
        zs = sb(es, "zs", [P, 4, 8])
        rz = sb(es, "rz", [P, 4, 8])
        bqm = sb(es, "bqm", [P, 2, KT])
        xs = ExitStack()
        wqh = sb(xs, "wqh", [P, 3, KT, 256], F32R)
        wql = sb(xs, "wql", [P, 3, KT, 256], F32R)
        wdh = sb(xs, "wdh", [P, REP, D], F32R)
        wdl = sb(xs, "wdl", [P, REP, D], F32R)
        kr = [sb(xs, f"kr{i}", [P, HB, S]) for i in range(2)]
        qr = [sb(xs, f"qr{i}", [P, HB, REP, S]) for i in range(2)]
        vt = sb(xs, "vt", [P, HB, 2, S])
        v2h, v2l = [None, None], [None, None]
        for i in range(2):
            v2h[i] = sb(xs, f"v2h{i}", [P, HB, DH], F32R)
            v2l[i] = sb(xs, f"v2l{i}", [P, HB, DH], F32R)
        ch = sb(xs, "ch", [P, REP, HALF], F32R)
        cl = sb(xs, "cl", [P, REP, HALF], F32R)
        pt = [sb(xs, f"pt{i}", [P, 1024], F32R) for i in range(2)]
        t1 = [sb(xs, f"t1{i}", [P, HALF]) for i in range(2)]
        sw = [sb(xs, f"sw{i}", [P, HALF]) for i in range(2)]
        xs.close()
        rawctx = [qr[i][:, :, :, :].rearrange("p b r s -> p (b r s)").rearrange("p (k t) -> p k t", k=KT)
                  for i in range(2)]

        ss = ExitStack()
        ws = [sb(ss, f"ws{i}", [P, 2, KT, 384], F32R) for i in range(KT)]
        kb, qm, vc = [None, None], [None, None], [None, None]
        kb[0] = sb(ss, "kb0", [P, HB, 4, S])
        qm[0] = sb(ss, "qm0", [P, HB, 2, S])
        vts = sb(ss, "vts", [P, HALF])
        vc[0] = sb(ss, "vc0", [P, HB, 2, 64])
        kb[1] = sb(ss, "kb1", [P, HB, 4, S])
        qm[1] = sb(ss, "qm1", [P, HB, 2, S])
        vc[1] = sb(ss, "vc1", [P, HB, 2, 64])
        brow_o = sb(ss, "brow_o", [P, D])
        ot = [sb(ss, f"ot{i}", [P, HALF]) for i in range(2)]
        osel = [sb(ss, f"osel{i}", [P, 2 * S]) for i in range(2)]
        pts = [sb(ss, f"pts{i}", [P, 512]) for i in range(2)]
        sb(ss, "gap_s", [P, 768])
        sm4 = sm + [sb(ss, f"sm{i}", [P, 512]) for i in (2, 3)]
        ss.close()
        fs = ExitStack()
        woh = sb(fs, "woh", [P, KT, D], F32R)
        wol = sb(fs, "wol", [P, KT, D], F32R)
        brow_b = sb(fs, "brow_b", [P, D])
        sb(fs, "gap_f", [P, 1536])
        wbh = sb(fs, "wbh", [P, KT, D], F32R)
        wbl = sb(fs, "wbl", [P, KT, D], F32R)
        weh = sb(fs, "weh", [P, D], F32R)
        wel = sb(fs, "wel", [P, D], F32R)
        wag = sb(fs, "wag", [P, KT, P + NG])
        sb(fs, "gap_g", [P, 1024 - KT * (P + NG)])
        xf = sb(fs, "xf", [P, KT, TOK])
        hg = sb(fs, "hg", [P, NT, P + NG])
        hw = sb(fs, "hw", [P, NT, P])
        hth = sb(fs, "hth", [P, TOK], F32R)
        htl = sb(fs, "htl", [P, TOK], F32R)
        gm = sb(fs, "gm", [P, NT])
        ge = sb(fs, "ge", [P, NT, NE])
        gz = sb(fs, "gz", [P, NT])
        gr = sb(fs, "gr", [P, NT])
        gt = sb(fs, "gt", [P, NT])
        gw = sb(fs, "gw", [P, NT, NE])
        gs = sb(fs, "gs", [P, NT])
        fs.close()

        def pb(name):
            return es.enter_context(nc.psum_tensor(name, [P, 2, 512], F32))
        pj, sc, tp, pv = pb("pj"), pb("sc"), pb("tp"), pb("pv")

        s_const = sem("s_const")
        s_cols = sem("s_cols")
        s_x = [sem(f"s_x{i}") for i in range(4)]
        s_ctx = [sem(f"s_ctx{i}") for i in range(4)]
        s_w = [sem(f"s_w{i}") for i in range(2)]
        s_row = sem("s_row")
        s_row2 = sem("s_row2")
        ln3_lo = sem("ln3_lo")
        s_out = sem("s_out")
        whi = sem("whi")
        wlo = sem("wlo")
        wd_lo = sem("wd_lo")
        chi = sem("chi")
        clo = sem("clo")
        mh_set = sem("mh_set")
        dve_seq = sem("dve_seq")
        ln_var = sem("ln_var")
        ln_rstd = sem("ln_rstd")
        ln_xn = sem("ln_xn")
        ln_t = sem("ln_t")
        ln_hi = sem("ln_hi")
        pj_dve = sem("pj_dve")
        pj_act = sem("pj_act")
        proj = sem("proj")
        t1_done = sem("t1_done")
        sin_done = sem("sin_done")
        rope = sem("rope")
        tp_t = sem("tp_t")
        tp_hi = sem("tp_hi")
        tp_lo = sem("tp_lo")
        scored = sem("scored")
        masked = sem("masked")
        maxed = sem("maxed")
        subbed = sem("subbed")
        exped = sem("exped")
        summed = sem("summed")
        recd = sem("recd")
        normed = sem("normed")
        pv_t = sem("pv_t")
        pv_hi = sem("pv_hi")
        pv_lo = sem("pv_lo")
        outp = sem("outp")
        zeroed = sem("zeroed")
        bq_done = sem("bq_done")
        k_done, q_done, v_done = sem("k_done"), sem("q_done"), sem("v_done")
        vt_t, vc_done = sem("vt_t"), sem("vc_done")
        pt_t, pt_done = sem("pt_t"), sem("pt_done")
        spv, ssel, ssel1 = sem("spv"), sem("ssel"), sem("ssel1")
        o_hi, o_lo = sem("o_hi"), sem("o_lo")
        xbo = sem("xbo")
        hg_t, hg_c = sem("hg_t"), sem("hg_c")
        gate = sem("gate")
        gexp = sem("gexp")
        hw_done = sem("hw_done")
        hw_t, hw_hi, hw_lo = sem("hw_t"), sem("hw_hi"), sem("hw_lo")
        fin_t, fin = sem("fin_t"), sem("fin")

        ident = cst[:, C_ID:C_ID + P]

        def rep(ap, n):
            return ap.unsqueeze(1).to_broadcast([ap.shape[0], n, S])

        def per_group(ap, n):
            return ap.unsqueeze(2).to_broadcast([P, n, S])

        mask3 = rep(cst[:, C_MASK:C_MASK + S], 8)
        W_X = 5 * NKV
        WL_X = 3 * NKV
        PD_LN1 = NT
        PD_14 = PD_LN1 + 4 * (NU - 1)
        PD_LN2A = PD_14 + 4
        PD_X = PD_LN2A + 4
        PD_LN2 = PD_X + 4
        PA_X = XT * NU
        N_SM = XCH * NU
        N_SS = SCH * NSU

        late = []
        for t in range(KT):
            late.append((w_s[t, :, 0:1024], ws[t][:, 0, :, 0:256], ws[t][:, 1, :, 0:256], 256))
            late.append((w_s[t, :, 1024:1536], ws[t][:, 0, :, 256:384], ws[t][:, 1, :, 256:384], 128))
        for i in range(2):
            late.append((w_o[:, i * 1024:(i + 1) * 1024], woh[:, 2 * i:2 * i + 2, :], wol[:, 2 * i:2 * i + 2, :], D))
        N_SELF = len(late)
        for i in range(2):
            late.append((w_b[:, i * 1024:(i + 1) * 1024], wbh[:, 2 * i:2 * i + 2, :], wbl[:, 2 * i:2 * i + 2, :], D))
        late.append((w_eb, weh[:, :].unsqueeze(1), wel[:, :].unsqueeze(1), D))
        LATE_AT = {4: 1, 5: 2, 6: 4, 7: 5, 8: 14, 9: 16}

        def late_buf(i):
            b = 1 - i % 2
            return b, 16 * ((17 if b == 0 else 23) + i // 2 + 1)

        def late_raw(i):
            width = late[i][3]
            n = late[i][1].shape[1]
            return raw[late_buf(i)[0]][:, 0:n * width].rearrange("p (k c) -> p k c", k=n)

        def ln_bank(n):
            return (pv, pj, tp)[n // NT][:, n % 2, :]

        def ln_tmp(n):
            stage = n // NT
            return (sm, (t1[1], sw[1]), sm)[stage][n % 2][:, :]

        def fin_bank(i):
            return (pj, pv, tp)[i // 2 % 3][:, i % 2, :]

        block = es.enter_context(nc.Block())

        @block.sync
        def _(sp):
            def load_x(i):
                sp.dma_start(X[:, 2 * i:2 * i + 2, :], x[:, 2 * i:2 * i + 2, :]).then_inc(s_x[i], 16)

            def load_ctx(half, i):
                sp.dma_start(rawctx[half][:, 2 * i:2 * i + 2, :],
                             ctxT[:, 2 * i:2 * i + 2, half * HALF:(half + 1) * HALF]).then_inc(s_ctx[2 * half + i], 16)

            sp.dma_start(raw[0][:, :], w_x[0, :, 0, :]).then_inc(s_w[0], 16)
            load_ctx(0, 0)
            load_ctx(0, 1)
            load_x(0)
            sp.dma_start(cst[:, :], consts).then_inc(s_const, 16)
            load_x(1)
            sp.dma_start(raw[1][:, :], w_x[0, :, 1, :]).then_inc(s_w[1], 16)
            sp.wait_ge(wlo, 1)
            sp.dma_start(raw[0][:, :], w_x[0, :, 2, :]).then_inc(s_w[0], 16)
            load_x(2)
            load_x(3)
            load_ctx(1, 0)
            load_ctx(1, 1)
            sp.dma_start(bcol[:, :, :], bias_cols).then_inc(s_cols, 16)
            sp.dma_start(bthr[:, :], b_thr).then_inc(s_cols, 16)

            def stream(g, last):
                srcs = [(g, 3), (g, 4)] + ([] if last else [(g + 1, 0), (g + 1, 1), (g + 1, 2)])
                for i, (gg, j) in enumerate(srcs):
                    src = w_x[gg, :, j, :]
                    b = (1, 0, 1, 0, 1)[i]
                    if i in (2, 3):
                        sp.wait_ge(wd_lo, 2 * g + i - 1)
                    else:
                        sp.wait_ge(wlo, 3 * g + (3 if i < 2 else 4))
                    sp.dma_start(raw[b][:, :], src).then_inc(s_w[b], 16)

            with sp.Fori(0, NKV - 1) as g:
                stream(g, False)
            stream(NKV - 1, True)

            def late_load(i):
                b, _ = late_buf(i)
                if i < 2:
                    sp.wait_ge(wd_lo, 2 * NKV - 1 + i)
                else:
                    sp.wait_ge(wlo, WL_X + i - 1)
                n = late[i][1].shape[1] * late[i][3]
                sp.dma_start(raw[b][:, 0:n], late[i][0]).then_inc(s_w[b], 16)

            for i in range(4):
                late_load(i)
            sp.wait_ge(pj_dve, PD_X)
            sp.dma_start(brow_o[:, :], bias_rows[0]).then_inc(s_row, 16)
            for i in range(4, N_SELF):
                late_load(i)
            sp.wait_ge(proj, PA_X + ST * NSU)
            sp.dma_start(wag[:, :, :], w_ag).then_inc(s_row2, 16)
            sp.dma_start(brow_b[:, :], bias_rows[1]).then_inc(s_row2, 16)
            for i in range(N_SELF, len(late)):
                late_load(i)
            for i in range(NT):
                sp.wait_ge(fin, i + 1)
                sp.dma_start(out[:, i, :], X[:, i, :]).then_inc(s_out, 16)
            sp.wait_ge(s_out, 16 * NT)

        @block.gpsimd
        def _(pool):
            pool.memset(mhalf[:, :], -0.5).then_inc(mh_set, 1)

            def split_out(v):
                t, h = UNITS[v]
                pool.wait_ge(o_hi, v + 1)
                pool.tensor_tensor(al[:, t, h * HALF:(h + 1) * HALF], ot[v % 2][:, :],
                                   ah[:, t, h * HALF:(h + 1) * HALF].bitcast(F32),
                                   ALU.subtract).then_inc(o_lo, 1)

            def split_lo(n, hi, lo, src):
                pool.wait_ge(whi, n + 1)
                pool.tensor_tensor(lo, src, hi.bitcast(F32), ALU.subtract).then_inc(wlo, 1)

            def split_x(n, j, b):
                split_lo(n, wqh[:, j].rearrange("p k c -> p (k c)"), wql[:, j].rearrange("p k c -> p (k c)"),
                         raw[b][:, :])

            def ln_pow(grp):
                pool.wait_ge(ln_var, grp + 1)
                c = slice(4 * (grp % 2), 4 * (grp % 2) + 4)
                pool.tensor_tensor(rstd[:, c], veps[:, c], mhalf[:, c], ALU.pow).then_inc(ln_rstd, 1)

            pool.wait_ge(mh_set, 1)
            split_x(0, 0, 0)
            ln_pow(0)

            def rope_tile(u, h, idx):
                par = (h + idx) % 2
                pj_n = XT * u + (1 if idx == 0 else 2 + idx)
                pool.wait_ge(pj_act, pj_n)
                pool.tensor_tensor(sw[par][:, :].rearrange("p (b s) -> p b s", s=S),
                                   sw[par][:, :].rearrange("p (b s) -> p b s", s=S),
                                   rep(cst[:, C_SIN:C_SIN + S], HB), ALU.mult).then_inc(sin_done, 1)
                pool.wait_ge(sin_done, 5 * u + idx + 1)
                o = kr[h][:, :, :] if idx == 0 else qr[h][:, :, idx - 1, :]
                pool.tensor_tensor(o, t1[par][:, :].rearrange("p (b s) -> p b s", s=S),
                                   sw[par][:, :].rearrange("p (b s) -> p b s", s=S),
                                   ALU.add).then_inc(rope, 1)

            def subtract_max(n, c):
                pool.wait_ge(maxed, n + 1)
                s3 = sm4[c][:, :].rearrange("p (n s) -> p n s", s=S)
                pool.tensor_tensor(s3, s3, per_group(mx[:, c, :], 8), ALU.subtract).then_inc(subbed, 1)

            def normalise(n, c):
                pool.wait_ge(recd, n + 1)
                s3 = sm4[c][:, :].rearrange("p (n s) -> p n s", s=S)
                pool.tensor_tensor(s3, s3, per_group(rz[:, c, :], 8), ALU.mult).then_inc(normed, 1)

            rope_tile(0, 0, 0)
            split_x(1, 1, 1)
            split_x(2, 2, 0)
            ln_pow(1)
            for idx in range(1, 5):
                rope_tile(0, 0, idx)

            def phase(u, h, g, nxt):
                subtract_max(2 * u, 0)
                subtract_max(2 * u + 1, 1)
                normalise(2 * u, 0)
                if nxt:
                    rope_tile(u + 1, 1 - h, 0)
                normalise(2 * u + 1, 1)
                if nxt:
                    rope_tile(u + 1, 1 - h, 1)
                rope_tile(u + 1, 1 - h, 2)
                rope_tile(u + 1, 1 - h, 3)
                if h == 0 and nxt == "loop":
                    split_x(5 * g + 5, 0, 1)
                rope_tile(u + 1, 1 - h, 4)
                if h == 0 and nxt == "loop":
                    split_x(5 * g + 6, 1, 0)
                    split_x(5 * g + 7, 2, 1)

            with pool.Fori(0, NKV - 1) as g:
                phase(2 * g, 0, g, "loop")
                phase(2 * g + 1, 1, g, "loop")
            phase(NU - 2, 0, NKV - 1, "last")

            def late_lo(i):
                split_lo(W_X + i, late[i][1], late[i][2], late_raw(i))

            late_lo(0)
            subtract_max(N_SM - 2, 0)
            late_lo(1)
            subtract_max(N_SM - 1, 1)
            normalise(N_SM - 2, 0)
            ln_pow(2)
            normalise(N_SM - 1, 1)
            pool.wait_ge(scored, N_SM)
            pool.memset(kb[0][:, :, :, :], 0.0).then_inc(zeroed, 1)
            pool.memset(vc[0][:, :, :, :], 0.0).then_inc(zeroed, 1)
            late_lo(2)
            pool.wait_ge(pv_t, N_SM)
            pool.memset(kb[1][:, :, :, :], 0.0).then_inc(zeroed, 1)
            subtract_max(N_SM, 0)
            subtract_max(N_SM + 1, 1)
            late_lo(3)
            normalise(N_SM, 0)
            normalise(N_SM + 1, 1)
            pool.wait_ge(pj_dve, PD_X)
            pool.memset(vc[1][:, :, :, :], 0.0).then_inc(zeroed, 1)
            ln_pow(3)

            for n in range(N_SS):
                v, c = n // SCH, n % SCH
                if c == 1 and v == NSU - 1:
                    split_out(v - 1)
                if n + 2 < N_SS:
                    subtract_max(N_SM + n + 2, (n + 2) % 4)
                if 1 <= n and n + 1 < N_SS:
                    normalise(N_SM + n + 1, (n + 1) % 4)
                for i, at in LATE_AT.items():
                    if at == n:
                        late_lo(i)
                if 6 <= n < 6 + NT:
                    i = n - 6
                    if i == 0:
                        pool.wait_ge(s_row, 16)
                        pool.wait_ge(ln_xn, 2 * NT)
                    pool.tensor_tensor(X[:, i, :], X[:, i, :], brow_o[:, :], ALU.add).then_inc(xbo, 1)
                if c == 1 and 0 < v < NSU - 1:
                    split_out(v - 1)
            for i in range(N_SELF, len(late)):
                late_lo(i)
            split_out(NSU - 1)
            ln_pow(4)
            ln_pow(5)
            pool.wait_ge(s_row2, 32)
            for i in range(NT):
                pool.wait_ge(ln_xn, 2 * NT + i + 1)
                pool.tensor_tensor(X[:, i, :], X[:, i, :], brow_b[:, :], ALU.add).then_inc(xbo, 1)

        @block.scalar
        def _(act):
            def hi(src, dst, s):
                act.activation(dst, src, ACT.Copy).then_inc(s, 1)

            def split_x(j, b, w_n):
                act.wait_ge(s_w[b], 16 * w_n)
                if j < 3:
                    hi(raw[b][:, :], wqh[:, j].rearrange("p k c -> p (k c)"), whi)
                else:
                    hi(raw[b][:, :], wdh[:, 2 * (j - 3):2 * (j - 3) + 2].rearrange("p k c -> p (k c)"), whi)

            def ln_hi_tile(n, also=None):
                i = n % NT
                act.wait_ge(ln_t, n + 1)
                src = ln_bank(n).rearrange("p (k t) -> p k t", k=KT)
                if also is not None:
                    act.activation(also[:, :, i * P:(i + 1) * P], src, ACT.Copy)
                hi(src, xh[:, :, i * P:(i + 1) * P], ln_hi)

            def ctx_hi(half, ks):
                for k in ks:
                    if k % 2 == 0:
                        act.wait_ge(s_ctx[2 * half + k // 2], 16)
                    hi(rawctx[half][:, k, :], ah[:, k, half * HALF:(half + 1) * HALF], chi)

            split_x(0, 0, 1)
            ctx_hi(0, range(KT))

            def swap_halves(u, h, idx, first):
                par = (h + idx) % 2
                act.wait_ge(t1_done, 5 * u + idx + 1)
                if not (first and idx < 2):
                    act.wait_ge(rope, 5 * u + idx - 1)
                bank = (1 + idx) % 2 if idx else 0
                src = pj[:, bank, :]
                act.activation(sw[par][0:64, :], src[64:128, :], ACT.Copy)
                act.activation(sw[par][64:128, :], src[0:64, :], ACT.Copy).then_inc(pj_act, 1)

            def copy_v(u):
                act.wait_ge(proj, XT * u + 2)
                act.activation(vt[:, :, :, :], pj[:, 1, :].rearrange("p (b s) -> p b s", s=S).unsqueeze(2)
                               .to_broadcast([P, HB, 2, S]), ACT.Copy).then_inc(pj_act, 1)

            def v_hi(u, h):
                act.wait_ge(tp_t, 3 * u + 1)
                hi(tp[:, :, :].rearrange("p a c -> p (a c)"), v2h[h][:, :, :].rearrange("p b d -> p (b d)"), tp_hi)

            def p_hi(u, c):
                act.wait_ge(tp_t, 3 * u + 2 + c)
                for hp in range(2):
                    last = act.activation(pt[c][0:64, :].rearrange("p (b r q) -> p b r q", b=4, r=2)[:, :, hp, :],
                                          tp[64 * hp:64 * hp + 64, c, :].rearrange("p (b q) -> p b q", b=4), ACT.Copy)
                last.then_inc(tp_hi, 1)

            def exp(n, c, scale):
                act.wait_ge(subbed, n + 1)
                act.activation(sm4[c][:, :], sm4[c][:, :], ACT.Exp, scale=scale).then_inc(exped, 1)

            def c_hi(u, c):
                act.wait_ge(pv_t, 2 * u + c + 1)
                for r in range(REP):
                    last = act.activation(
                        ch[:, r, c * 256:(c + 1) * 256].rearrange("p (b q) -> p b q", q=S),
                        pv[:, :, :].rearrange("p a (b r q) -> p (a b) r q", b=2, r=REP)[:, :, r, :], ACT.Copy)
                last.then_inc(pv_hi, 1)

            swap_halves(0, 0, 0, True)
            split_x(1, 1, 1)
            ln_hi_tile(0)
            ln_hi_tile(1)
            copy_v(0)
            ln_hi_tile(2)
            ln_hi_tile(3)
            split_x(2, 0, 2)
            swap_halves(0, 0, 1, True)
            swap_halves(0, 0, 2, True)
            ctx_hi(1, (0, 1))
            swap_halves(0, 0, 3, True)
            ln_hi_tile(4)
            ln_hi_tile(5)
            swap_halves(0, 0, 4, True)
            ln_hi_tile(6)
            ln_hi_tile(7)
            ctx_hi(1, (2, 3))
            v_hi(0, 0)

            def phase(u, h, g, nxt):
                exp(2 * u, 0, X_SCALE)
                swap_halves(u + 1, 1 - h, 0, False)
                exp(2 * u + 1, 1, X_SCALE)
                copy_v(u + 1)
                p_hi(u, 0)
                swap_halves(u + 1, 1 - h, 1, False)
                p_hi(u, 1)
                if h == 0:
                    act.wait_ge(pj_dve, PD_LN1 + 8 * g)
                    split_x(3, 1, 2 + 3 * g)
                    split_x(4, 0, 3 + 2 * g)
                swap_halves(u + 1, 1 - h, 2, False)
                c_hi(u, 0)
                swap_halves(u + 1, 1 - h, 3, False)
                if h == 0 and nxt == "loop":
                    split_x(0, 1, 3 + 3 * g)
                v_hi(u + 1, 1 - h)
                swap_halves(u + 1, 1 - h, 4, False)
                c_hi(u, 1)
                if h == 0 and nxt == "loop":
                    split_x(1, 0, 4 + 2 * g)
                    split_x(2, 1, 4 + 3 * g)

            with act.Fori(0, NKV - 1) as g:
                phase(2 * g, 0, g, "loop")
                phase(2 * g + 1, 1, g, "loop")
            phase(NU - 2, 0, NKV - 1, "last")

            def late_hi(i):
                b, n = late_buf(i)
                act.wait_ge(s_w[b], n)
                act.activation(late[i][1], late_raw(i), ACT.Copy).then_inc(whi, 1)

            def k_tile(v):
                t, h = UNITS[v]
                act.wait_ge(proj, PA_X + ST * v + 1)
                src = pj[:, (ST * v) % 2, :].rearrange("p (b s) -> p b s", s=S)
                for j in range(4):
                    r = slice(32 * j, 32 * j + 32)
                    last = act.activation(kb[v % 2][r, :, j, :], src[r], ACT.Identity, bias=bcol[r, 1, t:t + 1])
                last.then_inc(pj_act, 1)

            def q_tile(v):
                t, h = UNITS[v]
                act.wait_ge(proj, PA_X + ST * v + 2)
                src = pj[:, (ST * v + 1) % 2, :].rearrange("p (b s) -> p b s", s=S)
                for par in range(2):
                    last = act.activation(qm[v % 2][:, :, par, :], src, ACT.Identity,
                                          bias=bqm[:, par, t:t + 1], scale=cst[:, C_PAR + par:C_PAR + par + 1])
                last.then_inc(pj_act, 1)

            def v_tile(v):
                t = v // 2
                act.wait_ge(proj, PA_X + ST * v + 3)
                act.activation(vts[:, :], pj[:, (ST * v + 2) % 2, :], ACT.Copy).then_inc(pj_act, 1)

            def pt_copy(n):
                act.wait_ge(pt_t, n + 1)
                act.activation(pts[n % 2][:, :], tp[:, n % 2, :], ACT.Copy).then_inc(pt_done, 1)

            def out_hi(v):
                t, h = UNITS[v]
                act.wait_ge(ssel, SCH * v + SCH)
                hi(ot[v % 2][:, :], ah[:, t, h * HALF:(h + 1) * HALF], o_hi)

            late_hi(0)
            late_hi(1)
            act.wait_ge(s_cols, 32)
            for par in range(2):
                act.activation(bqm[:, par, :], bcol[:, 0, :], ACT.Copy,
                               scale=cst[:, C_PAR + par:C_PAR + par + 1]).then_inc(bq_done, 1)
            u = NU - 1
            exp(2 * u, 0, X_SCALE)
            exp(2 * u + 1, 1, X_SCALE)
            p_hi(u, 0)
            ln_hi_tile(NT)
            ln_hi_tile(NT + 1)
            p_hi(u, 1)
            ln_hi_tile(NT + 2)
            ln_hi_tile(NT + 3)
            late_hi(2)
            c_hi(u, 0)
            act.wait_ge(zeroed, 1)
            act.wait_ge(bq_done, 2)
            k_tile(0)
            c_hi(u, 1)
            q_tile(0)
            v_tile(0)
            late_hi(3)
            exp(N_SM, 0, S_SCALE)
            exp(N_SM + 1, 1, S_SCALE)
            act.wait_ge(zeroed, 3)
            k_tile(1)
            q_tile(1)
            v_tile(1)
            ln_hi_tile(NT + 4)
            for n in range(N_SS):
                v, c = n // SCH, n % SCH
                if n == 0:
                    ln_hi_tile(NT + 5)
                pt_copy(n)
                if n + 2 < N_SS:
                    exp(N_SM + n + 2, (n + 2) % 4, S_SCALE)
                if n == 0:
                    ln_hi_tile(NT + 6)
                    ln_hi_tile(NT + 7)
                elif c == 1 and 0 < v < NSU - 1:
                    v_tile(v + 1)
                elif c >= 2 and v + 2 < NSU:
                    (k_tile if c == 2 else q_tile)(v + 2)
                for i, at in LATE_AT.items():
                    if at == n:
                        late_hi(i)
                if c == 1 and v and v < NSU - 1 or c == 0 and v == NSU - 1:
                    out_hi(v - 1)
                if n >= N_SS - 3:
                    late_hi(N_SELF + n - N_SS + 3)
            out_hi(NSU - 1)
            for n in range(2 * NT, 3 * NT):
                ln_hi_tile(n, xf)
            act.wait_ge(gate, 3)
            act.activation(ge[:, :, :], ge[:, :, :], ACT.Exp)
            act.activation(gt[:, :], gt[:, :], ACT.Exp, scale=-1.0).then_inc(gexp, 1)
            for i in range(2):
                act.wait_ge(hw_t, i + 1)
                hi(sc[:, i, :], hth[:, i * 512:(i + 1) * 512], hw_hi)

        @block.vector
        def _(dve):
            seq = [0]

            def link(ins):
                seq[0] += 1
                ins.then_inc(dve_seq, 1)
                dve.wait_ge(dve_seq, seq[0])

            def ln_stats(i):
                dve.bn_stats(stats[:, i, :], X[:, i, :]).then_inc(dve_seq, 1)
                seq[0] += 1
                dve.wait_ge(dve_seq, seq[0])
                dve.bn_aggr(mv[:, i, :], stats[:, i, :]).then_inc(dve_seq, 1)
                seq[0] += 1

            def ln_eps(grp):
                dve.wait_ge(dve_seq, seq[0])
                c = slice(4 * grp, 4 * grp + 4)
                dve.tensor_scalar(veps[:, c], mv[:, c, 1], EPS, None, ALU.add).then_inc(ln_var, 1)

            def ln_apply(n):
                i = n % NT
                if i % 4 == 0:
                    dve.wait_ge(ln_rstd, n // 4 + 1)
                if i >= 2:
                    dve.wait_ge(ln_t, n - 1)
                dve.tensor_scalar(ln_tmp(n), X[:, i, :], mv[:, i, 0:1], rstd[:, i:i + 1],
                                  ALU.subtract, ALU.mult).then_inc(ln_xn, 1)

            def ln_lo(n):
                i = n % NT
                dve.wait_ge(ln_hi, n + 1)
                dve.tensor_tensor(xl[:, :, i * P:(i + 1) * P], ln_bank(n).rearrange("p (k t) -> p k t", k=KT),
                                  xh[:, :, i * P:(i + 1) * P].bitcast(F32),
                                  ALU.subtract).then_inc(pj_dve if n < 2 * NT else ln3_lo, 1)

            def ln_half(first):
                ln_apply(first)
                for n in range(first + 1, first + 4):
                    ln_apply(n)
                    ln_lo(n - 1)
                ln_lo(first + 3)

            def rope_cos(u, h, idx, first):
                par = (h + idx) % 2
                tile = 0 if idx == 0 else 1 + idx
                dve.wait_ge(proj, XT * u + tile + 1)
                if not (first and idx < 2):
                    dve.wait_ge(rope, 5 * u + idx - 1)
                bank = tile % 2
                dve.tensor_tensor(t1[par][:, :].rearrange("p (b s) -> p b s", s=S),
                                  pj[:, bank, :].rearrange("p (b s) -> p b s", s=S),
                                  rep(cst[:, C_COS:C_COS + S], HB), ALU.mult).then_inc(t1_done, 1)

            def mask_max(n, c):
                s3 = sm4[c][:, :].rearrange("p (n s) -> p n s", s=S)
                dve.wait_ge(scored, n + 1)
                dve.tensor_tensor(s3, sc[:, c % 2, :].rearrange("p (n s) -> p n s", s=S), mask3,
                                  ALU.add).then_inc(masked, 1)
                dve.wait_ge(masked, n + 1)
                dve.tensor_reduce(mx[:, c, :], s3, AXX, ALU.max).then_inc(maxed, 1)

            def sum_rec(n, c):
                dve.wait_ge(exped, n + 1)
                dve.tensor_reduce(zs[:, c, :], sm4[c][:, :].rearrange("p (n s) -> p n s", s=S), AXX,
                                  ALU.add).then_inc(summed, 1)
                dve.wait_ge(summed, n + 1)
                dve.reciprocal(rz[:, c, :], zs[:, c, :]).then_inc(recd, 1)

            def v_lo(u, h):
                dve.wait_ge(tp_hi, 3 * u + 1)
                dve.tensor_tensor(v2l[h][:, :, :].rearrange("p b d -> p (b d)"),
                                  tp[:, :, :].rearrange("p a c -> p (a c)"),
                                  v2h[h][:, :, :].rearrange("p b d -> p (b d)").bitcast(F32),
                                  ALU.subtract).then_inc(tp_lo, 1)

            def p_lo(u, c):
                dve.wait_ge(tp_hi, 3 * u + 2 + c)
                for hp in range(2):
                    p4 = pt[c][:, :].rearrange("p (b r q) -> p b r q", b=4, r=2)[:, :, hp, :]
                    last = dve.tensor_tensor(p4[64:128], tp[64 * hp:64 * hp + 64, c, :].rearrange("p (b q) -> p b q", b=4),
                                             p4[0:64].bitcast(F32), ALU.subtract)
                last.then_inc(tp_lo, 1)

            def c_lo(u, c):
                dve.wait_ge(pv_hi, 2 * u + c + 1)
                for r in range(REP):
                    cs = slice(c * 256, (c + 1) * 256)
                    last = dve.tensor_tensor(
                        cl[:, r, cs].rearrange("p (b q) -> p b q", q=S),
                        pv[:, :, :].rearrange("p a (b r q) -> p (a b) r q", b=2, r=REP)[:, :, r, :],
                        ch[:, r, cs].bitcast(F32).rearrange("p (b q) -> p b q", q=S), ALU.subtract)
                last.then_inc(pv_lo, 1)

            def wd_split(g, i):
                dve.wait_ge(whi, 5 * g + 4 + i)
                c = slice(2 * i, 2 * i + 2)
                dve.tensor_tensor(wdl[:, c].rearrange("p k c -> p (k c)"), raw[1 - i][:, :],
                                  wdh[:, c].rearrange("p k c -> p (k c)").bitcast(F32), ALU.subtract).then_inc(wd_lo, 1)

            def out_add(u, h, i):
                dve.wait_ge(outp, 4 * u + i + 1)
                dve.tensor_tensor(X[:, 4 * h + i, :], X[:, 4 * h + i, :], pj[:, i % 2, :],
                                  ALU.add).then_inc(pj_dve, 1)

            def stats_half(half):
                for i in range(4 * half, 4 * half + 4):
                    if i % 2 == 0:
                        dve.wait_ge(s_x[i // 2], 16)
                    ln_stats(i)
                ln_eps(half)

            def ctx_lo(half, ks):
                for k in ks:
                    c = slice(half * HALF, (half + 1) * HALF)
                    dve.wait_ge(chi, KT * half + k + 1)
                    dve.tensor_tensor(al[:, k, c], rawctx[half][:, k, :], ah[:, k, c].bitcast(F32),
                                      ALU.subtract).then_inc(clo, 1)

            ctx_lo(0, range(KT))
            stats_half(0)
            dve.wait_ge(s_const, 16)
            rope_cos(0, 0, 0, True)
            ln_apply(0)
            ln_apply(1)
            ln_lo(0)
            ln_apply(2)
            ln_lo(1)
            ln_apply(3)
            ln_lo(2)
            ln_lo(3)
            stats_half(1)
            rope_cos(0, 0, 1, True)
            rope_cos(0, 0, 2, True)
            ln_apply(4)
            ln_apply(5)
            ctx_lo(1, (0, 1))
            rope_cos(0, 0, 3, True)
            ln_lo(4)
            ln_apply(6)
            ln_lo(5)
            ln_apply(7)
            rope_cos(0, 0, 4, True)
            ln_lo(6)
            ln_lo(7)
            ctx_lo(1, (2, 3))
            v_lo(0, 0)

            def phase(u, h, g, nxt):
                mask_max(2 * u, 0)
                mask_max(2 * u + 1, 1)
                sum_rec(2 * u, 0)
                rope_cos(u + 1, 1 - h, 0, False)
                sum_rec(2 * u + 1, 1)
                p_lo(u, 0)
                rope_cos(u + 1, 1 - h, 1, False)
                p_lo(u, 1)
                rope_cos(u + 1, 1 - h, 2, False)
                if h == 0:
                    wd_split(g, 0)
                    wd_split(g, 1)
                c_lo(u, 0)
                rope_cos(u + 1, 1 - h, 3, False)
                rope_cos(u + 1, 1 - h, 4, False)
                v_lo(u + 1, 1 - h)
                if nxt == "loop":
                    out_add(u, h, 0)
                    c_lo(u, 1)
                    for i in range(1, 4):
                        out_add(u, h, i)
                else:
                    c_lo(u, 1)
                    for i in range(4):
                        if i >= 2:
                            mask_max(2 * u + i, i - 2)
                        if i == 3:
                            sum_rec(2 * u + 2, 0)
                        out_add(u, h, i)
                        dve.wait_ge(pj_dve, PD_LN1 + 4 * u + i + 1)
                        ln_stats(i)
                    ln_eps(0)

            with dve.Fori(0, NKV - 1) as g:
                phase(2 * g, 0, g, "loop")
                phase(2 * g + 1, 1, g, "loop")
            phase(NU - 2, 0, NKV - 1, "last")

            def vc_copy(v):
                h = v % 2
                dve.wait_ge(vt_t, v + 1)
                src = tp[:, 0, :].rearrange("p (b t j d) -> p b t j d", b=4, t=2, j=2)
                dst = vc[h][:, :, :, :].rearrange("p (b o) t c -> p b o t c", o=2)
                for j in range(2):
                    for odd in range(2):
                        last = dve.tensor_copy(dst[64 * j:64 * j + 64, :, odd, :, 32 * j:32 * j + 32],
                                               src[64 * odd:64 * odd + 64, :, :, j, :])
                last.then_inc(vc_done, 1)

            def select_out(n):
                v, c = n // SCH, n % SCH
                t, h = UNITS[v]
                src = pv[:, n % 2, 0:256].rearrange("p (b r q) -> p b r q", b=2, r=2)
                dve.wait_ge(spv, n + 1)
                if n >= 2:
                    dve.wait_ge(ssel, n - 1)
                o3 = osel[n % 2][:, :].rearrange("p (b q) -> p b q", q=S)
                dve.tensor_scalar(o3, src[:, :, 0, :], cst[:, C_PAR:C_PAR + 1], bcol[:, 2, t:t + 1],
                                  ALU.mult, ALU.add).then_inc(ssel1, 1)
                dve.wait_ge(ssel1, n + 1)
                if c == 0 and v >= 2:
                    dve.wait_ge(o_lo, v - 1)
                dve.scalar_tensor_tensor(ot[v % 2][:, c * P:(c + 1) * P].rearrange("p (b q) -> p b q", q=S),
                                         src[:, :, 1, :], cst[:, C_PAR + 1:C_PAR + 2], o3,
                                         ALU.mult, ALU.add).then_inc(ssel, 1)

            u = NU - 1
            sum_rec(2 * u + 1, 1)
            ln_apply(NT)
            ln_apply(NT + 1)
            p_lo(u, 0)
            ln_lo(NT)
            ln_apply(NT + 2)
            ln_lo(NT + 1)
            ln_apply(NT + 3)
            ln_lo(NT + 2)
            ln_lo(NT + 3)
            p_lo(u, 1)
            c_lo(u, 0)
            c_lo(u, 1)
            mask_max(N_SM, 0)
            mask_max(N_SM + 1, 1)
            dve.wait_ge(zeroed, 2)
            vc_copy(0)
            for i in range(4):
                dve.wait_ge(outp, 4 * u + i + 1)
                dve.tensor_tensor(X[:, 4 + i, :], X[:, 4 + i, :], pj[:, i % 2, :], ALU.add).then_inc(pj_dve, 1)
                dve.wait_ge(pj_dve, PD_LN2A + i + 1)
                ln_stats(4 + i)
                if i < 2:
                    sum_rec(N_SM + i, i)
            ln_eps(1)
            mask_max(N_SM + 2, 2)
            ln_apply(NT + 4)
            ln_apply(NT + 5)
            def out_add_s(i):
                dve.wait_ge(outp, 4 * NU + i + 1)
                dve.wait_ge(xbo, i + 1)
                dve.tensor_tensor(X[:, i, :], X[:, i, :], pj[:, i % 2, :], ALU.add).then_inc(pj_dve, 1)
                dve.wait_ge(pj_dve, PD_LN2 + i + 1)
                ln_stats(i)

            for n in range(N_SS):
                v, c = n // SCH, n % SCH
                if 1 <= n and n + 1 < N_SS:
                    sum_rec(N_SM + n + 1, (n + 1) % 4)
                if n == 0:
                    ln_lo(NT + 4)
                    ln_apply(NT + 6)
                    ln_lo(NT + 5)
                    ln_apply(NT + 7)
                    ln_lo(NT + 6)
                    ln_lo(NT + 7)
                else:
                    select_out(n - 1)
                if c == 3 and v + 1 < NSU:
                    if v == 0:
                        dve.wait_ge(zeroed, 4)
                    vc_copy(v + 1)
                if n + 3 < N_SS:
                    mask_max(N_SM + n + 3, (n + 3) % 4)
                if v == NSU - 1 and c >= 2:
                    out_add_s(c - 2)
            select_out(N_SS - 1)

            out_add_s(2)
            out_add_s(3)
            ln_eps(0)
            ln_apply(2 * NT)
            ln_apply(2 * NT + 1)
            out_add_s(4)
            ln_lo(2 * NT)
            ln_apply(2 * NT + 2)
            ln_lo(2 * NT + 1)
            ln_apply(2 * NT + 3)
            out_add_s(5)
            ln_lo(2 * NT + 2)
            out_add_s(6)
            out_add_s(7)
            ln_eps(1)
            ln_lo(2 * NT + 3)
            def hg_copy(i):
                dve.wait_ge(hg_t, i + 1)
                dve.tensor_copy(hg[:, 2 * i:2 * i + 2, :],
                                sc[:, i % 2, 0:2 * (P + NG)].rearrange("p (a c) -> p a c", a=2)).then_inc(hg_c, 1)

            hg_copy(0)
            hg_copy(1)
            ln_half(2 * NT + 4)
            hg_copy(2)
            hg_copy(3)
            dve.wait_ge(hg_c, 4)
            logits = hg[:, :, P:P + NE]

            def per_e(ap):
                return ap.unsqueeze(2).to_broadcast([P, NT, NE])

            dve.tensor_reduce(gm[:, :], logits, AXX, ALU.max).then_inc(gate, 1)
            dve.wait_ge(gate, 1)
            dve.tensor_tensor(ge[:, :, :], logits, per_e(gm[:, :]), ALU.subtract).then_inc(gate, 1)
            dve.wait_ge(s_cols, 32)
            dve.tensor_scalar(gt[:, :], hg[:, :, P + NE], bthr[:, 0:1], None, ALU.add).then_inc(gate, 1)
            dve.wait_ge(gexp, 1)
            link(dve.tensor_reduce(gz[:, :], ge[:, :, :], AXX, ALU.add))
            link(dve.reciprocal(gr[:, :], gz[:, :]))
            link(dve.tensor_tensor(ge[:, :, :], ge[:, :, :], per_e(gr[:, :]), ALU.mult))
            link(dve.tensor_scalar(gt[:, :], gt[:, :], 1.0, None, ALU.add))
            link(dve.reciprocal(gt[:, :], gt[:, :]))
            link(dve.tensor_scalar(gt[:, :], gt[:, :], MAX_THR, None, ALU.mult))
            link(dve.tensor_tensor(gw[:, :, :], ge[:, :, :], per_e(gt[:, :]), ALU.subtract))
            link(dve.tensor_scalar(gw[:, :, :], gw[:, :, :], 0.0, None, ALU.max))
            link(dve.tensor_reduce(gs[:, :], gw[:, :, :], AXX, ALU.add))
            link(dve.tensor_scalar(gm[:, :], gs[:, :], 0.0, None, ALU.is_equal))
            link(dve.tensor_tensor(gs[:, :], gs[:, :], gm[:, :], ALU.add))
            link(dve.reciprocal(gs[:, :], gs[:, :]))
            link(dve.tensor_scalar(gs[:, :], gs[:, :], SCALING, None, ALU.mult))
            link(dve.tensor_tensor(gw[:, :, :], gw[:, :, :], per_e(gs[:, :]), ALU.mult))
            for i in range(NT):
                dve.tensor_tensor(hw[:, i, :].rearrange("p (e r) -> p e r", r=NR),
                                  hg[:, i, 0:P].rearrange("p (e r) -> p e r", r=NR),
                                  gw[:, i, :].unsqueeze(2).to_broadcast([P, NE, NR]),
                                  ALU.mult).then_inc(hw_done, 1)
            for i in range(2):
                dve.wait_ge(hw_hi, i + 1)
                dve.tensor_tensor(htl[:, i * 512:(i + 1) * 512], sc[:, i, :],
                                  hth[:, i * 512:(i + 1) * 512].bitcast(F32), ALU.subtract).then_inc(hw_lo, 1)
            for i in range(NT):
                dve.wait_ge(fin_t, i + 1)
                dve.wait_ge(xbo, NT + i + 1)
                dve.tensor_tensor(X[:, i, :], X[:, i, :], fin_bank(i), ALU.add).then_inc(fin, 1)

        @block.tensor
        def _(pe):
            def three(o, pairs):
                n = 3 * len(pairs)
                m = 0
                for (wh, wl), (mh, ml) in pairs:
                    for w, r in ((wh, mh), (wh, ml), (wl, mh)):
                        last = pe.matmul(o, w, r, start=(m == 0), stop=(m == n - 1))
                        m += 1
                return last

            def ln_tile(n):
                pe.wait_ge(ln_xn, n + 1)
                for k in range(KT):
                    last = pe.transpose(ln_bank(n)[:, k * P:(k + 1) * P], ln_tmp(n)[:, k * P:(k + 1) * P], ident)
                last.then_inc(ln_t, 1)

            def proj_x(u, h, tile):
                piece, col = (0, tile) if tile < 2 else (1 + (tile - 2) // 2, tile % 2)
                tok = slice(h * HALF, (h + 1) * HALF)
                a, b = (ah, al) if tile < 2 else (xh, xl)
                c = slice(col * P, (col + 1) * P)
                three(pj[:, tile % 2, :],
                      [((wqh[:, piece, k, c], wql[:, piece, k, c]), (a[:, k, tok], b[:, k, tok]))
                       for k in range(KT)]).then_inc(proj, 1)

            def v_transposes(u, h):
                pe.wait_ge(pj_act, XT * u + 2)
                for b in range(HB):
                    last = pe.transpose(tp[:, b // 4, (b % 4) * P:(b % 4 + 1) * P],
                                        vt[:, b, :, :], ident)
                last.then_inc(tp_t, 1)

            def scores_x(u, h, c):
                for b in range(4):
                    bb = 4 * c + b
                    for hp in range(2):
                        last = pe.matmul(sc[:, c, (2 * b + hp) * S:(2 * b + hp + 1) * S],
                                         qr[h][:, bb, 2 * hp:2 * hp + 2, :], kr[h][:, bb, :],
                                         start=True, stop=True)
                last.then_inc(scored, 1)

            def p_transposes(u, c):
                for b in range(4):
                    last = pe.transpose(tp[:, c, b * P:(b + 1) * P], sm[c][:, b * P:(b + 1) * P], ident)
                last.then_inc(tp_t, 1)

            def pv_x(u, h, c):
                for b in range(4):
                    o = pv[:, b // 2, (b % 2) * 256:(b % 2 + 1) * 256]
                    p = pt[c][:, b * 256:(b + 1) * 256]
                    pe.matmul(o, v2h[h][:, 4 * c + b, :], p, start=True, stop=False)
                    last = pe.matmul(o, v2l[h][:, 4 * c + b, :], p, start=False, stop=True)
                last.then_inc(pv_t, 1)

            def out_x(u, i):
                tok = slice(i * P, (i + 1) * P)
                three(pj[:, i % 2, :], [((ch[:, r, tok], cl[:, r, tok]), (wdh[:, r, :], wdl[:, r, :]))
                                        for r in range(REP)]).then_inc(outp, 1)

            def ln1(n):
                if n >= 2:
                    pe.wait_ge(pj_dve, n - 1)
                ln_tile(n)

            pe.wait_ge(wlo, 1)
            pe.wait_ge(clo, KT)
            proj_x(0, 0, 0)
            proj_x(0, 0, 1)
            pe.wait_ge(s_const, 16)
            for n in range(4):
                ln1(n)
            for tile in range(2, XT):
                if tile == 2:
                    pe.wait_ge(pj_dve, 4)
                if tile in (2, 4):
                    pe.wait_ge(wlo, 1 + tile // 2)
                pe.wait_ge(pj_act, tile - 1)
                proj_x(0, 0, tile)
                if tile >= 4:
                    ln1(2 * tile - 4)
                    ln1(2 * tile - 3)
            v_transposes(0, 0)

            def phase(u, h, g, nxt):
                n = u + 1

                def project(tile):
                    if tile < 2:
                        pe.wait_ge(pj_act, XT * u + 5 + tile)
                        pe.wait_ge(pj_dve, PD_LN1 + 4 * u - 1 + tile)
                    else:
                        pe.wait_ge(pj_act, XT * n + tile - 1)
                    if h == 0 and tile == 0:
                        pe.wait_ge(clo, 2 * KT)
                    if h == 1 and tile in (0, 2, 4):
                        pe.wait_ge(wlo, 3 * (g + 1) + 1 + tile // 2)
                    proj_x(n, 1 - h, tile)

                pe.wait_ge(rope, 5 * u + 5)
                scores_x(u, h, 0)
                scores_x(u, h, 1)
                project(0)
                project(1)
                for c in range(XCH):
                    pe.wait_ge(normed, 2 * u + c + 1)
                    pe.wait_ge(tp_lo, 3 * u + 1)
                    p_transposes(u, c)
                    project(2 + c)
                pe.wait_ge(tp_lo, 3 * u + 2)
                pv_x(u, h, 0)
                project(4)
                pe.wait_ge(tp_lo, 3 * u + 3)
                v_transposes(n, 1 - h)
                project(5)
                pe.wait_ge(pv_lo, 2 * u + 1)
                pv_x(u, h, 1)
                if h == 0:
                    pe.wait_ge(wd_lo, 2 * g + 2)
                for i in range(4):
                    if i % 2 == 0:
                        pe.wait_ge(pv_lo, 2 * u + i // 2 + 1)
                    if i < 2:
                        pe.wait_ge(pj_act, XT * n + 5 + i)
                    pe.wait_ge(pj_dve, PD_LN1 + 4 * u + i - 1)
                    out_x(u, i)
                    if nxt == "last" and i in (1, 2):
                        if i == 1:
                            pe.wait_ge(rope, 5 * n + 5)
                        scores_x(n, 1, i - 1)

            with pe.Fori(0, NKV - 1) as g:
                phase(2 * g, 0, g, "loop")
                phase(2 * g + 1, 1, g, "loop")
            phase(NU - 2, 0, NKV - 1, "last")

            def proj_s(v, tile, first=0, end=3 * KT):
                t, h = UNITS[v]
                k = ST * v + tile
                c = (slice(0, P), slice(256, 384), slice(P, 256))[tile]
                tok = slice(h * HALF, (h + 1) * HALF)
                if first == 0:
                    proj_s_free(k, t, h, tile)
                for m in range(first, end):
                    i, part = m // 3, m % 3
                    last = pe.matmul(pj[:, k % 2, :], ws[t][:, part // 2, i, c], (xl if part == 1 else xh)[:, i, tok],
                                     start=(m == 0), stop=(m == 3 * KT - 1))
                if end == 3 * KT:
                    last.then_inc(proj, 1)

            def proj_s_free(k, t, h, tile):
                if k == 0:
                    pe.wait_ge(pj_dve, PD_LN2A)
                elif k == ST:
                    pe.wait_ge(pj_dve, PD_X)
                elif k == 2 * ST:
                    pe.wait_ge(pj_dve, PD_LN2)
                if k >= 2:
                    pe.wait_ge(pj_act, PA_X + k - 1)
                if h == 0:
                    pe.wait_ge(wlo, WL_X + 2 * t + (2 if tile == 1 else 1))

            def proj_s_share(v, c):
                tiles = ([(v + 1, 2)] if 0 < v < NSU - 1 else []) + ([(v + 2, 0), (v + 2, 1)] if v + 2 < NSU else [])
                cuts = {3: (0, 9, 18, 27, 36), 2: (0, 0, 8, 16, 24), 1: (0, 6, 12, 12, 12), 0: (0,) * 5}[len(tiles)]
                for i, (n, tile) in enumerate(tiles):
                    first, end = (min(max(cuts[c + j] - 3 * KT * i, 0), 3 * KT) for j in range(2))
                    if first < end:
                        proj_s(n, tile, first, end)

            def v_transposes_s(v):
                pe.wait_ge(pj_act, PA_X + ST * v + 3)
                if v:
                    pe.wait_ge(pt_done, SCH * (v - 1) + 3)
                for b in range(4):
                    last = pe.transpose(tp[:, 0, b * P:(b + 1) * P], vts[:, b * P:(b + 1) * P], ident)
                last.then_inc(vt_t, 1)

            def scores_s(n):
                v, c = n // SCH, n % SCH
                h = v % 2
                if c == 0:
                    pe.wait_ge(pj_act, PA_X + ST * v + 2)
                if n >= 2:
                    pe.wait_ge(masked, N_SM + n - 1)
                for b in range(2):
                    bb = 2 * c + b
                    last = pe.matmul(sc[:, n % 2, b * 256:(b + 1) * 256], qm[h][:, bb, :, :], kb[h][:, bb, :, :],
                                     start=True, stop=True)
                last.then_inc(scored, 1)

            def p_transposes_s(n):
                pe.wait_ge(normed, N_SM + n + 1)
                if n == 0:
                    pe.wait_ge(vc_done, 1)
                elif n % SCH == 0:
                    pe.wait_ge(vc_done, n // SCH + 1)
                if n >= 2:
                    pe.wait_ge(pt_done, n - 1)
                for i in range(4):
                    last = pe.transpose(tp[:, n % 2, i * P:(i + 1) * P], sm4[n % 4][:, i * P:(i + 1) * P], ident)
                last.then_inc(pt_t, 1)

            def pv_s(n):
                v, c = n // SCH, n % SCH
                h = v % 2
                pe.wait_ge(pt_done, n + 1)
                if n >= 2:
                    pe.wait_ge(ssel, n - 1)
                for b in range(2):
                    for t in range(2):
                        last = pe.matmul(pv[64 * t:64 * t + 64, n % 2, b * P:(b + 1) * P],
                                         vc[h][:, 2 * c + b, t, :],
                                         pts[n % 2][:, (2 * b + t) * P:(2 * b + t + 1) * P], start=True, stop=True)
                last.then_inc(spv, 1)

            u = NU - 1

            def ln2(i):
                if i < 2:
                    pe.wait_ge(pj_act, PA_X - 1 + i)
                if i < 4:
                    pe.wait_ge(pj_dve, PD_14 - 1 + i)
                elif i < 6:
                    pe.wait_ge(pj_act, PA_X + ST + i - 2)
                else:
                    pe.wait_ge(pj_dve, PD_X - 5 + i)
                ln_tile(NT + i)

            def p_x(c):
                pe.wait_ge(normed, 2 * u + c + 1)
                p_transposes(u, c)

            pe.wait_ge(tp_lo, 3 * u + 1)
            p_x(0)
            p_x(1)
            for i in range(4):
                ln2(i)
            pe.wait_ge(tp_lo, 3 * u + 2)
            pv_x(u, 1, 0)
            proj_s(0, 0)
            pe.wait_ge(tp_lo, 3 * u + 3)
            pe.wait_ge(pv_lo, 2 * u + 1)
            pv_x(u, 1, 1)
            proj_s(0, 1)
            proj_s(0, 2)
            scores_s(0)
            scores_s(1)
            v_transposes_s(0)
            pe.wait_ge(pj_act, PA_X + ST)
            for i in range(4):
                if i % 2 == 0:
                    pe.wait_ge(pv_lo, 2 * u + i // 2 + 1)
                if i >= 2:
                    pe.wait_ge(pj_dve, PD_LN2A + i - 1)
                if i == 2:
                    scores_s(2)
                out_x(u, i)
            for tile in range(ST):
                proj_s(1, tile)
            ln2(4)
            def out_s(i):
                if i == 0:
                    pe.wait_ge(wlo, WL_X + N_SELF)
                    pe.wait_ge(o_lo, NSU - 1)
                if i == 4:
                    pe.wait_ge(o_lo, NSU)
                if i < 2:
                    pe.wait_ge(pj_act, PA_X + ST * NSU - 1 + i)
                else:
                    pe.wait_ge(pj_dve, PD_LN2 + i - 1)
                tok = slice(i * P, (i + 1) * P)
                three(pj[:, i % 2, :], [((ah[:, k, tok], al[:, k, tok]), (woh[:, k, :], wol[:, k, :]))
                                        for k in range(KT)]).then_inc(outp, 1)

            for n in range(N_SS):
                v, c = n // SCH, n % SCH
                p_transposes_s(n)
                proj_s_share(v, c)
                if n == 0:
                    ln2(5)
                if n + 3 < N_SS:
                    scores_s(n + 3)
                if n == 0:
                    ln2(6)
                if v == NSU - 1 and c:
                    out_s(c - 1)
                pv_s(n)
                if n == 0:
                    ln2(7)
                if c == 2 and v + 1 < NSU:
                    v_transposes_s(v + 1)

            def ln3(i):
                if i >= 2:
                    pe.wait_ge(ln3_lo, i - 1)
                ln_tile(2 * NT + i)

            def hidden(i):
                if i == 0:
                    pe.wait_ge(s_row2, 32)
                    pe.wait_ge(masked, N_SM + N_SS)
                pe.wait_ge(ln_hi, 2 * NT + i + 1)
                if i % 2 == 0 and i >= 4:
                    pe.wait_ge(hg_c, i // 2 - 1)
                o = sc[:, i // 2 % 2, (i % 2) * (P + NG):(i % 2 + 1) * (P + NG)]
                for k in range(KT):
                    last = pe.matmul(o, xf[:, k, i * P:(i + 1) * P], wag[:, k, :], start=(k == 0), stop=(k == KT - 1))
                if i % 2:
                    last.then_inc(hg_t, 1)

            def base(i):
                pe.wait_ge(wlo, WL_X + len(late))
                if i < 2:
                    pe.wait_ge(pj_dve, PD_LN2 + 7 + i)
                elif i < 4:
                    pe.wait_ge(ssel, N_SS)
                elif i < 6:
                    pe.wait_ge(ln3_lo, NT)
                else:
                    pe.wait_ge(fin, i - 5)
                pe.wait_ge(ln3_lo, i + 1)
                tok = slice(i * P, (i + 1) * P)
                m = 0
                for k in range(KT):
                    for w, r in ((xh, wbh), (xh, wbl), (xl, wbh)):
                        pe.matmul(fin_bank(i), w[:, k, tok], r[:, k, :], start=(m == 0), stop=False)
                        m += 1

            def moe(i):
                tok = slice(i * P, (i + 1) * P)
                if i % 4 == 0:
                    pe.wait_ge(hw_lo, i // 4 + 1)
                pe.matmul(fin_bank(i), hth[:, tok], weh[:, :], start=False, stop=False)
                pe.matmul(fin_bank(i), hth[:, tok], wel[:, :], start=False, stop=False)
                pe.matmul(fin_bank(i), htl[:, tok], weh[:, :], start=False, stop=True).then_inc(fin_t, 1)

            out_s(3)
            out_s(4)
            ln3(0)
            ln3(1)
            out_s(5)
            ln3(2)
            out_s(6)
            ln3(3)
            hidden(0)
            hidden(1)
            out_s(7)
            hidden(2)
            hidden(3)
            base(0)
            ln3(4)
            ln3(5)
            base(1)
            ln3(6)
            base(2)
            ln3(7)
            base(3)
            for i in range(4, NT):
                hidden(i)
            base(4)
            base(5)
            pe.wait_ge(hg_c, 4)
            for i in range(NT):
                pe.wait_ge(hw_done, i + 1)
                last = pe.transpose(sc[:, i // 4, (i % 4) * P:(i % 4 + 1) * P], hw[:, i, :], ident)
                if i % 4 == 3:
                    last.then_inc(hw_t, 1)
            for i in range(6):
                moe(i)
            for i in range(6, NT):
                base(i)
                moe(i)


def kernel(x, ctx_4096, L0_xattn_Wq, L0_xattn_Wk, L0_xattn_Wv, L0_xattn_Wd, L0_attn_Wq, L0_attn_bq,
           L0_attn_Wk, L0_attn_bk, L0_attn_Wv, L0_attn_bv, L0_attn_Wo, L0_attn_bo, L0_ffn_W_base,
           L0_ffn_b_base, L0_ffn_W_gate, L0_ffn_W_thr, L0_ffn_b_thr, L0_ffn_A, L0_ffn_B):
    import numpy as np
    import concourse.bacc as bacc
    from concourse.bass_utils import run_bass_kernel_spmd

    def A(a):
        return np.asarray(a)

    consts = np.zeros((P, NCONST), np.float32)
    consts[:, C_ID:C_ID + P] = np.eye(P, dtype=np.float32)
    inv = (np.float32(1.0) / np.float32(10000.0) ** (np.arange(0, DH, 2, dtype=np.float32) / np.float32(DH)))
    ang = (np.arange(S, dtype=np.float32)[None, :] * inv.astype(np.float32)[:, None]).astype(np.float32)
    consts[:, C_COS:C_COS + S] = np.concatenate([np.cos(ang), np.cos(ang)], 0)
    consts[:, C_SIN:C_SIN + S] = np.concatenate([-np.sin(ang), np.sin(ang)], 0)
    row = np.arange(P)[:, None] % S
    consts[:, C_MASK:C_MASK + S] = np.where(np.arange(S)[None, :] <= row, 0.0, NEG)
    consts[:, C_PAR] = np.arange(P) // SD % 2 == 0
    consts[:, C_PAR + 1] = np.arange(P) // SD % 2 == 1

    def rows(w):
        return A(w).T.reshape(-1, P, A(w).shape[0]).transpose(1, 0, 2)

    xin = A(x).reshape(NT, P, D).transpose(1, 0, 2)
    ctxT = A(ctx_4096)[:, :S, :].reshape(TOK, KT, P).transpose(2, 1, 0)
    wq, wk, wv = (rows(w) for w in (L0_xattn_Wq, L0_xattn_Wk, L0_xattn_Wv))
    wd = rows(L0_xattn_Wd)
    w_x = np.empty((NKV, P, 5, PIECE), np.float32)
    for g in range(NKV):
        kv = slice(g * P, (g + 1) * P)
        w_x[g, :, 0] = np.concatenate([wk[:, :, kv], wv[:, :, kv]], 2).reshape(P, -1)
        for i in range(2):
            q = slice((REP * g + 2 * i) * P, (REP * g + 2 * i + 2) * P)
            w_x[g, :, 1 + i] = wq[:, :, q].reshape(P, -1)
            w_x[g, :, 3 + i] = wd[:, REP * g + 2 * i:REP * g + 2 * i + 2].reshape(P, -1)
    sq, sk, sv = (rows(w) for w in (L0_attn_Wq, L0_attn_Wk, L0_attn_Wv))
    w_s = np.empty((KT, P, 1536), np.float32)
    for t in range(KT):
        c = slice(t * P, (t + 1) * P)
        w_s[t, :, :1024] = np.concatenate([sk[:, :, c], sv[:, :, c]], 2).reshape(P, -1)
        w_s[t, :, 1024:] = sq[:, :, c].reshape(P, -1)
    arrays = {
        "x": xin, "ctxT": ctxT, "w_x": w_x, "w_s": w_s,
        "w_o": rows(L0_attn_Wo).reshape(P, -1), "w_b": rows(L0_ffn_W_base).reshape(P, -1),
        "w_ag": np.concatenate([rows(A(L0_ffn_A).reshape(NE * NR, D)), rows(L0_ffn_W_gate), rows(L0_ffn_W_thr)], 2),
        "w_eb": A(L0_ffn_B).transpose(0, 2, 1).reshape(NE * NR, D),
        "consts": consts,
        "bias_cols": np.stack([A(b).reshape(KT, P).T for b in (L0_attn_bq, L0_attn_bk, L0_attn_bv)], 1),
        "bias_rows": np.stack([np.broadcast_to(A(b), (P, D)) for b in (L0_attn_bo, L0_ffn_b_base)]),
        "b_thr": np.broadcast_to(A(L0_ffn_b_thr), (P, 1)),
    }
    nc = bacc.Bacc("TRN2", target_bir_lowering=False, num_devices=1)
    arrays = {f"in_{n}": np.ascontiguousarray(a) for n, a in arrays.items()}
    args = [nc.dram_tensor(n, a.shape, mybir.dt.from_np(a.dtype), kind="ExternalInput").ap()
            for n, a in arrays.items()]
    out = nc.dram_tensor("out", (P, NT, D), F32, kind="ExternalOutput").ap()
    build(nc, *args, out)
    r = run_bass_kernel_spmd(nc, [arrays], core_ids=[0])
    return r.results[0]["out"].reshape(P, NT, D).transpose(1, 0, 2).reshape(B, S, D)
```

```python
from contextlib import ExitStack

import concourse.bass as bass
from concourse import mybir

F32 = mybir.dt.float32
F32R = mybir.dt.float32r
ALU = mybir.AluOpType
ACT = mybir.ActivationFunctionType
AXX = mybir.AxisListType.X

P = 128
B, S, D = 16, 64, 512
KT = D // P
TOK = B * S
NT = TOK // P
HALF = TOK // 2
HB = B // 2
DH = 128
NKV = 8
REP = 4
SH = 32
SD = D // SH
NE, NR = 8, 16
NG = NE + 1
EPS = 1e-5
NEG = -1.0e30
X_SCALE = float(DH) ** -0.5
S_SCALE = float(SD) ** -0.5
MAX_THR = 0.125
SCALING = 2.0

XT = 2 + REP
NU = 2 * NKV
XCH = 2
ST = 3
SCH = 4
NSU = 2 * KT
UNITS = [(0, 0), (1, 0), (0, 1), (1, 1), (2, 0), (3, 0), (2, 1), (3, 1)]
WARM_UP = 16
PIECE = 1024
C_ID, C_COS, C_SIN, C_MASK, C_PAR = 0, 128, 192, 256, 320
NCONST = 322


def build(nc, x, ctxT, w_x, w_s, w_o, w_b, w_ag, w_eb, consts, bias_cols, bias_rows, b_thr, out):
    es = ExitStack()
    with es:
        def sem(name):
            return es.enter_context(nc.semaphore(name))

        def sb(stack, name, shape, dt=F32):
            return stack.enter_context(nc.sbuf_tensor(name, shape, dt))

        X = sb(es, "X", [P, NT, D])
        xh = sb(es, "xh", [P, KT, TOK], F32R)
        xl = sb(es, "xl", [P, KT, TOK], F32R)
        ah = sb(es, "ah", [P, KT, TOK], F32R)
        al = sb(es, "al", [P, KT, TOK], F32R)
        raw = [sb(es, f"raw{i}", [P, PIECE]) for i in range(2)]
        sm = [sb(es, f"sm{i}", [P, 512]) for i in range(2)]
        cst = sb(es, "cst", [P, NCONST])
        bcol = sb(es, "bcol", [P, 3, KT])
        bthr = sb(es, "bthr", [P, 1])
        stats = sb(es, "stats", [P, NT, 6])
        mv = sb(es, "mv", [P, NT, 2])
        veps = sb(es, "veps", [P, NT])
        rstd = sb(es, "rstd", [P, NT])
        mhalf = sb(es, "mhalf", [P, NT])
        mx = sb(es, "mx", [P, 4, 8])
        zs = sb(es, "zs", [P, 4, 8])
        rz = sb(es, "rz", [P, 4, 8])
        bqm = sb(es, "bqm", [P, 2, KT])
        xs = ExitStack()
        wqh = sb(xs, "wqh", [P, 3, KT, 256], F32R)
        wql = sb(xs, "wql", [P, 3, KT, 256], F32R)
        wdh = sb(xs, "wdh", [P, REP, D], F32R)
        wdl = sb(xs, "wdl", [P, REP, D], F32R)
        kr = [sb(xs, f"kr{i}", [P, HB, S]) for i in range(2)]
        qr = [sb(xs, f"qr{i}", [P, HB, REP, S]) for i in range(2)]
        vt = sb(xs, "vt", [P, HB, S])
        sb(xs, "gap_x", [P, 512])
        v2h, v2l = [None, None], [None, None]
        for i in range(2):
            v2h[i] = sb(xs, f"v2h{i}", [P, HB, DH], F32R)
            v2l[i] = sb(xs, f"v2l{i}", [P, HB, DH], F32R)
        ch = sb(xs, "ch", [P, REP, HALF], F32R)
        cl = sb(xs, "cl", [P, REP, HALF], F32R)
        pt = [sb(xs, f"pt{i}", [P, 1024], F32R) for i in range(2)]
        t1 = [sb(xs, f"t1{i}", [P, HALF]) for i in range(2)]
        sw = [sb(xs, f"sw{i}", [P, HALF]) for i in range(2)]
        xs.close()
        rawctx = [qr[i][:, :, :, :].rearrange("p b r s -> p (b r s)").rearrange("p (k t) -> p k t", k=KT)
                  for i in range(2)]

        ss = ExitStack()
        ws = [sb(ss, f"ws{i}", [P, 2, KT, 384], F32R) for i in range(KT)]
        kb, qm, vc = [None, None], [None, None], [None, None]
        kb[0] = sb(ss, "kb0", [P, HB, 4, S])
        qm[0] = sb(ss, "qm0", [P, HB, 2, S])
        vts = sb(ss, "vts", [P, HALF])
        vc[0] = sb(ss, "vc0", [P, HB, 2, 64])
        kb[1] = sb(ss, "kb1", [P, HB, 4, S])
        qm[1] = sb(ss, "qm1", [P, HB, 2, S])
        vc[1] = sb(ss, "vc1", [P, HB, 2, 64])
        brow_o = sb(ss, "brow_o", [P, D])
        ot = [sb(ss, f"ot{i}", [P, HALF]) for i in range(2)]
        osel = [sb(ss, f"osel{i}", [P, 2 * S]) for i in range(2)]
        pts = [sb(ss, f"pts{i}", [P, 512]) for i in range(2)]
        sb(ss, "gap_s", [P, 768])
        sm4 = sm + [sb(ss, f"sm{i}", [P, 512]) for i in (2, 3)]
        ss.close()
        fs = ExitStack()
        woh = sb(fs, "woh", [P, KT, D], F32R)
        wol = sb(fs, "wol", [P, KT, D], F32R)
        brow_b = sb(fs, "brow_b", [P, D])
        sb(fs, "gap_f", [P, 1536])
        wbh = sb(fs, "wbh", [P, KT, D], F32R)
        wbl = sb(fs, "wbl", [P, KT, D], F32R)
        weh = sb(fs, "weh", [P, D], F32R)
        wel = sb(fs, "wel", [P, D], F32R)
        wag = sb(fs, "wag", [P, KT, P + NG])
        sb(fs, "gap_g", [P, 1024 - KT * (P + NG)])
        xf = sb(fs, "xf", [P, KT, TOK])
        hg = sb(fs, "hg", [P, NT, P + NG])
        hw = sb(fs, "hw", [P, NT, P])
        hth = sb(fs, "hth", [P, TOK], F32R)
        htl = sb(fs, "htl", [P, TOK], F32R)
        gm = sb(fs, "gm", [P, NT])
        ge = sb(fs, "ge", [P, NT, NE])
        gz = sb(fs, "gz", [P, NT])
        gr = sb(fs, "gr", [P, NT])
        gt = sb(fs, "gt", [P, NT])
        gw = sb(fs, "gw", [P, NT, NE])
        gs = sb(fs, "gs", [P, NT])
        fs.close()

        def pb(name):
            return es.enter_context(nc.psum_tensor(name, [P, 2, 512], F32))
        pj, sc, tp, pv = pb("pj"), pb("sc"), pb("tp"), pb("pv")

        s_const = sem("s_const")
        s_cols = sem("s_cols")
        s_x = [sem(f"s_x{i}") for i in range(4)]
        s_ctx = [sem(f"s_ctx{i}") for i in range(4)]
        s_w = [sem(f"s_w{i}") for i in range(2)]
        s_row = sem("s_row")
        s_row2 = sem("s_row2")
        ln3_lo = sem("ln3_lo")
        s_out = sem("s_out")
        whi = sem("whi")
        wlo = sem("wlo")
        wd_lo = sem("wd_lo")
        chi = sem("chi")
        clo = sem("clo")
        mh_set = sem("mh_set")
        warm_set = sem("warm_set")
        dve_seq = sem("dve_seq")
        ln_var = sem("ln_var")
        ln_rstd = sem("ln_rstd")
        ln_xn = sem("ln_xn")
        ln_t = sem("ln_t")
        ln_hi = sem("ln_hi")
        pj_dve = sem("pj_dve")
        pj_act = sem("pj_act")
        proj = sem("proj")
        t1_done = sem("t1_done")
        sin_done = sem("sin_done")
        rope = sem("rope")
        tp_t = sem("tp_t")
        tp_hi = sem("tp_hi")
        tp_lo = sem("tp_lo")
        scored = sem("scored")
        masked = sem("masked")
        maxed = sem("maxed")
        subbed = sem("subbed")
        exped = sem("exped")
        summed = sem("summed")
        recd = sem("recd")
        normed = sem("normed")
        pv_t = sem("pv_t")
        pv_hi = sem("pv_hi")
        pv_lo = sem("pv_lo")
        outp = sem("outp")
        zeroed = sem("zeroed")
        bq_done = sem("bq_done")
        k_done, q_done, v_done = sem("k_done"), sem("q_done"), sem("v_done")
        vt_t, vc_done = sem("vt_t"), sem("vc_done")
        pt_t, pt_done = sem("pt_t"), sem("pt_done")
        spv, ssel, ssel1 = sem("spv"), sem("ssel"), sem("ssel1")
        o_hi, o_lo = sem("o_hi"), sem("o_lo")
        xbo = sem("xbo")
        hg_t, hg_c = sem("hg_t"), sem("hg_c")
        gate = sem("gate")
        gexp = sem("gexp")
        hw_done = sem("hw_done")
        hw_t, hw_hi, hw_lo = sem("hw_t"), sem("hw_hi"), sem("hw_lo")
        fin_t, fin = sem("fin_t"), sem("fin")

        ident = cst[:, C_ID:C_ID + P]

        def rep(ap, n):
            return ap.unsqueeze(1).to_broadcast([ap.shape[0], n, S])

        def per_group(ap, n):
            return ap.unsqueeze(2).to_broadcast([P, n, S])

        mask3 = rep(cst[:, C_MASK:C_MASK + S], 8)
        W_X = 5 * NKV
        WL_X = 3 * NKV
        PD_LN1 = NT
        PD_14 = PD_LN1 + 4 * (NU - 1)
        PD_LN2A = PD_14 + 4
        PD_X = PD_LN2A + 4
        PD_LN2 = PD_X + 4
        PA_X = XT * NU
        N_SM = XCH * NU
        N_SS = SCH * NSU

        late = []
        for t in range(KT):
            late.append((w_s[t, :, 0:1024], ws[t][:, 0, :, 0:256], ws[t][:, 1, :, 0:256], 256))
            late.append((w_s[t, :, 1024:1536], ws[t][:, 0, :, 256:384], ws[t][:, 1, :, 256:384], 128))
        for i in range(2):
            late.append((w_o[:, i * 1024:(i + 1) * 1024], woh[:, 2 * i:2 * i + 2, :], wol[:, 2 * i:2 * i + 2, :], D))
        N_SELF = len(late)
        for i in range(2):
            late.append((w_b[:, i * 1024:(i + 1) * 1024], wbh[:, 2 * i:2 * i + 2, :], wbl[:, 2 * i:2 * i + 2, :], D))
        late.append((w_eb, weh[:, :].unsqueeze(1), wel[:, :].unsqueeze(1), D))
        LATE_AT = {4: 1, 5: 4, 6: 8, 7: 10, 8: 16, 9: 20}
        BIAS_AT = (6, 7, 11, 12, 14, 15, 18, 19)
        OUT_AT = N_SS - 6
        OUT_SHARE = 6

        def late_buf(i):
            b = 1 - i % 2
            return b, 16 * ((17 if b == 0 else 23) + i // 2 + 1)

        def late_raw(i):
            width = late[i][3]
            n = late[i][1].shape[1]
            return raw[late_buf(i)[0]][:, 0:n * width].rearrange("p (k c) -> p k c", k=n)

        def ln_bank(n):
            t, b = (((pv, 0), (pv, 1), (sc, 0), (sc, 1)), ((pv, 0), (pv, 1), (pj, 0), (pv, 0)),
                    ((pj, 0), (pj, 1), (sc, 0), (sc, 1)), ((pv, 0), (pv, 1), (sc, 1), (tp, 1)),
                    ((sc, 0), (sc, 1), (tp, 0), (tp, 1)), ((tp, 0), (tp, 1), (tp, 0), (tp, 1)))[n // 4][n % 4]
            return t[:, b, :]

        def ln_tmp(n):
            if 4 <= n < 8:
                return sm[n % 2][:, :]
            return ((sm[0], sm[1], t1[1], sw[1]), (t1[1], sw[1], t1[0], sw[0]), sm4)[n // NT][n % 4][:, :]

        def fin_bank(i):
            return (pj, pv, tp)[i // 2 % 3][:, i % 2, :]

        block = es.enter_context(nc.Block())

        @block.sync
        def _(sp):
            def load_x(i):
                sp.dma_start(X[:, 2 * i:2 * i + 2, :], x[:, 2 * i:2 * i + 2, :]).then_inc(s_x[i], 16)

            def load_ctx(half, i):
                sp.dma_start(rawctx[half][:, 2 * i:2 * i + 2, :],
                             ctxT[:, 2 * i:2 * i + 2, half * HALF:(half + 1) * HALF]).then_inc(s_ctx[2 * half + i], 16)

            sp.dma_start(raw[0][:, :], w_x[0, :, 0, :]).then_inc(s_w[0], 16)
            load_ctx(0, 0)
            load_ctx(0, 1)
            load_x(0)
            sp.dma_start(cst[:, :], consts).then_inc(s_const, 16)
            load_x(1)
            sp.dma_start(raw[1][:, :], w_x[0, :, 1, :]).then_inc(s_w[1], 16)
            sp.wait_ge(wlo, 1)
            sp.dma_start(raw[0][:, :], w_x[0, :, 2, :]).then_inc(s_w[0], 16)
            load_x(2)
            load_x(3)
            load_ctx(1, 0)
            load_ctx(1, 1)
            sp.dma_start(bcol[:, :, :], bias_cols).then_inc(s_cols, 16)
            sp.dma_start(bthr[:, :], b_thr).then_inc(s_cols, 16)

            def stream(g, last):
                srcs = [(g, 3), (g, 4)] + ([] if last else [(g + 1, 0), (g + 1, 1), (g + 1, 2)])
                for i, (gg, j) in enumerate(srcs):
                    src = w_x[gg, :, j, :]
                    b = (1, 0, 1, 0, 1)[i]
                    if i in (2, 3):
                        sp.wait_ge(wd_lo, 2 * g + i - 1)
                    else:
                        sp.wait_ge(wlo, 3 * g + (3 if i < 2 else 4))
                    sp.dma_start(raw[b][:, :], src).then_inc(s_w[b], 16)

            with sp.Fori(0, NKV - 1) as g:
                stream(g, False)
            stream(NKV - 1, True)

            def late_load(i):
                b, _ = late_buf(i)
                if i < 2:
                    sp.wait_ge(wd_lo, 2 * NKV - 1 + i)
                else:
                    sp.wait_ge(wlo, WL_X + i - 1)
                n = late[i][1].shape[1] * late[i][3]
                sp.dma_start(raw[b][:, 0:n], late[i][0]).then_inc(s_w[b], 16)

            for i in range(4):
                late_load(i)
            sp.wait_ge(pj_dve, PD_X)
            sp.dma_start(brow_o[:, :], bias_rows[0]).then_inc(s_row, 16)
            for i in range(4, N_SELF):
                late_load(i)
            sp.wait_ge(proj, PA_X + ST * NSU)
            sp.dma_start(wag[:, :, :], w_ag).then_inc(s_row2, 16)
            sp.dma_start(brow_b[:, :], bias_rows[1]).then_inc(s_row2, 16)
            for i in range(N_SELF, len(late)):
                late_load(i)
            for i in range(NT):
                sp.wait_ge(fin, i + 1)
                sp.dma_start(out[:, i, :], X[:, i, :]).then_inc(s_out, 16)
            sp.wait_ge(s_out, 16 * NT)

        @block.gpsimd
        def _(pool):
            pool.memset(pt[0][:, 0:640].bitcast(F32), 0.0).then_inc(warm_set, 1)
            pool.memset(mhalf[:, :], -0.5).then_inc(mh_set, 1)

            def split_out(v):
                t, h = UNITS[v]
                pool.wait_ge(o_hi, v + 1)
                pool.tensor_tensor(al[:, t, h * HALF:(h + 1) * HALF], ot[v % 2][:, :],
                                   ah[:, t, h * HALF:(h + 1) * HALF].bitcast(F32),
                                   ALU.subtract).then_inc(o_lo, 1)

            def split_lo(n, hi, lo, src):
                pool.wait_ge(whi, n + 1)
                pool.tensor_tensor(lo, src, hi.bitcast(F32), ALU.subtract).then_inc(wlo, 1)

            def split_x(n, j, b):
                split_lo(n, wqh[:, j].rearrange("p k c -> p (k c)"), wql[:, j].rearrange("p k c -> p (k c)"),
                         raw[b][:, :])

            def ln_pow(grp):
                pool.wait_ge(ln_var, grp + 1)
                c = slice(4 * (grp % 2), 4 * (grp % 2) + 4)
                pool.tensor_tensor(rstd[:, c], veps[:, c], mhalf[:, c], ALU.pow).then_inc(ln_rstd, 1)

            pool.wait_ge(mh_set, 1)
            split_x(0, 0, 0)
            ln_pow(0)

            def rope_tile(u, h, idx):
                par = (h + idx) % 2
                pj_n = XT * u + (1 if idx == 0 else 2 + idx)
                pool.wait_ge(pj_act, pj_n)
                pool.tensor_tensor(sw[par][:, :].rearrange("p (b s) -> p b s", s=S),
                                   sw[par][:, :].rearrange("p (b s) -> p b s", s=S),
                                   rep(cst[:, C_SIN:C_SIN + S], HB), ALU.mult).then_inc(sin_done, 1)
                pool.wait_ge(sin_done, 5 * u + idx + 1)
                o = kr[h][:, :, :] if idx == 0 else qr[h][:, :, idx - 1, :]
                pool.tensor_tensor(o, t1[par][:, :].rearrange("p (b s) -> p b s", s=S),
                                   sw[par][:, :].rearrange("p (b s) -> p b s", s=S),
                                   ALU.add).then_inc(rope, 1)

            def subtract_max(n, c):
                pool.wait_ge(maxed, n + 1)
                s3 = sm4[c][:, :].rearrange("p (n s) -> p n s", s=S)
                pool.tensor_tensor(s3, s3, per_group(mx[:, c, :], 8), ALU.subtract).then_inc(subbed, 1)

            def normalise(n, c):
                pool.wait_ge(recd, n + 1)
                s3 = sm4[c][:, :].rearrange("p (n s) -> p n s", s=S)
                pool.tensor_tensor(s3, s3, per_group(rz[:, c, :], 8), ALU.mult).then_inc(normed, 1)

            split_x(1, 1, 1)
            rope_tile(0, 0, 0)
            split_x(2, 2, 0)
            ln_pow(1)
            for idx in range(1, 4):
                rope_tile(0, 0, idx)

            def phase(u, h, g, nxt):
                subtract_max(2 * u, 0)
                subtract_max(2 * u + 1, 1)
                normalise(2 * u, 0)
                normalise(2 * u + 1, 1)
                rope_tile(u + 1, 1 - h, 0)
                rope_tile(u + 1, 1 - h, 1)
                rope_tile(u + 1, 1 - h, 2)
                rope_tile(u + 1, 1 - h, 3)
                if h == 0 and nxt == "loop":
                    split_x(5 * g + 5, 0, 1)
                rope_tile(u + 1, 1 - h, 4)
                if h == 0 and nxt == "loop":
                    split_x(5 * g + 6, 1, 0)
                    split_x(5 * g + 7, 2, 1)

            with pool.Fori(0, NKV - 1) as g:
                phase(2 * g, 0, g, "loop")
                phase(2 * g + 1, 1, g, "loop")
            phase(NU - 2, 0, NKV - 1, "last")

            def late_lo(i):
                split_lo(W_X + i, late[i][1], late[i][2], late_raw(i))

            late_lo(0)
            subtract_max(N_SM - 2, 0)
            late_lo(1)
            normalise(N_SM - 2, 0)
            ln_pow(2)
            subtract_max(N_SM - 1, 1)
            pool.wait_ge(scored, N_SM)
            pool.memset(kb[0][:, :, :, :], 0.0).then_inc(zeroed, 1)
            normalise(N_SM - 1, 1)
            pool.memset(vc[0][:, :, :, :], 0.0).then_inc(zeroed, 1)
            late_lo(2)
            pool.wait_ge(pv_t, N_SM)
            pool.memset(kb[1][:, :, :, :], 0.0).then_inc(zeroed, 1)
            subtract_max(N_SM, 0)
            subtract_max(N_SM + 1, 1)
            late_lo(3)
            normalise(N_SM, 0)
            normalise(N_SM + 1, 1)
            pool.wait_ge(pj_dve, PD_X)
            pool.memset(vc[1][:, :, :, :], 0.0).then_inc(zeroed, 1)
            ln_pow(3)

            for n in range(N_SS):
                v, c = n // SCH, n % SCH
                if n + 2 < N_SS:
                    subtract_max(N_SM + n + 2, (n + 2) % 4)
                if 1 <= n and n + 1 < N_SS:
                    normalise(N_SM + n + 1, (n + 1) % 4)
                for i, at in LATE_AT.items():
                    if at == n:
                        late_lo(i)
                if n in BIAS_AT:
                    i = BIAS_AT.index(n)
                    if i == 0:
                        pool.wait_ge(s_row, 16)
                        pool.wait_ge(ln_xn, 2 * NT)
                    pool.tensor_tensor(X[:, i, :], X[:, i, :], brow_o[:, :], ALU.add).then_inc(xbo, 1)
                if v and c == (1 if v == NSU - 2 else 2):
                    split_out(v - 1)
            split_out(NSU - 1)
            ln_pow(4)
            for i in range(N_SELF, len(late)):
                late_lo(i)
            ln_pow(5)
            pool.wait_ge(s_row2, 32)
            for i in range(NT):
                pool.wait_ge(ln_xn, 2 * NT + i + 1)
                pool.tensor_tensor(X[:, i, :], X[:, i, :], brow_b[:, :], ALU.add).then_inc(xbo, 1)

        @block.scalar
        def _(act):
            def hi(src, dst, s):
                act.activation(dst, src, ACT.Copy).then_inc(s, 1)

            def split_x(j, b, w_n):
                act.wait_ge(s_w[b], 16 * w_n)
                if j < 3:
                    hi(raw[b][:, :], wqh[:, j].rearrange("p k c -> p (k c)"), whi)
                else:
                    hi(raw[b][:, :], wdh[:, 2 * (j - 3):2 * (j - 3) + 2].rearrange("p k c -> p (k c)"), whi)

            def ln_hi_tile(n, also=None):
                i = n % NT
                act.wait_ge(ln_t, n + 1)
                src = ln_bank(n).rearrange("p (k t) -> p k t", k=KT)
                if also is not None:
                    act.activation(also[:, :, i * P:(i + 1) * P], src, ACT.Copy)
                hi(src, xh[:, :, i * P:(i + 1) * P], ln_hi)

            def ctx_hi(half, ks):
                for k in ks:
                    if k % 2 == 0:
                        act.wait_ge(s_ctx[2 * half + k // 2], 16)
                    hi(rawctx[half][:, k, :], ah[:, k, half * HALF:(half + 1) * HALF], chi)

            split_x(0, 0, 1)
            ctx_hi(0, range(KT))

            def swap_halves(u, h, idx, first):
                par = (h + idx) % 2
                act.wait_ge(t1_done, 5 * u + idx + 1)
                if not (first and idx < 2):
                    act.wait_ge(rope, 5 * u + idx - 1)
                bank = (1 + idx) % 2 if idx else 0
                src = pj[:, bank, :]
                act.activation(sw[par][0:64, :], src[64:128, :], ACT.Copy)
                act.activation(sw[par][64:128, :], src[0:64, :], ACT.Copy).then_inc(pj_act, 1)

            def copy_v(u):
                act.wait_ge(proj, XT * u + 2)
                act.activation(vt[:, :, :].rearrange("p b s -> p (b s)"), pj[:, 1, :], ACT.Copy).then_inc(pj_act, 1)

            def v_hi(u, h):
                act.wait_ge(tp_t, 3 * u + 1)
                for odd in range(2):
                    for half in range(2):
                        last = act.activation(
                            v2h[h][64 * half:64 * half + 64].rearrange("p (b o) d -> p b o d", o=2)[:, :, odd, :],
                            tp[64 * odd:64 * odd + 64, 0, :].rearrange("p (b d) -> p b d", d=DH), ACT.Copy)
                last.then_inc(tp_hi, 1)

            def p_hi(u, c):
                act.wait_ge(tp_t, 3 * u + 2 + c)
                for hp in range(2):
                    last = act.activation(pt[c][0:64, :].rearrange("p (b r q) -> p b r q", b=4, r=2)[:, :, hp, :],
                                          tp[64 * hp:64 * hp + 64, c, :].rearrange("p (b q) -> p b q", b=4), ACT.Copy)
                last.then_inc(tp_hi, 1)

            def exp(n, c, scale):
                act.wait_ge(subbed, n + 1)
                act.activation(sm4[c][:, :], sm4[c][:, :], ACT.Exp, scale=scale).then_inc(exped, 1)

            def c_hi(u, c):
                act.wait_ge(pv_t, 2 * u + c + 1)
                for r in range(REP):
                    last = act.activation(
                        ch[:, r, c * 256:(c + 1) * 256].rearrange("p (b q) -> p b q", q=S),
                        pv[:, :, :].rearrange("p a (b r q) -> p (a b) r q", b=2, r=REP)[:, :, r, :], ACT.Copy)
                last.then_inc(pv_hi, 1)

            split_x(1, 1, 1)
            swap_halves(0, 0, 0, True)
            ln_hi_tile(0)
            ln_hi_tile(1)
            ln_hi_tile(2)
            ln_hi_tile(3)
            copy_v(0)
            split_x(2, 0, 2)
            ctx_hi(1, range(KT))
            swap_halves(0, 0, 1, True)
            swap_halves(0, 0, 2, True)
            ln_hi_tile(4)
            ln_hi_tile(5)
            swap_halves(0, 0, 3, True)
            swap_halves(0, 0, 4, True)
            ln_hi_tile(6)
            ln_hi_tile(7)
            v_hi(0, 0)

            def phase(u, h, g, nxt):
                exp(2 * u, 0, X_SCALE)
                swap_halves(u + 1, 1 - h, 0, False)
                exp(2 * u + 1, 1, X_SCALE)
                copy_v(u + 1)
                p_hi(u, 0)
                swap_halves(u + 1, 1 - h, 1, False)
                p_hi(u, 1)
                if h == 0:
                    act.wait_ge(pj_dve, PD_LN1 + 8 * g)
                    split_x(3, 1, 2 + 3 * g)
                    split_x(4, 0, 3 + 2 * g)
                swap_halves(u + 1, 1 - h, 2, False)
                c_hi(u, 0)
                swap_halves(u + 1, 1 - h, 3, False)
                if h == 0 and nxt == "loop":
                    split_x(0, 1, 3 + 3 * g)
                swap_halves(u + 1, 1 - h, 4, False)
                c_hi(u, 1)
                v_hi(u + 1, 1 - h)
                if h == 0 and nxt == "loop":
                    split_x(1, 0, 4 + 2 * g)
                    split_x(2, 1, 4 + 3 * g)

            with act.Fori(0, NKV - 1) as g:
                phase(2 * g, 0, g, "loop")
                phase(2 * g + 1, 1, g, "loop")
            phase(NU - 2, 0, NKV - 1, "last")

            def late_hi(i):
                b, n = late_buf(i)
                act.wait_ge(s_w[b], n)
                act.activation(late[i][1], late_raw(i), ACT.Copy).then_inc(whi, 1)

            def k_tile(v):
                t, h = UNITS[v]
                act.wait_ge(proj, PA_X + ST * v + 1)
                src = pj[:, (ST * v) % 2, :].rearrange("p (b s) -> p b s", s=S)
                for j in range(4):
                    r = slice(32 * j, 32 * j + 32)
                    last = act.activation(kb[v % 2][r, :, j, :], src[r], ACT.Identity, bias=bcol[r, 1, t:t + 1])
                last.then_inc(pj_act, 1)

            def q_tile(v):
                t, h = UNITS[v]
                act.wait_ge(proj, PA_X + ST * v + 2)
                src = pj[:, (ST * v + 1) % 2, :].rearrange("p (b s) -> p b s", s=S)
                for par in range(2):
                    last = act.activation(qm[v % 2][:, :, par, :], src, ACT.Identity,
                                          bias=bqm[:, par, t:t + 1], scale=cst[:, C_PAR + par:C_PAR + par + 1])
                last.then_inc(pj_act, 1)

            def v_tile(v):
                t = v // 2
                act.wait_ge(proj, PA_X + ST * v + 3)
                act.activation(vts[:, :], pj[:, (ST * v + 2) % 2, :], ACT.Copy).then_inc(pj_act, 1)

            def pt_copy(n):
                act.wait_ge(pt_t, n + 1)
                act.activation(pts[n % 2][:, :], tp[:, n % 2, :], ACT.Copy).then_inc(pt_done, 1)

            def out_hi(v):
                t, h = UNITS[v]
                act.wait_ge(ssel, SCH * v + SCH)
                hi(ot[v % 2][:, :], ah[:, t, h * HALF:(h + 1) * HALF], o_hi)

            late_hi(0)
            late_hi(1)
            act.wait_ge(s_cols, 32)
            for par in range(2):
                act.activation(bqm[:, par, :], bcol[:, 0, :], ACT.Copy,
                               scale=cst[:, C_PAR + par:C_PAR + par + 1]).then_inc(bq_done, 1)
            u = NU - 1
            exp(2 * u, 0, X_SCALE)
            p_hi(u, 0)
            ln_hi_tile(NT)
            ln_hi_tile(NT + 1)
            exp(2 * u + 1, 1, X_SCALE)
            ln_hi_tile(NT + 2)
            ln_hi_tile(NT + 3)
            act.wait_ge(zeroed, 1)
            act.wait_ge(bq_done, 2)
            k_tile(0)
            p_hi(u, 1)
            c_hi(u, 0)
            q_tile(0)
            late_hi(2)
            v_tile(0)
            c_hi(u, 1)
            late_hi(3)
            exp(N_SM, 0, S_SCALE)
            exp(N_SM + 1, 1, S_SCALE)
            act.wait_ge(zeroed, 3)
            k_tile(1)
            q_tile(1)
            for n in range(NT + 4, 2 * NT):
                ln_hi_tile(n)
            v_tile(1)
            for n in range(N_SS):
                v, c = n // SCH, n % SCH
                pt_copy(n)
                if n + 2 < N_SS:
                    exp(N_SM + n + 2, (n + 2) % 4, S_SCALE)
                for i, at in LATE_AT.items():
                    if at == n + 1:
                        late_hi(i)
                if c == 1 and v:
                    out_hi(v - 1)
                if c == 1 and 0 < v < NSU - 1:
                    v_tile(v + 1)
                elif c >= 2 and v + 2 < NSU:
                    (k_tile if c == 2 else q_tile)(v + 2)
                if n >= N_SS - 2:
                    late_hi(N_SELF + n - N_SS + 2)
            out_hi(NSU - 1)
            for n in range(2 * NT, 3 * NT):
                ln_hi_tile(n, xf)
                if n == 2 * NT + 3:
                    late_hi(len(late) - 1)
            act.wait_ge(gate, 3)
            act.activation(ge[:, :, :], ge[:, :, :], ACT.Exp)
            act.activation(gt[:, :], gt[:, :], ACT.Exp, scale=-1.0).then_inc(gexp, 1)
            for i in range(2):
                act.wait_ge(hw_t, i + 1)
                hi(sc[:, i, :], hth[:, i * 512:(i + 1) * 512], hw_hi)

        @block.vector
        def _(dve):
            seq = [0]

            def link(ins):
                seq[0] += 1
                ins.then_inc(dve_seq, 1)
                dve.wait_ge(dve_seq, seq[0])

            def ln_stats(i):
                dve.bn_stats(stats[:, i, :], X[:, i, :]).then_inc(dve_seq, 1)
                seq[0] += 1
                dve.wait_ge(dve_seq, seq[0])
                dve.bn_aggr(mv[:, i, :], stats[:, i, :]).then_inc(dve_seq, 1)
                seq[0] += 1

            def ln_eps(grp):
                dve.wait_ge(dve_seq, seq[0])
                c = slice(4 * grp, 4 * grp + 4)
                dve.tensor_scalar(veps[:, c], mv[:, c, 1], EPS, None, ALU.add).then_inc(ln_var, 1)

            def ln_apply(n):
                i = n % NT
                if i % 4 == 0:
                    dve.wait_ge(ln_rstd, n // 4 + 1)
                if n >= 4:
                    dve.wait_ge(ln_t, n - 1 if n in (6, 7) else n - 3)
                if n == 2 * NT:
                    dve.wait_ge(pt_t, N_SS)
                dve.tensor_scalar(ln_tmp(n), X[:, i, :], mv[:, i, 0:1], rstd[:, i:i + 1],
                                  ALU.subtract, ALU.mult).then_inc(ln_xn, 1)

            def ln_lo(n):
                i = n % NT
                dve.wait_ge(ln_hi, n + 1)
                dve.tensor_tensor(xl[:, :, i * P:(i + 1) * P], ln_bank(n).rearrange("p (k t) -> p k t", k=KT),
                                  xh[:, :, i * P:(i + 1) * P].bitcast(F32),
                                  ALU.subtract).then_inc(pj_dve if n < 2 * NT else ln3_lo, 1)

            def ln_half(first):
                ln_apply(first)
                for n in range(first + 1, first + 4):
                    ln_apply(n)
                    ln_lo(n - 1)
                ln_lo(first + 3)

            def rope_cos(u, h, idx, first):
                par = (h + idx) % 2
                tile = 0 if idx == 0 else 1 + idx
                dve.wait_ge(proj, XT * u + tile + 1)
                if not (first and idx < 2):
                    dve.wait_ge(rope, 5 * u + idx - 1)
                bank = tile % 2
                dve.tensor_tensor(t1[par][:, :].rearrange("p (b s) -> p b s", s=S),
                                  pj[:, bank, :].rearrange("p (b s) -> p b s", s=S),
                                  rep(cst[:, C_COS:C_COS + S], HB), ALU.mult).then_inc(t1_done, 1)

            def mask_max(n, c):
                s3 = sm4[c][:, :].rearrange("p (n s) -> p n s", s=S)
                dve.wait_ge(scored, n + 1)
                dve.tensor_tensor(s3, sc[:, c % 2, :].rearrange("p (n s) -> p n s", s=S), mask3,
                                  ALU.add).then_inc(masked, 1)
                dve.wait_ge(masked, n + 1)
                dve.tensor_reduce(mx[:, c, :], s3, AXX, ALU.max).then_inc(maxed, 1)

            def sum_rec(n, c):
                dve.wait_ge(exped, n + 1)
                dve.tensor_reduce(zs[:, c, :], sm4[c][:, :].rearrange("p (n s) -> p n s", s=S), AXX,
                                  ALU.add).then_inc(summed, 1)
                dve.wait_ge(summed, n + 1)
                dve.reciprocal(rz[:, c, :], zs[:, c, :]).then_inc(recd, 1)

            def v_lo(u, h):
                dve.wait_ge(tp_hi, 3 * u + 1)
                for odd in range(2):
                    for half in range(2):
                        r = slice(64 * half, 64 * half + 64)
                        last = dve.tensor_tensor(
                            v2l[h][r].rearrange("p (b o) d -> p b o d", o=2)[:, :, odd, :],
                            tp[64 * odd:64 * odd + 64, 0, :].rearrange("p (b d) -> p b d", d=DH),
                            v2h[h][r].rearrange("p (b o) d -> p b o d", o=2)[:, :, odd, :].bitcast(F32), ALU.subtract)
                last.then_inc(tp_lo, 1)

            def p_lo(u, c):
                dve.wait_ge(tp_hi, 3 * u + 2 + c)
                for hp in range(2):
                    p4 = pt[c][:, :].rearrange("p (b r q) -> p b r q", b=4, r=2)[:, :, hp, :]
                    last = dve.tensor_tensor(p4[64:128], tp[64 * hp:64 * hp + 64, c, :].rearrange("p (b q) -> p b q", b=4),
                                             p4[0:64].bitcast(F32), ALU.subtract)
                last.then_inc(tp_lo, 1)

            def c_lo(u, c):
                dve.wait_ge(pv_hi, 2 * u + c + 1)
                for r in range(REP):
                    cs = slice(c * 256, (c + 1) * 256)
                    last = dve.tensor_tensor(
                        cl[:, r, cs].rearrange("p (b q) -> p b q", q=S),
                        pv[:, :, :].rearrange("p a (b r q) -> p (a b) r q", b=2, r=REP)[:, :, r, :],
                        ch[:, r, cs].bitcast(F32).rearrange("p (b q) -> p b q", q=S), ALU.subtract)
                last.then_inc(pv_lo, 1)

            def wd_split(g, i):
                dve.wait_ge(whi, 5 * g + 4 + i)
                c = slice(2 * i, 2 * i + 2)
                dve.tensor_tensor(wdl[:, c].rearrange("p k c -> p (k c)"), raw[1 - i][:, :],
                                  wdh[:, c].rearrange("p k c -> p (k c)").bitcast(F32), ALU.subtract).then_inc(wd_lo, 1)

            def out_add(u, h, i):
                dve.wait_ge(outp, 4 * u + i + 1)
                dve.tensor_tensor(X[:, 4 * h + i, :], X[:, 4 * h + i, :], pj[:, i % 2, :],
                                  ALU.add).then_inc(pj_dve, 1)

            def stats_half(half):
                for i in range(4 * half, 4 * half + 4):
                    if i % 2 == 0:
                        dve.wait_ge(s_x[i // 2], 16)
                    dve.bn_stats(stats[:, i, :], X[:, i, :]).then_inc(dve_seq, 1)
                seq[0] += 4
                for i in range(4 * half, 4 * half + 4):
                    dve.wait_ge(dve_seq, seq[0] - 3 + i % 4)
                    dve.bn_aggr(mv[:, i, :], stats[:, i, :]).then_inc(dve_seq, 1)
                seq[0] += 4
                ln_eps(half)

            def ctx_lo(half, ks):
                for k in ks:
                    c = slice(half * HALF, (half + 1) * HALF)
                    dve.wait_ge(chi, KT * half + k + 1)
                    dve.tensor_tensor(al[:, k, c], rawctx[half][:, k, :], ah[:, k, c].bitcast(F32),
                                      ALU.subtract).then_inc(clo, 1)

            ctx_lo(0, range(KT))
            stats_half(0)
            dve.wait_ge(s_const, 16)
            rope_cos(0, 0, 0, True)
            for n in range(4):
                ln_apply(n)
            for n in range(4):
                ln_lo(n)
            stats_half(1)
            rope_cos(0, 0, 1, True)
            ln_apply(4)
            ln_apply(5)
            rope_cos(0, 0, 2, True)
            ln_apply(6)
            ln_apply(7)
            ln_lo(4)
            ln_lo(5)
            rope_cos(0, 0, 3, True)
            ctx_lo(1, (0, 1, 2))
            rope_cos(0, 0, 4, True)
            ctx_lo(1, (3,))
            s3 = sw[0][:, :].rearrange("p (b s) -> p b s", s=S)
            dve.wait_ge(pj_act, XT)
            dve.wait_ge(sin_done, 4)
            dve.tensor_tensor(s3, s3, rep(cst[:, C_SIN:C_SIN + S], HB), ALU.mult).then_inc(sin_done, 1)
            dve.wait_ge(sin_done, 5)
            dve.wait_ge(rope, 4)
            dve.tensor_tensor(qr[0][:, :, REP - 1, :], t1[0][:, :].rearrange("p (b s) -> p b s", s=S), s3,
                              ALU.add).then_inc(rope, 1)
            ln_lo(6)
            ln_lo(7)
            v_lo(0, 0)

            def phase(u, h, g, nxt):
                mask_max(2 * u, 0)
                mask_max(2 * u + 1, 1)
                sum_rec(2 * u, 0)
                rope_cos(u + 1, 1 - h, 0, False)
                sum_rec(2 * u + 1, 1)
                p_lo(u, 0)
                rope_cos(u + 1, 1 - h, 1, False)
                p_lo(u, 1)
                rope_cos(u + 1, 1 - h, 2, False)
                if h == 0:
                    wd_split(g, 0)
                    wd_split(g, 1)
                c_lo(u, 0)
                rope_cos(u + 1, 1 - h, 3, False)
                rope_cos(u + 1, 1 - h, 4, False)
                if nxt == "loop":
                    out_add(u, h, 0)
                    c_lo(u, 1)
                    out_add(u, h, 1)
                    v_lo(u + 1, 1 - h)
                    out_add(u, h, 2)
                    out_add(u, h, 3)
                else:
                    c_lo(u, 1)
                    for i in range(4):
                        if i == 2:
                            mask_max(2 * u + 2, 0)
                            v_lo(u + 1, 1 - h)
                        if i == 3:
                            sum_rec(2 * u + 2, 0)
                        out_add(u, h, i)
                        dve.wait_ge(pj_dve, PD_LN1 + 4 * u + i + 1)
                        ln_stats(i)
                    ln_eps(0)

            with dve.Fori(0, NKV - 1) as g:
                phase(2 * g, 0, g, "loop")
                phase(2 * g + 1, 1, g, "loop")
            phase(NU - 2, 0, NKV - 1, "last")

            def vc_copy(v):
                h = v % 2
                dve.wait_ge(vt_t, v + 1)
                src = tp[:, 0, :].rearrange("p (b t j d) -> p b t j d", b=4, t=2, j=2)
                dst = vc[h][:, :, :, :].rearrange("p (b o) t c -> p b o t c", o=2)
                for j in range(2):
                    for odd in range(2):
                        last = dve.tensor_copy(dst[64 * j:64 * j + 64, :, odd, :, 32 * j:32 * j + 32],
                                               src[64 * odd:64 * odd + 64, :, :, j, :])
                last.then_inc(vc_done, 1)

            def select_out(n):
                v, c = n // SCH, n % SCH
                t, h = UNITS[v]
                src = pv[:, n % 2, 0:256].rearrange("p (b r q) -> p b r q", b=2, r=2)
                dve.wait_ge(spv, n + 1)
                if n >= 2:
                    dve.wait_ge(ssel, n - 1)
                o3 = osel[n % 2][:, :].rearrange("p (b q) -> p b q", q=S)
                dve.tensor_scalar(o3, src[:, :, 0, :], cst[:, C_PAR:C_PAR + 1], bcol[:, 2, t:t + 1],
                                  ALU.mult, ALU.add).then_inc(ssel1, 1)
                dve.wait_ge(ssel1, n + 1)
                if c == 0 and v >= 2:
                    dve.wait_ge(o_lo, v - 1)
                dve.scalar_tensor_tensor(ot[v % 2][:, c * P:(c + 1) * P].rearrange("p (b q) -> p b q", q=S),
                                         src[:, :, 1, :], cst[:, C_PAR + 1:C_PAR + 2], o3,
                                         ALU.mult, ALU.add).then_inc(ssel, 1)

            u = NU - 1
            mask_max(2 * u + 1, 1)
            for n in range(NT, NT + 4):
                ln_apply(n)
            ln_lo(NT)
            ln_lo(NT + 1)
            sum_rec(2 * u + 1, 1)
            ln_lo(NT + 2)
            ln_lo(NT + 3)
            p_lo(u, 0)
            p_lo(u, 1)
            c_lo(u, 0)
            c_lo(u, 1)
            mask_max(N_SM, 0)
            mask_max(N_SM + 1, 1)
            dve.wait_ge(zeroed, 2)
            vc_copy(0)
            for i in range(4):
                dve.wait_ge(outp, 4 * u + i + 1)
                dve.tensor_tensor(X[:, 4 + i, :], X[:, 4 + i, :], pj[:, (i + 1) % 2, :], ALU.add).then_inc(pj_dve, 1)
                dve.wait_ge(pj_dve, PD_LN2A + i + 1)
                ln_stats(4 + i)
                if i < 2:
                    sum_rec(N_SM + i, i)
            ln_eps(1)
            mask_max(N_SM + 2, 2)
            for n in range(NT + 4, 2 * NT):
                ln_apply(n)
            def out_add_s(i):
                dve.wait_ge(outp, 4 * NU + i + 1)
                dve.wait_ge(xbo, i + 1)
                dve.tensor_tensor(X[:, i, :], X[:, i, :], pj[:, i % 2, :], ALU.add).then_inc(pj_dve, 1)
                dve.wait_ge(pj_dve, PD_LN2 + i + 1)
                ln_stats(i)

            for n in range(N_SS):
                v, c = n // SCH, n % SCH
                if 1 <= n and n + 1 < N_SS:
                    sum_rec(N_SM + n + 1, (n + 1) % 4)
                if n in (OUT_AT + 3, OUT_AT + 5):
                    out_add_s((n - OUT_AT - 3) // 2)
                if n == 0:
                    for i in range(NT + 4, 2 * NT):
                        ln_lo(i)
                else:
                    select_out(n - 1)
                if c == 3 and v + 1 < NSU:
                    if v == 0:
                        dve.wait_ge(zeroed, 4)
                    vc_copy(v + 1)
                if n + 3 < N_SS:
                    mask_max(N_SM + n + 3, (n + 3) % 4)
            select_out(N_SS - 1)
            out_add_s(2)
            out_add_s(3)
            ln_eps(0)
            for n in range(2 * NT, 2 * NT + 4):
                ln_apply(n)
            out_add_s(4)
            out_add_s(5)
            for n in range(2 * NT, 2 * NT + 4):
                ln_lo(n)
            out_add_s(6)
            out_add_s(7)
            ln_eps(1)
            def hg_copy(i):
                dve.wait_ge(hg_t, i + 1)
                dve.tensor_copy(hg[:, 2 * i:2 * i + 2, :],
                                sc[:, i % 2, 0:2 * (P + NG)].rearrange("p (a c) -> p a c", a=2)).then_inc(hg_c, 1)

            hg_copy(0)
            hg_copy(1)
            ln_half(2 * NT + 4)
            hg_copy(2)
            hg_copy(3)
            dve.wait_ge(hg_c, 4)
            logits = hg[:, :, P:P + NE]

            def per_e(ap):
                return ap.unsqueeze(2).to_broadcast([P, NT, NE])

            dve.tensor_reduce(gm[:, :], logits, AXX, ALU.max).then_inc(gate, 1)
            dve.wait_ge(gate, 1)
            dve.tensor_tensor(ge[:, :, :], logits, per_e(gm[:, :]), ALU.subtract).then_inc(gate, 1)
            dve.wait_ge(s_cols, 32)
            dve.tensor_scalar(gt[:, :], hg[:, :, P + NE], bthr[:, 0:1], None, ALU.add).then_inc(gate, 1)
            dve.wait_ge(gexp, 1)
            link(dve.tensor_reduce(gz[:, :], ge[:, :, :], AXX, ALU.add))
            link(dve.reciprocal(gr[:, :], gz[:, :]))
            link(dve.tensor_tensor(ge[:, :, :], ge[:, :, :], per_e(gr[:, :]), ALU.mult))
            link(dve.tensor_scalar(gt[:, :], gt[:, :], 1.0, None, ALU.add))
            link(dve.reciprocal(gt[:, :], gt[:, :]))
            link(dve.tensor_scalar(gt[:, :], gt[:, :], MAX_THR, None, ALU.mult))
            link(dve.tensor_tensor(gw[:, :, :], ge[:, :, :], per_e(gt[:, :]), ALU.subtract))
            link(dve.tensor_scalar(gw[:, :, :], gw[:, :, :], 0.0, None, ALU.max))
            link(dve.tensor_reduce(gs[:, :], gw[:, :, :], AXX, ALU.add))
            link(dve.tensor_scalar(gm[:, :], gs[:, :], 0.0, None, ALU.is_equal))
            link(dve.tensor_tensor(gs[:, :], gs[:, :], gm[:, :], ALU.add))
            link(dve.reciprocal(gs[:, :], gs[:, :]))
            link(dve.tensor_scalar(gs[:, :], gs[:, :], SCALING, None, ALU.mult))
            link(dve.tensor_tensor(gw[:, :, :], gw[:, :, :], per_e(gs[:, :]), ALU.mult))
            for i in range(NT):
                dve.tensor_tensor(hw[:, i, :].rearrange("p (e r) -> p e r", r=NR),
                                  hg[:, i, 0:P].rearrange("p (e r) -> p e r", r=NR),
                                  gw[:, i, :].unsqueeze(2).to_broadcast([P, NE, NR]),
                                  ALU.mult).then_inc(hw_done, 1)
            for i in range(2):
                dve.wait_ge(hw_hi, i + 1)
                dve.tensor_tensor(htl[:, i * 512:(i + 1) * 512], sc[:, i, :],
                                  hth[:, i * 512:(i + 1) * 512].bitcast(F32), ALU.subtract).then_inc(hw_lo, 1)
            for i in range(NT):
                dve.wait_ge(fin_t, i + 1)
                dve.wait_ge(xbo, NT + i + 1)
                dve.tensor_tensor(X[:, i, :], X[:, i, :], fin_bank(i), ALU.add).then_inc(fin, 1)

        @block.tensor
        def _(pe):
            def three(o, pairs, ready=None, lo_ready=None):
                n = 3 * len(pairs)
                m = 0
                if lo_ready is not None:
                    for (wh, wl), (mh, _) in pairs:
                        for w in (wh, wl):
                            pe.matmul(o, w, mh, start=(m == 0), stop=False)
                            m += 1
                    pe.wait_ge(*lo_ready)
                    for (wh, _), (_, ml) in pairs:
                        last = pe.matmul(o, wh, ml, start=False, stop=(m == n - 1))
                        m += 1
                    return last
                for (wh, wl), (mh, ml) in pairs:
                    if ready is not None:
                        pe.wait_ge(ready, m // 3 + 1)
                    for w, r in ((wh, mh), (wh, ml), (wl, mh)):
                        last = pe.matmul(o, w, r, start=(m == 0), stop=(m == n - 1))
                        m += 1
                return last

            def ln_tile(n):
                pe.wait_ge(ln_xn, n + 1)
                for k in range(KT):
                    last = pe.transpose(ln_bank(n)[:, k * P:(k + 1) * P], ln_tmp(n)[:, k * P:(k + 1) * P], ident)
                last.then_inc(ln_t, 1)

            def proj_x(u, h, tile, ready=None, lo_ready=None):
                piece, col = (0, tile) if tile < 2 else (1 + (tile - 2) // 2, tile % 2)
                tok = slice(h * HALF, (h + 1) * HALF)
                a, b = (ah, al) if tile < 2 else (xh, xl)
                c = slice(col * P, (col + 1) * P)
                three(pj[:, tile % 2, :],
                      [((wqh[:, piece, k, c], wql[:, piece, k, c]), (a[:, k, tok], b[:, k, tok]))
                       for k in range(KT)], ready, lo_ready).then_inc(proj, 1)

            def v_transposes(u, h):
                pe.wait_ge(pj_act, XT * u + 2)
                for b in range(HB // 2):
                    last = pe.transpose(tp[:, 0, b * P:(b + 1) * P], vt[:, 2 * b:2 * b + 2, :], ident)
                last.then_inc(tp_t, 1)

            def scores_x(u, h, c):
                for b in range(4):
                    bb = 4 * c + b
                    for hp in range(2):
                        last = pe.matmul(sc[:, c, (2 * b + hp) * S:(2 * b + hp + 1) * S],
                                         qr[h][:, bb, 2 * hp:2 * hp + 2, :], kr[h][:, bb, :],
                                         start=True, stop=True)
                last.then_inc(scored, 1)

            def p_transposes(u, c):
                for b in range(4):
                    last = pe.transpose(tp[:, c, b * P:(b + 1) * P], sm[c][:, b * P:(b + 1) * P], ident)
                last.then_inc(tp_t, 1)

            def pv_x(u, h, c):
                for b in range(4):
                    o = pv[:, b // 2, (b % 2) * 256:(b % 2 + 1) * 256]
                    p = pt[c][:, b * 256:(b + 1) * 256]
                    pe.matmul(o, v2h[h][:, 4 * c + b, :], p, start=True, stop=False)
                    last = pe.matmul(o, v2l[h][:, 4 * c + b, :], p, start=False, stop=True)
                last.then_inc(pv_t, 1)

            def out_x(u, i, bank=0):
                tok = slice(i * P, (i + 1) * P)
                three(pj[:, (i + bank) % 2, :], [((ch[:, r, tok], cl[:, r, tok]), (wdh[:, r, :], wdl[:, r, :]))
                                        for r in range(REP)]).then_inc(outp, 1)

            def ln1(n):
                if n == 6:
                    pe.wait_ge(pj_act, 5)
                elif n >= 4:
                    pe.wait_ge(pj_dve, 5 if n == 7 else n - 3)
                ln_tile(n)

            pe.wait_ge(warm_set, 1)
            for _ in range(WARM_UP):
                pe.matmul(pv[:, 0, :], pt[0][:, 0:P], pt[0][:, P:640], start=True, stop=True)
            pe.wait_ge(wlo, 1)
            proj_x(0, 0, 0, clo)
            proj_x(0, 0, 1)
            pe.wait_ge(s_const, 16)
            for n in range(4):
                ln1(n)
            for tile in range(2, XT):
                if tile == 2:
                    pe.wait_ge(ln_hi, 4)
                if tile in (2, 4):
                    pe.wait_ge(wlo, 1 + tile // 2)
                pe.wait_ge(pj_act, tile - 1)
                proj_x(0, 0, tile, None, (pj_dve, 4) if tile == 2 else None)
                if tile in (3, 5):
                    ln1(tile + 1)
                    ln1(tile + 2)
            v_transposes(0, 0)

            def phase(u, h, g, nxt):
                n = u + 1

                def project(tile):
                    if tile < 2:
                        pe.wait_ge(pj_act, XT * u + 5 + tile)
                        pe.wait_ge(pj_dve, PD_LN1 + 4 * u - 1 + tile)
                    else:
                        pe.wait_ge(pj_act, XT * n + tile - 1)
                    if h == 0 and tile == 0:
                        pe.wait_ge(clo, 2 * KT)
                    if h == 1 and tile in (0, 2, 4):
                        pe.wait_ge(wlo, 3 * (g + 1) + 1 + tile // 2)
                    proj_x(n, 1 - h, tile)

                pe.wait_ge(rope, 5 * u + 5)
                scores_x(u, h, 0)
                scores_x(u, h, 1)
                project(0)
                project(1)
                for c in range(XCH):
                    pe.wait_ge(normed, 2 * u + c + 1)
                    pe.wait_ge(tp_lo, 3 * u + 1)
                    p_transposes(u, c)
                    project(2 + c)
                pe.wait_ge(tp_lo, 3 * u + 2)
                pv_x(u, h, 0)
                project(4)
                pe.wait_ge(tp_lo, 3 * u + 3)
                v_transposes(n, 1 - h)
                project(5)
                pe.wait_ge(pv_lo, 2 * u + 1)
                pv_x(u, h, 1)
                if h == 0:
                    pe.wait_ge(wd_lo, 2 * g + 2)
                for i in range(4):
                    if i % 2 == 0:
                        pe.wait_ge(pv_lo, 2 * u + i // 2 + 1)
                    if i < 2:
                        pe.wait_ge(pj_act, XT * n + 5 + i)
                    pe.wait_ge(pj_dve, PD_LN1 + 4 * u + i - 1)
                    out_x(u, i)
                    if nxt == "last" and i in (1, 3):
                        if i == 1:
                            pe.wait_ge(rope, 5 * n + 5)
                        scores_x(n, 1, i // 2)

            with pe.Fori(0, NKV - 1) as g:
                phase(2 * g, 0, g, "loop")
                phase(2 * g + 1, 1, g, "loop")
            phase(NU - 2, 0, NKV - 1, "last")

            def proj_s(v, tile, first=0, end=3 * KT):
                t, h = UNITS[v]
                k = ST * v + tile
                c = (slice(0, P), slice(256, 384), slice(P, 256))[tile]
                tok = slice(h * HALF, (h + 1) * HALF)
                if first == 0:
                    proj_s_free(k, t, h, tile)
                for m in range(first, end):
                    i, part = m // 3, m % 3
                    if k == 0:
                        i, part = (m // 2, m % 2 * 2) if m < 2 * KT else (m - 2 * KT, 1)
                        if m == 2 * KT:
                            pe.wait_ge(pj_dve, PD_LN2A)
                    last = pe.matmul(pj[:, k % 2, :], ws[t][:, part // 2, i, c], (xl if part == 1 else xh)[:, i, tok],
                                     start=(m == 0), stop=(m == 3 * KT - 1))
                if end == 3 * KT:
                    last.then_inc(proj, 1)

            def proj_s_free(k, t, h, tile):
                if k == 0:
                    pe.wait_ge(ln_hi, NT + 4)
                    pe.wait_ge(pj_dve, PD_14 + 1)
                elif k in (ST, ST + 1):
                    pe.wait_ge(pj_dve, PD_X - 1 + k - ST)
                elif k == 2 * ST:
                    pe.wait_ge(pj_dve, PD_LN2)
                if k >= 2:
                    pe.wait_ge(pj_act, PA_X + k - 1)
                if h == 0:
                    pe.wait_ge(wlo, WL_X + 2 * t + (2 if tile == 1 else 1))

            def proj_s_share(v, c):
                tiles = ([(v + 1, 2)] if 0 < v < NSU - 1 else []) + ([(v + 2, 0), (v + 2, 1)] if v + 2 < NSU else [])
                cuts = {3: (0, 9, 18, 27, 36), 2: (0, 0, 8, 16, 24), 1: (0, 6, 12, 12, 12), 0: (0,) * 5}[len(tiles)]
                for i, (n, tile) in enumerate(tiles):
                    first, end = (min(max(cuts[c + j] - 3 * KT * i, 0), 3 * KT) for j in range(2))
                    if first < end:
                        proj_s(n, tile, first, end)

            def v_transposes_s(v):
                pe.wait_ge(pj_act, PA_X + ST * v + 3)
                if v:
                    pe.wait_ge(pt_done, SCH * (v - 1) + 3)
                for b in range(4):
                    last = pe.transpose(tp[:, 0, b * P:(b + 1) * P], vts[:, b * P:(b + 1) * P], ident)
                last.then_inc(vt_t, 1)

            def scores_s(n):
                v, c = n // SCH, n % SCH
                h = v % 2
                if c == 0:
                    pe.wait_ge(pj_act, PA_X + ST * v + 2)
                if n >= 2:
                    pe.wait_ge(masked, N_SM + n - 1)
                for b in range(2):
                    bb = 2 * c + b
                    last = pe.matmul(sc[:, n % 2, b * 256:(b + 1) * 256], qm[h][:, bb, :, :], kb[h][:, bb, :, :],
                                     start=True, stop=True)
                last.then_inc(scored, 1)

            def p_transposes_s(n):
                pe.wait_ge(normed, N_SM + n + 1)
                if n == 0:
                    pe.wait_ge(vc_done, 1)
                elif n % SCH == 0:
                    pe.wait_ge(vc_done, n // SCH + 1)
                if n >= 2:
                    pe.wait_ge(pt_done, n - 1)
                for i in range(4):
                    last = pe.transpose(tp[:, n % 2, i * P:(i + 1) * P], sm4[n % 4][:, i * P:(i + 1) * P], ident)
                last.then_inc(pt_t, 1)

            def pv_s(n):
                v, c = n // SCH, n % SCH
                h = v % 2
                pe.wait_ge(pt_done, n + 1)
                if n >= 2:
                    pe.wait_ge(ssel, n - 1)
                for b in range(2):
                    for t in range(2):
                        last = pe.matmul(pv[64 * t:64 * t + 64, n % 2, b * P:(b + 1) * P],
                                         vc[h][:, 2 * c + b, t, :],
                                         pts[n % 2][:, (2 * b + t) * P:(2 * b + t + 1) * P], start=True, stop=True)
                last.then_inc(spv, 1)

            u = NU - 1

            def ln2(i):
                if i < 2:
                    pe.wait_ge(pj_act, PA_X - 1 + i)
                    pe.wait_ge(pj_dve, PD_14 - 1 + i)
                elif i == 2:
                    pe.wait_ge(masked, N_SM)
                elif i == 6:
                    pe.wait_ge(masked, N_SM + 2)
                ln_tile(NT + i)

            def p_x(c):
                pe.wait_ge(normed, 2 * u + c + 1)
                p_transposes(u, c)

            pe.wait_ge(tp_lo, 3 * u + 1)
            p_x(0)
            for i in range(4):
                ln2(i)
            proj_s(0, 0)
            p_x(1)
            pe.wait_ge(tp_lo, 3 * u + 2)
            pv_x(u, 1, 0)
            proj_s(0, 1)
            proj_s(0, 2)
            pe.wait_ge(tp_lo, 3 * u + 3)
            pe.wait_ge(pv_lo, 2 * u + 1)
            pv_x(u, 1, 1)
            scores_s(0)
            scores_s(1)
            v_transposes_s(0)
            pe.wait_ge(pj_act, PA_X + ST)
            for i in range(4):
                if i % 2 == 0:
                    pe.wait_ge(pv_lo, 2 * u + i // 2 + 1)
                if i >= 2:
                    pe.wait_ge(pj_dve, PD_LN2A + i - 1)
                if i == 2:
                    scores_s(2)
                out_x(u, i, 1)
            proj_s(1, 0)
            proj_s(1, 1)
            for i in range(4, 8):
                ln2(i)
            proj_s(1, 2)

            def ln3(i):
                if i == 0:
                    pe.wait_ge(masked, N_SM + N_SS)
                elif i >= 4:
                    pe.wait_ge(ln3_lo, i - 1)
                ln_tile(2 * NT + i)

            def out_s(i, first=0, end=3 * KT):
                if first == 0:
                    out_s_free(i)
                tok = slice(i * P, (i + 1) * P)
                for m in range(first, end):
                    k, part = m // 3, m % 3
                    if i == 4:
                        k, part = (m // 2, m % 2) if m < 2 * KT else (m - 2 * KT, 2)
                        if m == 2 * KT:
                            pe.wait_ge(o_lo, NSU)
                    last = pe.matmul(pj[:, i % 2, :], (al if part == 2 else ah)[:, k, tok],
                                     (wol if part == 1 else woh)[:, k, :], start=(m == 0), stop=(m == 3 * KT - 1))
                if end == 3 * KT:
                    last.then_inc(outp, 1)

            def out_s_free(i):
                if i == 0:
                    pe.wait_ge(wlo, WL_X + N_SELF)
                    pe.wait_ge(o_lo, NSU - 2)
                if i == 4:
                    pe.wait_ge(o_hi, NSU)
                if i < 2:
                    pe.wait_ge(pj_act, PA_X + ST * NSU - 1 + i)
                else:
                    pe.wait_ge(pj_dve, PD_LN2 + i - 1)

            for n in range(N_SS):
                v, c = n // SCH, n % SCH
                p_transposes_s(n)
                proj_s_share(v, c)
                if n == 0:
                    pe.wait_ge(pj_dve, PD_LN2)
                if n + 3 < N_SS:
                    scores_s(n + 3)
                if n >= OUT_AT:
                    m = OUT_SHARE * (n - OUT_AT)
                    out_s(m // (3 * KT), m % (3 * KT), m % (3 * KT) + OUT_SHARE)
                pv_s(n)
                if c == 2 and v + 1 < NSU:
                    v_transposes_s(v + 1)

            def hidden(i):
                if i == 0:
                    pe.wait_ge(s_row2, 32)
                if i in (0, 2):
                    pe.wait_ge(ln3_lo, 1 + i // 2)
                pe.wait_ge(ln_hi, 2 * NT + i + 1)
                if i % 2 == 0 and i >= 4:
                    pe.wait_ge(hg_c, i // 2 - 1)
                o = sc[:, i // 2 % 2, (i % 2) * (P + NG):(i % 2 + 1) * (P + NG)]
                for k in range(KT):
                    last = pe.matmul(o, xf[:, k, i * P:(i + 1) * P], wag[:, k, :], start=(k == 0), stop=(k == KT - 1))
                if i % 2:
                    last.then_inc(hg_t, 1)

            def base(i):
                pe.wait_ge(wlo, WL_X + len(late))
                if i < 2:
                    pe.wait_ge(pj_dve, PD_LN2 + 7 + i)
                elif i < 4:
                    pe.wait_ge(ssel, N_SS)
                elif i < 6:
                    pe.wait_ge(ln3_lo, NT)
                else:
                    pe.wait_ge(fin, i - 5)
                pe.wait_ge(ln3_lo, i + 1)
                tok = slice(i * P, (i + 1) * P)
                m = 0
                for k in range(KT):
                    for w, r in ((xh, wbh), (xh, wbl), (xl, wbh)):
                        pe.matmul(fin_bank(i), w[:, k, tok], r[:, k, :], start=(m == 0), stop=False)
                        m += 1

            def moe(i):
                tok = slice(i * P, (i + 1) * P)
                if i % 4 == 0:
                    pe.wait_ge(hw_lo, i // 4 + 1)
                pe.matmul(fin_bank(i), hth[:, tok], weh[:, :], start=False, stop=False)
                pe.matmul(fin_bank(i), hth[:, tok], wel[:, :], start=False, stop=False)
                pe.matmul(fin_bank(i), htl[:, tok], weh[:, :], start=False, stop=True).then_inc(fin_t, 1)

            out_s(3)
            out_s(4)
            out_s(5)
            for i in range(4):
                ln3(i)
            out_s(6)
            hidden(0)
            hidden(1)
            out_s(7)
            hidden(2)
            hidden(3)
            base(0)
            ln3(4)
            ln3(5)
            base(1)
            ln3(6)
            base(2)
            ln3(7)
            base(3)
            for i in range(4, NT):
                hidden(i)
            base(4)
            base(5)
            pe.wait_ge(hg_c, 4)
            for i in range(NT):
                pe.wait_ge(hw_done, i + 1)
                last = pe.transpose(sc[:, i // 4, (i % 4) * P:(i % 4 + 1) * P], hw[:, i, :], ident)
                if i % 4 == 3:
                    last.then_inc(hw_t, 1)
            for i in range(6):
                moe(i)
            for i in range(6, NT):
                base(i)
                moe(i)


def kernel(x, ctx_4096, L0_xattn_Wq, L0_xattn_Wk, L0_xattn_Wv, L0_xattn_Wd, L0_attn_Wq, L0_attn_bq,
           L0_attn_Wk, L0_attn_bk, L0_attn_Wv, L0_attn_bv, L0_attn_Wo, L0_attn_bo, L0_ffn_W_base,
           L0_ffn_b_base, L0_ffn_W_gate, L0_ffn_W_thr, L0_ffn_b_thr, L0_ffn_A, L0_ffn_B):
    import numpy as np
    import concourse.bacc as bacc
    from concourse.bass_utils import run_bass_kernel_spmd

    def A(a):
        return np.asarray(a)

    consts = np.zeros((P, NCONST), np.float32)
    consts[:, C_ID:C_ID + P] = np.eye(P, dtype=np.float32)
    inv = (np.float32(1.0) / np.float32(10000.0) ** (np.arange(0, DH, 2, dtype=np.float32) / np.float32(DH)))
    ang = (np.arange(S, dtype=np.float32)[None, :] * inv.astype(np.float32)[:, None]).astype(np.float32)
    consts[:, C_COS:C_COS + S] = np.concatenate([np.cos(ang), np.cos(ang)], 0)
    consts[:, C_SIN:C_SIN + S] = np.concatenate([-np.sin(ang), np.sin(ang)], 0)
    row = np.arange(P)[:, None] % S
    consts[:, C_MASK:C_MASK + S] = np.where(np.arange(S)[None, :] <= row, 0.0, NEG)
    consts[:, C_PAR] = np.arange(P) // SD % 2 == 0
    consts[:, C_PAR + 1] = np.arange(P) // SD % 2 == 1

    def rows(w):
        return A(w).T.reshape(-1, P, A(w).shape[0]).transpose(1, 0, 2)

    xin = A(x).reshape(NT, P, D).transpose(1, 0, 2)
    ctxT = A(ctx_4096)[:, :S, :].reshape(TOK, KT, P).transpose(2, 1, 0)
    wq, wk, wv = (rows(w) for w in (L0_xattn_Wq, L0_xattn_Wk, L0_xattn_Wv))
    wd = rows(L0_xattn_Wd)
    w_x = np.empty((NKV, P, 5, PIECE), np.float32)
    for g in range(NKV):
        kv = slice(g * P, (g + 1) * P)
        w_x[g, :, 0] = np.concatenate([wk[:, :, kv], wv[:, :, kv]], 2).reshape(P, -1)
        for i in range(2):
            q = slice((REP * g + 2 * i) * P, (REP * g + 2 * i + 2) * P)
            w_x[g, :, 1 + i] = wq[:, :, q].reshape(P, -1)
            w_x[g, :, 3 + i] = wd[:, REP * g + 2 * i:REP * g + 2 * i + 2].reshape(P, -1)
    sq, sk, sv = (rows(w) for w in (L0_attn_Wq, L0_attn_Wk, L0_attn_Wv))
    w_s = np.empty((KT, P, 1536), np.float32)
    for t in range(KT):
        c = slice(t * P, (t + 1) * P)
        w_s[t, :, :1024] = np.concatenate([sk[:, :, c], sv[:, :, c]], 2).reshape(P, -1)
        w_s[t, :, 1024:] = sq[:, :, c].reshape(P, -1)
    arrays = {
        "x": xin, "ctxT": ctxT, "w_x": w_x, "w_s": w_s,
        "w_o": rows(L0_attn_Wo).reshape(P, -1), "w_b": rows(L0_ffn_W_base).reshape(P, -1),
        "w_ag": np.concatenate([rows(A(L0_ffn_A).reshape(NE * NR, D)), rows(L0_ffn_W_gate), rows(L0_ffn_W_thr)], 2),
        "w_eb": A(L0_ffn_B).transpose(0, 2, 1).reshape(NE * NR, D),
        "consts": consts,
        "bias_cols": np.stack([A(b).reshape(KT, P).T for b in (L0_attn_bq, L0_attn_bk, L0_attn_bv)], 1),
        "bias_rows": np.stack([np.broadcast_to(A(b), (P, D)) for b in (L0_attn_bo, L0_ffn_b_base)]),
        "b_thr": np.broadcast_to(A(L0_ffn_b_thr), (P, 1)),
    }
    nc = bacc.Bacc("TRN2", target_bir_lowering=False, num_devices=1)
    arrays = {f"in_{n}": np.ascontiguousarray(a) for n, a in arrays.items()}
    args = [nc.dram_tensor(n, a.shape, mybir.dt.from_np(a.dtype), kind="ExternalInput").ap()
            for n, a in arrays.items()]
    out = nc.dram_tensor("out", (P, NT, D), F32, kind="ExternalOutput").ap()
    build(nc, *args, out)
    r = run_bass_kernel_spmd(nc, [arrays], core_ids=[0])
    return r.results[0]["out"].reshape(P, NT, D).transpose(1, 0, 2).reshape(B, S, D)
```
